# Optimizing a Trainium2 kernel written in Bass

```python
import numpy as np
import jax
import jax.numpy as jnp

def _softmax(x, axis=-1):
    return jax.nn.softmax(x, axis=axis)

def _gelu(x):
    return jax.nn.gelu(x, approximate=True)

def _silu(x):
    return jax.nn.silu(x)

def _sigmoid(x):
    return jax.nn.sigmoid(x)

def _layernorm(x, axis=-1, eps=1e-05):
    m = jnp.mean(x, axis=axis, keepdims=True)
    v = jnp.var(x, axis=axis, keepdims=True)
    return (x - m) / jnp.sqrt(v + eps)

def _scatter_add(tgt, idx, src, axis=0):
    return tgt.at[idx].add(src)

def _segment_sum(src, seg, n):
    return jax.ops.segment_sum(src, seg, n)
kernel_name = 'mk_decoder_preln_d1_seqx_r4_886439'

def setup_inputs(seed: int=0):
    np.random.seed(seed)
    _w = jnp.asarray

    def _rec_inputs():
        import jax
        import jax.numpy as jnp
        _rk = jax.random.key(seed)
        x = -0.0003929 + 0.9999 * jax.random.normal(jax.random.fold_in(_rk, 1), (16, 112, 512), jnp.float32)
        _lenS = 112 - jax.random.randint(jax.random.fold_in(_rk, 7), (16,), 0, max(1, 112 // 4) + 1, jnp.int32)
        _lenS2 = 375 - jax.random.randint(jax.random.fold_in(_rk, 8), (16,), 0, max(1, 375 // 4) + 1, jnp.int32)
        _ctx_1024P = jax.random.normal(jax.random.fold_in(_rk, 11), (16, 16, 256), jnp.float32)
        _ctx_1024c = jax.random.dirichlet(jax.random.fold_in(_rk, 511), 0.3 * jnp.ones((16,), jnp.float32), (16, 375))
        _ctx_1024t = jnp.einsum('bsk,bkd->bsd', _ctx_1024c, _ctx_1024P)
        _ctx_1024t = _ctx_1024t * jax.lax.rsqrt(jnp.mean(jnp.square(_ctx_1024t)) + 1e-12) * 0.953939
        ctx_1024 = -0.000494167 + 1.00018 * (_ctx_1024t + 0.3 * jax.random.normal(jax.random.fold_in(_rk, 611), (16, 375, 256), jnp.float32))
        _validS = jnp.arange(112)[None, :] < _lenS[:, None]
        _validS2 = jnp.arange(375)[None, :] < _lenS2[:, None]
        _causal = jnp.tril(jnp.ones((112, 112), dtype=bool))
        mask_BxS2_bf1 = jnp.ones((16, 375), dtype=bool)
        return (x, ctx_1024, mask_BxS2_bf1)
    x, ctx_1024, mask_BxS2_bf1 = _rec_inputs()

    def _L0_attn_setup():
        import jax, jax.numpy as jnp
        from jax import lax
        import numpy as np
        B, L, D_MODEL = (1, 256, 512)
        H, P, G, S = (32, 64, 8, 32)
        D_SSM = H * P
        CONV_DIM = D_SSM + 2 * G * S
        PROJ_DIM = 2 * D_SSM + 2 * G * S + H
        K = 4
        EPS = 1e-05

        def _forward(hidden_states, W_in, b_in, conv_w, conv_b, A_log, D_param, dt_bias, norm_w, W_out, b_out, mup_vector):
            Bb, Ll, _ = hidden_states.shape
            zxbcdt = (hidden_states @ W_in + b_in) * mup_vector
            z = zxbcdt[..., :D_SSM]
            xBC = zxbcdt[..., D_SSM:D_SSM + CONV_DIM]
            dt = zxbcdt[..., D_SSM + CONV_DIM:]
            xBC_t = jnp.transpose(xBC, (0, 2, 1))
            conv = lax.conv_general_dilated(xBC_t, conv_w[:, None, :], (1,), [(K - 1, 0)], dimension_numbers=('NCH', 'OIH', 'NCH'), feature_group_count=CONV_DIM)
            xBC = jnp.transpose(jax.nn.silu(conv + conv_b[None, :, None]), (0, 2, 1))
            x = xBC[..., :D_SSM].reshape(Bb, Ll, H, P)
            Bm = xBC[..., D_SSM:D_SSM + G * S].reshape(Bb, Ll, G, S)
            Cm = xBC[..., D_SSM + G * S:].reshape(Bb, Ll, G, S)
            rep = H // G
            Bh = jnp.repeat(Bm, rep, axis=2)
            Ch = jnp.repeat(Cm, rep, axis=2)
            dt = jax.nn.softplus(dt + dt_bias)
            a = jnp.exp(dt * -jnp.exp(A_log))
            db = dt[..., None, None] * x[..., None] * Bh[:, :, :, None, :]

            def combine(e1, e2):
                a1, s1 = e1
                a2, s2 = e2
                return (a1 * a2, a2[..., None, None] * s1 + s2)
            states = lax.associative_scan(combine, (a, db), axis=1)[1]
            y = jnp.einsum('blhps,blhs->blhp', states, Ch) + D_param[None, None, :, None] * x
            y = y.reshape(Bb, Ll, D_SSM) * jax.nn.silu(z)
            yg = y.reshape(Bb, Ll, G, D_SSM // G)
            var = jnp.mean(yg * yg, axis=-1, keepdims=True)
            y = (yg * lax.rsqrt(var + EPS)).reshape(Bb, Ll, D_SSM) * norm_w
            return y @ W_out + b_out
        key = jax.random.key(seed)
        ks = jax.random.split(key, 12)
        mults = np.array([0.9, 1.1, 0.8, 1.2, 1.0], dtype=np.float32)
        mv = np.ones(PROJ_DIM, dtype=np.float32)
        mv[:D_SSM] *= mults[0]
        mv[D_SSM:2 * D_SSM] *= mults[1]
        mv[2 * D_SSM:2 * D_SSM + G * S] *= mults[2]
        mv[2 * D_SSM + G * S:2 * D_SSM + 2 * G * S] *= mults[3]
        mv[2 * D_SSM + 2 * G * S:] *= mults[4]
        return {'hidden_states': jax.random.normal(ks[0], (B, L, D_MODEL), jnp.float32), 'W_in': jax.random.normal(ks[1], (D_MODEL, PROJ_DIM), jnp.float32) * 0.02, 'b_in': jax.random.normal(ks[2], (PROJ_DIM,), jnp.float32) * 0.01, 'conv_w': jax.random.normal(ks[3], (CONV_DIM, K), jnp.float32) * 0.2, 'conv_b': jax.random.normal(ks[4], (CONV_DIM,), jnp.float32) * 0.01, 'A_log': jnp.log(jax.random.uniform(ks[5], (H,), jnp.float32, 1.0, 16.0)), 'D_param': jax.random.normal(ks[6], (H,), jnp.float32) * 0.5 + 1.0, 'dt_bias': jax.random.normal(ks[7], (H,), jnp.float32) * 0.5, 'norm_w': jnp.ones((D_SSM,), jnp.float32) + 0.01 * jax.random.normal(ks[8], (D_SSM,), jnp.float32), 'W_out': jax.random.normal(ks[9], (D_SSM, D_MODEL), jnp.float32) * 0.02, 'b_out': jnp.zeros((D_MODEL,), jnp.float32), 'mup_vector': jnp.asarray(mv)}
    _L0_attn_all = _L0_attn_setup()
    _L0_attn_in = {k: v for k, v in _L0_attn_all.items() if k in ('W_in', 'b_in', 'conv_w', 'conv_b', 'A_log', 'D_param', 'dt_bias', 'norm_w', 'W_out', 'b_out', 'mup_vector')}
    del _L0_attn_all

    def _L0_xattn_setup():
        import jax, jax.numpy as jnp
        import numpy as np
        N_HEADS = 16
        N_KV_HEADS = 8
        HEAD_DIM = 128
        D_TEXT = 512
        D_VISION = 256
        GROUPS = N_HEADS // N_KV_HEADS
        key = jax.random.key(seed)
        ks = jax.random.split(key, 6)
        B, T_text, T_vis = (4, 512, 144)
        text_hidden = jax.random.normal(ks[0], (B, T_text, D_TEXT), dtype=jnp.float32)
        vision_tokens = jax.random.normal(ks[1], (B, T_vis, D_VISION), dtype=jnp.float32)
        vision_mask = jnp.ones((B, T_vis), dtype=bool)
        s = 0.02
        Wq = jax.random.normal(ks[2], (D_TEXT, N_HEADS * HEAD_DIM), dtype=jnp.float32) * s
        Wk = jax.random.normal(ks[3], (D_VISION, N_KV_HEADS * HEAD_DIM), dtype=jnp.float32) * s
        Wv = jax.random.normal(ks[4], (D_VISION, N_KV_HEADS * HEAD_DIM), dtype=jnp.float32) * s
        Wo = jax.random.normal(ks[5], (N_HEADS * HEAD_DIM, D_TEXT), dtype=jnp.float32) * s
        return {'text_hidden': text_hidden, 'vision_tokens': vision_tokens, 'vision_mask': vision_mask, 'Wq': Wq, 'Wk': Wk, 'Wv': Wv, 'Wo': Wo}
    _L0_xattn_all = _L0_xattn_setup()
    _L0_xattn_in = {k: v for k, v in _L0_xattn_all.items() if k in ('Wq', 'Wk', 'Wv', 'Wo')}
    del _L0_xattn_all

    def _L0_ffn_setup():
        import jax, jax.numpy as jnp
        import numpy as np
        B, S, H = (2, 256, 512)
        E, K = (8, 2)
        I = 352
        IS = 1408
        WSCALE = 0.02
        key = jax.random.key(seed)
        ks = jax.random.split(key, 9)
        f32 = jnp.float32
        return {'hidden_states': jax.random.normal(ks[0], (B, S, H), dtype=f32), 'gate_w': jax.random.normal(ks[1], (E, H), dtype=f32) * WSCALE, 'w_gate': jax.random.normal(ks[2], (E, H, I), dtype=f32) * WSCALE, 'w_up': jax.random.normal(ks[3], (E, H, I), dtype=f32) * WSCALE, 'w_down': jax.random.normal(ks[4], (E, I, H), dtype=f32) * WSCALE, 'sw_gate': jax.random.normal(ks[5], (H, IS), dtype=f32) * WSCALE, 'sw_up': jax.random.normal(ks[6], (H, IS), dtype=f32) * WSCALE, 'sw_down': jax.random.normal(ks[7], (IS, H), dtype=f32) * WSCALE, 'shared_gate_w': jax.random.normal(ks[8], (H, 1), dtype=f32) * WSCALE}
    _L0_ffn_all = _L0_ffn_setup()
    _L0_ffn_in = {k: v for k, v in _L0_ffn_all.items() if k in ('gate_w', 'w_gate', 'w_up', 'w_down', 'sw_gate', 'sw_up', 'sw_down', 'shared_gate_w')}
    del _L0_ffn_all
    return {'x': x, 'ctx_1024': ctx_1024, 'mask_BxS2_bf1': mask_BxS2_bf1, 'L0_attn_W_in': _L0_attn_in['W_in'], 'L0_attn_b_in': _L0_attn_in['b_in'], 'L0_attn_conv_w': _L0_attn_in['conv_w'], 'L0_attn_conv_b': _L0_attn_in['conv_b'], 'L0_attn_A_log': _L0_attn_in['A_log'], 'L0_attn_D_param': _L0_attn_in['D_param'], 'L0_attn_dt_bias': _L0_attn_in['dt_bias'], 'L0_attn_norm_w': _L0_attn_in['norm_w'], 'L0_attn_W_out': _L0_attn_in['W_out'], 'L0_attn_b_out': _L0_attn_in['b_out'], 'L0_attn_mup_vector': _L0_attn_in['mup_vector'], 'L0_xattn_Wq': _L0_xattn_in['Wq'], 'L0_xattn_Wk': _L0_xattn_in['Wk'], 'L0_xattn_Wv': _L0_xattn_in['Wv'], 'L0_xattn_Wo': _L0_xattn_in['Wo'], 'L0_ffn_gate_w': _L0_ffn_in['gate_w'], 'L0_ffn_w_gate': _L0_ffn_in['w_gate'], 'L0_ffn_w_up': _L0_ffn_in['w_up'], 'L0_ffn_w_down': _L0_ffn_in['w_down'], 'L0_ffn_sw_gate': _L0_ffn_in['sw_gate'], 'L0_ffn_sw_up': _L0_ffn_in['sw_up'], 'L0_ffn_sw_down': _L0_ffn_in['sw_down'], 'L0_ffn_shared_gate_w': _L0_ffn_in['shared_gate_w']}

def reference(x, ctx_1024, mask_BxS2_bf1, L0_attn_W_in, L0_attn_b_in, L0_attn_conv_w, L0_attn_conv_b, L0_attn_A_log, L0_attn_D_param, L0_attn_dt_bias, L0_attn_norm_w, L0_attn_W_out, L0_attn_b_out, L0_attn_mup_vector, L0_xattn_Wq, L0_xattn_Wk, L0_xattn_Wv, L0_xattn_Wo, L0_ffn_gate_w, L0_ffn_w_gate, L0_ffn_w_up, L0_ffn_w_down, L0_ffn_sw_gate, L0_ffn_sw_up, L0_ffn_sw_down, L0_ffn_shared_gate_w):
    import jax
    import jax.numpy as jnp

    def _L0_attn_ref(hidden_states, W_in, b_in, conv_w, conv_b, A_log, D_param, dt_bias, norm_w, W_out, b_out, mup_vector):
        import jax, jax.numpy as jnp
        from jax import lax
        import numpy as np
        B, L, D_MODEL = (1, 256, 512)
        H, P, G, S = (32, 64, 8, 32)
        D_SSM = H * P
        CONV_DIM = D_SSM + 2 * G * S
        PROJ_DIM = 2 * D_SSM + 2 * G * S + H
        K = 4
        EPS = 1e-05

        def _forward(hidden_states, W_in, b_in, conv_w, conv_b, A_log, D_param, dt_bias, norm_w, W_out, b_out, mup_vector):
            Bb, Ll, _ = hidden_states.shape
            zxbcdt = (hidden_states @ W_in + b_in) * mup_vector
            z = zxbcdt[..., :D_SSM]
            xBC = zxbcdt[..., D_SSM:D_SSM + CONV_DIM]
            dt = zxbcdt[..., D_SSM + CONV_DIM:]
            xBC_t = jnp.transpose(xBC, (0, 2, 1))
            conv = lax.conv_general_dilated(xBC_t, conv_w[:, None, :], (1,), [(K - 1, 0)], dimension_numbers=('NCH', 'OIH', 'NCH'), feature_group_count=CONV_DIM)
            xBC = jnp.transpose(jax.nn.silu(conv + conv_b[None, :, None]), (0, 2, 1))
            x = xBC[..., :D_SSM].reshape(Bb, Ll, H, P)
            Bm = xBC[..., D_SSM:D_SSM + G * S].reshape(Bb, Ll, G, S)
            Cm = xBC[..., D_SSM + G * S:].reshape(Bb, Ll, G, S)
            rep = H // G
            Bh = jnp.repeat(Bm, rep, axis=2)
            Ch = jnp.repeat(Cm, rep, axis=2)
            dt = jax.nn.softplus(dt + dt_bias)
            a = jnp.exp(dt * -jnp.exp(A_log))
            db = dt[..., None, None] * x[..., None] * Bh[:, :, :, None, :]

            def combine(e1, e2):
                a1, s1 = e1
                a2, s2 = e2
                return (a1 * a2, a2[..., None, None] * s1 + s2)
            states = lax.associative_scan(combine, (a, db), axis=1)[1]
            y = jnp.einsum('blhps,blhs->blhp', states, Ch) + D_param[None, None, :, None] * x
            y = y.reshape(Bb, Ll, D_SSM) * jax.nn.silu(z)
            yg = y.reshape(Bb, Ll, G, D_SSM // G)
            var = jnp.mean(yg * yg, axis=-1, keepdims=True)
            y = (yg * lax.rsqrt(var + EPS)).reshape(Bb, Ll, D_SSM) * norm_w
            return y @ W_out + b_out
        return _forward(hidden_states, W_in, b_in, conv_w, conv_b, A_log, D_param, dt_bias, norm_w, W_out, b_out, mup_vector)

    def _L0_xattn_ref(text_hidden, vision_tokens, vision_mask, Wq, Wk, Wv, Wo):
        import jax, jax.numpy as jnp
        import numpy as np
        N_HEADS = 16
        N_KV_HEADS = 8
        HEAD_DIM = 128
        D_TEXT = 512
        D_VISION = 256
        GROUPS = N_HEADS // N_KV_HEADS
        B, T_text, _ = text_hidden.shape
        T_vis = vision_tokens.shape[1]
        scale = jnp.float32(np.sqrt(HEAD_DIM))
        q = (text_hidden @ Wq).reshape(B, T_text, N_HEADS, HEAD_DIM).transpose(0, 2, 1, 3)
        k = (vision_tokens @ Wk).reshape(B, T_vis, N_KV_HEADS, HEAD_DIM).transpose(0, 2, 1, 3)
        v = (vision_tokens @ Wv).reshape(B, T_vis, N_KV_HEADS, HEAD_DIM).transpose(0, 2, 1, 3)
        k = jnp.repeat(k, GROUPS, axis=1)
        v = jnp.repeat(v, GROUPS, axis=1)
        scores = jnp.einsum('bhtd,bhsd->bhts', q, k) / scale
        mask = vision_mask[:, None, None, :]
        scores = jnp.where(mask, scores, -jnp.inf)
        attn = jax.nn.softmax(scores, axis=-1)
        attn = jnp.nan_to_num(attn, nan=0.0)
        out = jnp.einsum('bhts,bhsd->bhtd', attn, v)
        out = out.transpose(0, 2, 1, 3).reshape(B, T_text, N_HEADS * HEAD_DIM)
        return out @ Wo

    def _L0_ffn_ref(hidden_states, gate_w, w_gate, w_up, w_down, sw_gate, sw_up, sw_down, shared_gate_w):
        import jax, jax.numpy as jnp
        import numpy as np
        B, S, H = (2, 256, 512)
        E, K = (8, 2)
        I = 352
        IS = 1408
        WSCALE = 0.02
        x = hidden_states
        logits = jnp.einsum('bsh,eh->bse', x, gate_w)
        probs = jax.nn.softmax(logits, axis=-1)
        top_w, top_i = jax.lax.top_k(probs, K)
        top_w = top_w / jnp.sum(top_w, axis=-1, keepdims=True)
        onehot = jax.nn.one_hot(top_i, E, dtype=x.dtype)
        combine = jnp.einsum('bsk,bske->bse', top_w, onehot)
        g = jnp.einsum('bsh,ehi->besi', x, w_gate)
        u = jnp.einsum('bsh,ehi->besi', x, w_up)
        h = jax.nn.silu(g) * u
        expert_out = jnp.einsum('besi,eih->besh', h, w_down)
        moe_out = jnp.einsum('besh,bse->bsh', expert_out, combine)
        sh = jax.nn.silu(x @ sw_gate) * (x @ sw_up)
        shared_out = sh @ sw_down
        shared_gate = jax.nn.sigmoid(x @ shared_gate_w)
        return moe_out + shared_out * shared_gate
    x = x + _L0_attn_ref(_layernorm(x, axis=-1), L0_attn_W_in, L0_attn_b_in, L0_attn_conv_w, L0_attn_conv_b, L0_attn_A_log, L0_attn_D_param, L0_attn_dt_bias, L0_attn_norm_w, L0_attn_W_out, L0_attn_b_out, L0_attn_mup_vector)
    x = x + _L0_xattn_ref(_layernorm(x, axis=-1), ctx_1024, mask_BxS2_bf1, L0_xattn_Wq, L0_xattn_Wk, L0_xattn_Wv, L0_xattn_Wo)
    x = x + _L0_ffn_ref(_layernorm(x, axis=-1), L0_ffn_gate_w, L0_ffn_w_gate, L0_ffn_w_up, L0_ffn_w_down, L0_ffn_sw_gate, L0_ffn_sw_up, L0_ffn_sw_down, L0_ffn_shared_gate_w)
    return x

_drawn_inputs = setup_inputs


def setup_inputs(seed=0):
    import zlib

    import numpy as np

    out = dict(_drawn_inputs(seed))
    spreads = {'L0_attn_b_out': (0.0, 1.705)}
    factors = {'L0_attn_b_in': 2.708,
     'L0_attn_A_log': 64.0,
     'L0_attn_dt_bias': 8.0,
     'L0_attn_norm_w': 121.37,
     'L0_xattn_Wq': 27.642,
     'L0_xattn_Wk': 26.732,
     'L0_ffn_gate_w': 24.392,
     'L0_ffn_shared_gate_w': 64.0,
     'L0_ffn_w_gate': 8.0,
     'L0_ffn_w_up': 8.0,
     'L0_ffn_w_down': 8.0,
     'L0_ffn_sw_gate': 8.0,
     'L0_ffn_sw_up': 7.898,
     'L0_ffn_sw_down': 7.903,
     'ctx_1024': 3.268,
     'L0_xattn_Wv': 3.017,
     'L0_xattn_Wo': 3.044}
    for name, (base, spread) in spreads.items():
        noise = np.random.default_rng([zlib.crc32(name.encode()), seed]).standard_normal(out[name].shape)
        drawn = base * np.exp(spread * noise) if base else spread * noise
        out[name] = jnp.asarray(drawn.astype(out[name].dtype))
    for name, factor in factors.items():
        out[name] = (out[name] * factor).astype(out[name].dtype)
    return out
```

```python
from contextlib import ExitStack

import concourse.bass as bass
from concourse import mybir

F32 = mybir.dt.float32
F32R = mybir.dt.float32r
ALU = mybir.AluOpType
ACT = mybir.ActivationFunctionType
AX = mybir.AxisListType

P = 128
DM = 512
KD = DM // P
LN_EPS = 1e-5
TOKENS = 16 * 112


def opener(nc, ctx, prefix):
    def sb(name, shape, dt=F32):
        return ctx.enter_context(nc.sbuf_tensor(f"{prefix}_{name}", shape, dt))

    def ps(name, shape):
        return ctx.enter_context(nc.psum_tensor(f"{prefix}_ps_{name}", shape, F32))

    used = []

    def sem(name):
        used.append(nc.alloc_semaphore(f"{prefix}_{name}"))
        return used[-1]

    def give_back():
        if used:
            nc.clear_and_free_semaphores(used)
            nc.all_engine_barrier()

    ctx.callback(give_back)

    return sb, ps, sem


def matmul_split(pe, out, w_hi, w_lo, x_hi, x_lo, start, stop):
    pe.matmul(out, w_hi, x_hi, start=start, stop=False)
    pe.matmul(out, w_hi, x_lo, start=False, stop=False)
    return pe.matmul(out, w_lo, x_hi, start=False, stop=stop)



class Norm:

    def __init__(self, sb, sem, rows, tiles, x, xt_hi, xt_lo, ident, banks, loads):
        self.rows, self.tiles, self.x, self.xt_hi, self.xt_lo = rows, tiles, x, xt_hi, xt_lo
        self.ident, self.banks, self.loads = ident, banks, loads
        self.stats = sb("ln_stats", [rows, tiles, 6])
        self.mv = sb("ln_mv", [rows, tiles, 2])
        self.std = sb("ln_std", [rows, tiles])
        self.rstd = sb("ln_rstd", [rows, tiles])
        self.xn = sb("ln_xn", [rows, 2, DM])
        self.x_in = [sem(f"ln_x_in{n}") for n in range(len(loads))]
        self.ident_in = sem("ln_ident_in")
        self.stats_done = sem("ln_stats_done")
        self.moments = sem("ln_moments")
        self.std_done = sem("ln_std_done")
        self.rstd_done = sem("ln_rstd_done")
        self.xn_done = sem("ln_xn_done")
        self.turned = sem("ln_turned")
        self.hi_done = sem("ln_hi_done")
        self.lo_done = sem("ln_lo_done")


def norm_load(s, eng, x_dram, ident_dram):
    eng.dma_start(s.ident[:], ident_dram).then_inc(s.ident_in, 16)
    for n, (a, b) in enumerate(s.loads):
        eng.dma_start(s.x[:, a:b, :], x_dram[:, a:b, :]).then_inc(s.x_in[n], 16)


def norm_vector(s, dve):
    for n, (a, b) in enumerate(s.loads):
        dve.wait_ge(s.x_in[n], 16)
        for t in range(a, b):
            dve.bn_stats(s.stats[:, t, :], s.x[:, t, :]).then_inc(s.stats_done, 1)
    for t in range(s.tiles):
        dve.wait_ge(s.stats_done, t + 1)
        dve.bn_aggr(s.mv[:, t, :], s.stats[:, t, :]).then_inc(s.moments, 1)
    dve.wait_ge(s.moments, s.tiles)
    dve.tensor_scalar(s.std[:], s.mv[:, :, 1], LN_EPS, None, ALU.add).then_inc(s.moments, 1)
    dve.wait_ge(s.std_done, 1)
    dve.reciprocal(s.rstd[:], s.std[:]).then_inc(s.rstd_done, 1)
    dve.wait_ge(s.rstd_done, 1)
    for t in range(s.tiles + 1):
        if t < s.tiles:
            if t >= 2:
                dve.wait_ge(s.turned, t - 1)
            dve.tensor_scalar(s.xn[:, t % 2, :], s.x[:, t, :], s.mv[:, t, 0:1], s.rstd[:, t:t + 1],
                              ALU.subtract, ALU.mult).then_inc(s.xn_done, 1)
        if t >= 1:
            dve.wait_ge(s.hi_done, t)
            bank = s.banks[(t - 1) % len(s.banks)]
            cols = slice((t - 1) * s.rows, t * s.rows)
            dve.tensor_tensor(s.xt_lo[:, :, cols], turned_view(s, bank),
                              s.xt_hi[:, :, cols].bitcast(F32), ALU.subtract).then_inc(s.lo_done, 1)


def turned_view(s, bank):
    return bank[:, 0:KD * s.rows].rearrange("p (k t) -> p k t", k=KD)


def norm_scalar(s, act):
    act.wait_ge(s.moments, s.tiles + 1)
    act.activation(s.std[:], s.std[:], ACT.Sqrt).then_inc(s.std_done, 1)
    for t in range(s.tiles):
        act.wait_ge(s.turned, t + 1)
        act.activation(s.xt_hi[:, :, t * s.rows:(t + 1) * s.rows],
                       turned_view(s, s.banks[t % len(s.banks)]), ACT.Copy).then_inc(s.hi_done, 1)


def norm_tensor(s, pe):
    pe.wait_ge(s.ident_in, 16)
    for t in range(s.tiles):
        pe.wait_ge(s.xn_done, t + 1)
        if t >= len(s.banks):
            pe.wait_ge(s.lo_done, t - len(s.banks) + 1)
        view = turned_view(s, s.banks[t % len(s.banks)])
        for k in range(KD):
            ins = pe.transpose(view[:, k, :], s.xn[:, t % 2, k * P:(k + 1) * P],
                               s.ident[0:s.rows, 0:s.rows])
        ins.then_inc(s.turned, 1)


B = 16
T = 112
HB = B // 2
HT = HB * T
TGB = 4
TGT = TGB * T
NG = 8
NH = 4
HP = 64
ST = 32
GC = NH * HP
GJ = GC // P
HEADS = NG * NH
TAPS = 4
PADT = T + TAPS - 1
WIN = 2 * GJ * DM
WOUT = GJ * DM
NBC = 5
LEAST_LOG = -200.0
MOST_LOG_A = 88.0
SCALED_A = 1024.0
BIAS_, MUP_, TAP_, CONVB_, EXTRA_ = 0, 1, 2, 6, 7
NPAR = 8
NSLOT = 2 * NG


def convolve(dve, out, padded, par, done, base):
    dve.tensor_scalar(out, padded[:, :, 0:T], par[:, TAP_:TAP_ + 1], par[:, CONVB_:CONVB_ + 1],
                      ALU.mult, ALU.add).then_inc(done, 1)
    for k in range(1, TAPS):
        dve.wait_ge(done, base + k)
        dve.scalar_tensor_tensor(out, padded[:, :, k:k + T], par[:, TAP_ + k:TAP_ + k + 1], out,
                                 ALU.mult, ALU.add).then_inc(done, 1)


class Kept:

    def __init__(self, sb):
        self.x = sb("x", [T, HB, DM])
        self.xt_hi = sb("xt_hi", [P, KD, HT], F32R)
        self.xt_lo = sb("xt_lo", [P, KD, HT], F32R)
        self.ident = sb("ident", [P, P])
        self.below_raw = sb("below_raw", [T, T])
        self.below = sb("below", [T, T], F32R)
        self.tri = sb("tri", [T, T])
        self.skip = sb("skip", [T, HEADS])
        self.b_out = sb("b_out", [T, DM])
        self.cb = sb("cb", [T, HB, NG, T])
        self.dt = sb("dt", [T, HB, HEADS])
        self.da_hi = sb("da_hi", [T, HB, HEADS], F32R)
        self.da_lo = sb("da_lo", [T, HB, HEADS], F32R)


def attn_prepare(nc, half, x_dram, d, keep):
    with ExitStack() as ctx:
        sb, ps, sem = opener(nc, ctx, f"ap{half}")
        w_raw = sb("w_raw", [P, KD, NBC * P])
        w_hi = sb("w_hi", [P, KD, NBC * P], F32R)
        w_lo = sb("w_lo", [P, KD, NBC * P], F32R)
        par = sb("par", [P, NBC, NPAR])
        bias = sb("bias", [P, NBC])
        a_rate = sb("a_rate", [ST, 2])
        pad = sb("pad", [P, 2, TGB, PADT])
        conv = sb("conv", [P, 2, TGB, T])
        bc = sb("bc", [P, NBC - 1, HT])
        tri = sb("tri", [T, T])
        u = sb("u", [HEADS, HT])
        e = sb("e", [HEADS, HT])
        w1 = sb("w1", [HEADS, HT])
        lnw = sb("lnw", [HEADS, HT])
        rest = sb("rest", [HEADS, HT])
        dt = sb("dt", [HEADS, HT])
        da = sb("da", [HEADS, HT])
        banks = [ps(f"bank{i}", [P, 512]) for i in range(4)]
        proj = [ps(f"proj{i}", [P, 512]) for i in range(2)]
        ln = Norm(sb, sem, T, HB, keep.x, keep.xt_hi, keep.xt_lo, keep.ident, banks, [(0, 2), (2, 5), (5, 8)])
        w_in, w_hi_done, w_lo_done = sem("w_in"), sem("w_hi_done"), sem("w_lo_done")
        par_in, bias_done = sem("par_in"), sem("bias_done")
        const_in, const_done = sem("const_in"), sem("const_done")
        zeroed = sem("zeroed")
        proj_done, drained, conv_done, silu_done = sem("proj_done"), sem("drained"), sem("conv_done"), sem("silu_done")
        cb_done, cb_out = sem("cb_done"), sem("cb_out")
        soft, exp_done = sem("soft"), sem("exp_done")
        dt_turned, dt_out = sem("dt_turned"), sem("dt_out")
        x_biased = sem("x_biased")
        NC4 = NBC - 1
        block = ctx.enter_context(nc.Block())

        @block.sync
        def _(sp):
            norm_load(ln, sp, x_dram.rearrange("(b t) d -> t b d", t=T)[:, half * HB:(half + 1) * HB, :], d["ident"])
            sp.dma_start(w_raw[:], d["w_bcdt"]).then_inc(w_in, 16)
            sp.dma_start(par[:], d["par_bcdt"]).then_inc(par_in, 16)
            sp.dma_start(tri[:], d["tri"]).then_inc(const_in, 16)
            sp.dma_start(keep.below_raw[:], d["below"]).then_inc(const_in, 16)
            sp.dma_start(keep.skip[:], d["skip"].to_broadcast([T, HEADS])).then_inc(const_in, 16)
            sp.dma_start(keep.b_out[:], d["b_out"].to_broadcast([T, DM])).then_inc(const_in, 16)

        @block.gpsimd
        def _(pool):
            pool.memset(pad[:, :, :, 0:TAPS - 1], 0.0).then_inc(zeroed, 1)
            pool.wait_ge(w_hi_done, 1)
            pool.tensor_tensor(w_lo[:], w_raw[:], w_hi[:].bitcast(F32), ALU.subtract).then_inc(w_lo_done, 1)
            pool.wait_ge(const_in, 64)
            pool.tensor_copy(keep.tri[:], tri[:]).then_inc(const_done, 1)
            pool.wait_ge(ln.xn_done, HB)
            for b in range(HB):
                pool.tensor_tensor(keep.x[:, b, :], keep.x[:, b, :], keep.b_out[:], ALU.add).then_inc(x_biased, 1)

        @block.tensor
        def _(pe):
            norm_tensor(ln, pe)
            pe.wait_ge(ln.lo_done, HB)
            pe.wait_ge(w_lo_done, 1)
            n = 0
            for g in range(2):
                a = slice(g * TGT, (g + 1) * TGT)
                for c in (NC4, 0, 1, 2, 3):
                    if n >= 2:
                        pe.wait_ge(drained, n - 1)
                    for k in range(KD):
                        w = slice(c * P, (c + 1) * P)
                        ins = matmul_split(pe, proj[n % 2][:, 0:TGT], w_hi[:, k, w], w_lo[:, k, w],
                                           keep.xt_hi[:, k, a], keep.xt_lo[:, k, a], k == 0, k == KD - 1)
                    ins.then_inc(proj_done, 1)
                    n += 1
            pe.wait_ge(drained, 2 * NBC)
            pe.wait_ge(soft, 10)
            view = proj[0][0:T, :].rearrange("t (b k h) -> t b k h", b=HB, k=2)
            for b in range(HB):
                for k, src in enumerate((dt, da)):
                    ins = pe.transpose(view[:, b, k, :], src[:, b * T:(b + 1) * T], keep.ident[0:HEADS, 0:HEADS])
            ins.then_inc(dt_turned, 1)
            pe.wait_ge(silu_done, 2 * NC4)
            for b in range(0, HB, 2):
                for r in range(4):
                    if b:
                        pe.wait_ge(cb_out, (b // 2 - 1) * 4 + r + 1)
                    else:
                        pe.wait_ge(ln.lo_done, HB)
                    rows = slice(r * ST, (r + 1) * ST)
                    for i in range(2):
                        for q in range(2):
                            o = (i * 2 + q) * T
                            a = slice((b + i) * T, (b + i + 1) * T)
                            ins = pe.matmul(banks[r][0:T, o:o + T], bc[rows, q, a], bc[rows, 2 + q, a], start=True, stop=True)
                    ins.then_inc(cb_done, 1)

        def silu(act, m):
            g, c = m // NC4, m % NC4
            act.wait_ge(conv_done, TAPS * (m + 1))
            act.activation(bc[:, c, g * TGT:(g + 1) * TGT].rearrange("p (b t) -> p b t", b=TGB), conv[:, c % 2], ACT.Silu).then_inc(silu_done, 1)

        @block.scalar
        def _(act):
            act.wait_ge(w_in, 16)
            act.activation(w_hi[:], w_raw[:], ACT.Copy).then_inc(w_hi_done, 1)
            norm_scalar(ln, act)
            act.wait_ge(par_in, 16)
            act.wait_ge(bias_done, 3)
            act.activation(a_rate[:, 1:2], a_rate[:, 0:1], ACT.Exp).then_inc(exp_done, 1)
            act.wait_ge(zeroed, 1)
            n = 0
            for g in range(2):
                for c in (NC4, 0, 1, 2, 3):
                    act.wait_ge(proj_done, n + 1)
                    if c == NC4:
                        act.activation(u[:, g * TGT:(g + 1) * TGT], proj[n % 2][0:HEADS, 0:TGT], ACT.Identity,
                                       bias=bias[0:HEADS, c:c + 1], scale=par[0:HEADS, c, MUP_:MUP_ + 1]).then_inc(drained, 1)
                    else:
                        m = g * NC4 + c
                        if m >= 2:
                            act.wait_ge(conv_done, TAPS * (m - 1))
                        act.activation(pad[:, c % 2, :, TAPS - 1:], proj[n % 2][:, 0:TGT].rearrange("p (b t) -> p b t", b=TGB),
                                       ACT.Identity, bias=bias[:, c:c + 1], scale=par[:, c, MUP_:MUP_ + 1]).then_inc(drained, 1)
                        if m >= 1:
                            silu(act, m - 1)
                    n += 1
            silu(act, 2 * NC4 - 1)
            act.wait_ge(soft, 1)
            act.activation(e[:], e[:], ACT.Exp, scale=-1.0).then_inc(exp_done, 1)
            act.wait_ge(soft, 2)
            act.activation(lnw[:], w1[:], ACT.Ln).then_inc(exp_done, 1)
            act.wait_ge(dt_turned, 1)
            act.activation(keep.da_hi[:], proj[0][0:T, :].rearrange("t (b k h) -> t b k h", b=HB, k=2)[:, :, 1, :],
                           ACT.Copy).then_inc(dt_out, 1)

        @block.vector
        def _(dve):
            dve.wait_ge(par_in, 16)
            dve.tensor_tensor(bias[:], par[:, :, BIAS_], par[:, :, MUP_], ALU.mult).then_inc(bias_done, 1)
            dve.wait_ge(bias_done, 1)
            dve.tensor_tensor(bias[:, NC4:NBC], bias[:, NC4:NBC], par[:, NC4, EXTRA_:EXTRA_ + 1], ALU.add).then_inc(bias_done, 1)
            dve.tensor_scalar(a_rate[:, 0:1], par[0:HEADS, NC4, TAP_:TAP_ + 1], MOST_LOG_A, None, ALU.min).then_inc(bias_done, 1)
            norm_vector(ln, dve)
            dve.wait_ge(const_in, 64)
            dve.tensor_copy(keep.below[:], keep.below_raw[:]).then_inc(const_done, 1)
            for g in range(2):
                for c in range(NC4):
                    m = g * NC4 + c
                    dve.wait_ge(drained, g * NBC + c + 2)
                    if m >= 2:
                        dve.wait_ge(silu_done, m - 1)
                    convolve(dve, conv[:, c % 2], pad[:, c % 2], par[:, c, :], conv_done, TAPS * m)

            chain = [0]

            def link(ins):
                chain[0] += 1
                ins.then_inc(soft, 1)
                dve.wait_ge(soft, chain[0])

            link(dve.scalar_tensor_tensor(e[:], u[:], -1.0, u[:], ALU.mult, ALU.max))
            dve.wait_ge(exp_done, 2)
            link(dve.tensor_scalar(w1[:], e[:], 1.0, None, ALU.add))
            link(dve.tensor_scalar(rest[:], w1[:], 1.0, None, ALU.subtract))
            link(dve.tensor_tensor(rest[:], e[:], rest[:], ALU.subtract))
            link(dve.reciprocal(e[:], w1[:]))
            link(dve.tensor_tensor(rest[:], rest[:], e[:], ALU.mult))
            dve.wait_ge(exp_done, 3)
            link(dve.tensor_tensor(rest[:], rest[:], lnw[:], ALU.add))
            link(dve.scalar_tensor_tensor(dt[:], u[:], 0.0, rest[:], ALU.max, ALU.add))
            link(dve.tensor_scalar(da[:], dt[:], 1.0 / SCALED_A, a_rate[:, 1:2], ALU.mult, ALU.mult))
            link(dve.tensor_scalar(da[:], da[:], -LEAST_LOG / SCALED_A, -SCALED_A, ALU.min, ALU.mult))
            view = proj[0][0:T, :].rearrange("t (b k h) -> t b k h", b=HB, k=2)
            dve.wait_ge(dt_out, 1)
            dve.tensor_copy(keep.dt[:], view[:, :, 0, :]).then_inc(dt_out, 1)
            dve.wait_ge(dt_out, 2)
            dve.tensor_tensor(keep.da_lo[:], view[:, :, 1, :], keep.da_hi[:].bitcast(F32), ALU.subtract).then_inc(dt_out, 1)
            for n in range(HB // 2 * 4):
                b, r = n // 4 * 2, n % 4
                dve.wait_ge(cb_done, n + 1)
                for i in range(2):
                    ins = dve.tensor_tensor(keep.cb[:, b + i, r:NG:4, :], banks[r][0:T, 2 * i * T:2 * (i + 1) * T].rearrange("s (q t) -> s q t", q=2),
                                            tri[:].unsqueeze(1).to_broadcast([T, 2, T]), ALU.mult)
                ins.then_inc(cb_out, 1)


def attn_main(nc, half, d, out_dram, keep):
    with ExitStack() as ctx:
        sb, ps, sem = opener(nc, ctx, f"am{half}")
        wi_raw = sb("wi_raw", [P, 4, KD * P])
        wi_hi = sb("wi_hi", [P, 4, KD * P], F32R)
        wi_lo = sb("wi_lo", [P, 4, KD * P], F32R)
        wo_raw = sb("wo_raw", [P, WOUT])
        wo_hi = sb("wo_hi", [P, WOUT], F32R)
        wo_lo = sb("wo_lo", [P, WOUT], F32R)
        par_raw = sb("par_raw", [P, 5, NPAR])
        par = sb("par", [P, 5, NPAR])
        bias = sb("bias", [P, 4])
        norm_w = sb("norm_w", [P, GJ])
        pad = sb("pad", [P, GJ, TGB, PADT])
        conv = sb("conv", [P, GJ, TGB, T])
        xs = sb("xs", [P, 2, GJ, TGT])
        zs = sb("zs", [P, 2, GJ, TGT])
        steps_hi = sb("steps_hi", [T, 2, NH, T], F32R)
        steps_lo = sb("steps_lo", [T, 2, NH, T], F32R)
        decay = sb("decay", [T, 2, NH, T])
        mix = sb("mix", [T, 2, NH, T])
        x_dt = sb("x_dt", [T, 2, NH, HP])
        x_skip = sb("x_skip", [T, 2, GC])
        y = sb("y", [T, 2, TGB, GC])
        square = sb("square", [T, GC])
        power = sb("power", [T, 2, TGB])
        std = sb("std", [T, 2, TGB])
        rstd = sb("rstd", [T, 2, TGB])
        yt_hi = sb("yt_hi", [P, GJ, TGT], F32R)
        yt_lo = sb("yt_lo", [P, GJ, TGT], F32R)
        p_ps = [ps(f"p{i}", [P, 512]) for i in range(2)]
        xz_ps, seg_ps, y_ps, r_ps = ps("xz", [P, 512]), ps("seg", [P, 512]), ps("y", [P, 512]), ps("r", [P, 512])
        t_ps = [ps(f"t{j}", [P, 512]) for j in range(GJ)]

        wi_in = [sem(f"wi_in{c}") for c in range(4)]
        wi_hi_done = [sem(f"wi_hi_done{c}") for c in range(4)]
        wi_lo_done = [sem(f"wi_lo_done{c}") for c in range(4)]
        wo_in, wo_hi_done, wo_lo_done = sem("wo_in"), sem("wo_hi_done"), sem("wo_lo_done")
        par_in, par_done, norm_w_done = sem("par_in"), sem("par_done"), sem("norm_w_done")
        zeroed = sem("zeroed")
        proj_done = sem("proj_done")
        drained = sem("drained")
        conv_done = sem("conv_done")
        silu_done = sem("silu_done")
        xz_done = sem("xz_done")
        steps_done = sem("steps_done")
        seg_done, decay_done, mix_done = sem("seg_done"), sem("decay_done"), sem("mix_done")
        x_dt_done, x_skip_done = sem("x_dt_done"), sem("x_skip_done")
        y_done, y_skip_done, y_gated = sem("y_done"), sem("y_skip_done"), sem("y_gated")
        square_done, var_done, std_done, rstd_done = sem("square_done"), sem("var_done"), sem("std_done"), sem("rstd_done")
        y_normed = sem("y_normed")
        yt_done, yt_hi_done, yt_lo_done = sem("yt_done"), sem("yt_hi_done"), sem("yt_lo_done")
        r_done, added = sem("r_done"), sem("added")
        stored = sem("stored")
        held_pool = sem("held_pool")

        def slots(eng, slot):
            for u in (-1, 0):
                slot(0, u, False)
            with eng.Fori(0, NG - 1) as g:
                for u in (1, 2):
                    slot(g, u, False)
            for u in (1, 2):
                slot(NG - 1, u, True)

        def parts(u, last):
            return u >= 0 and not (last and u == 2), not last, u >= 1

        def wait(eng, sem_, value):
            if not isinstance(value, int) or value > 0:
                eng.wait_ge(sem_, value)

        block = ctx.enter_context(nc.Block())

        @block.sync
        def _(sp):
            def load(i, g):
                for c in range(4):
                    wait(sp, wi_lo_done[c], i)
                    sp.dma_start(wi_raw[:, c, :], d["w_mix"][bass.ds(g, 1), :, c * DM:(c + 1) * DM].rearrange("o p n -> p (o n)")).then_inc(wi_in[c], 16)
                if isinstance(i, int) and i == NG:
                    return
                wait(sp, par_done, 2 * i)
                sp.dma_start(par_raw[:], d["par_mix"][bass.ds(g, 1)].rearrange("o p r n -> p (o r) n")).then_inc(par_in, 16)
                wait(sp, wo_lo_done, i)
                sp.dma_start(wo_raw[:], d["w_mix"][bass.ds(g, 1), :, 4 * DM:].rearrange("o p n -> p (o n)")).then_inc(wo_in, 16)

            load(0, 0)
            with sp.Fori(1, NG) as g:
                load(g, g)
            load(NG, NG - 1)
            out_v = out_dram.rearrange("(b t) d -> t b d", t=T)[:, half * HB:(half + 1) * HB, :]
            for a in range(0, HB, TGB):
                sp.wait_ge(added, 1 + (NG - 1) * HB + a + TGB)
                sp.dma_start(out_v[:, a:a + TGB, :], keep.x[:, a:a + TGB, :]).then_inc(stored, 16)
            sp.wait_ge(stored, 32)

        @block.tensor
        def _(pe):
            def slot(g, u, last):
                scan, project, product = parts(u, last)
                G = 2 * g + u

                def output(b):
                    a = slice(b * T, (b + 1) * T)
                    pe.wait_ge(added, 4 * (G - 1) + b + 1)
                    for j in range(GJ):
                        w = slice(j * DM, (j + 1) * DM)
                        ins = matmul_split(pe, r_ps[0:T, :], yt_hi[:, j, a], yt_lo[:, j, a], wo_hi[:, w], wo_lo[:, w],
                                           j == 0, j == GJ - 1)
                    ins.then_inc(r_done, 1)

                for b in range(TGB):
                    U = 4 * G + b
                    if scan:
                        pe.wait_ge(steps_done, 2 * U + 2)
                        wait(pe, decay_done, U)
                        pe.matmul(seg_ps[0:T, 0:NH * T], keep.below[:], steps_hi[:, b % 2].rearrange("s h t -> s (h t)"), start=True, stop=False)
                        pe.matmul(seg_ps[0:T, 0:NH * T], keep.below[:], steps_lo[:, b % 2].rearrange("s h t -> s (h t)"), start=False, stop=True).then_inc(seg_done, 1)
                    if project:
                        if (u + 1) % 2 == 0:
                            pe.wait_ge(wi_lo_done[b], g + (u + 1) // 2 + 1)
                        wait(pe, drained, 4 * (G + 1) + b - 1)
                        a = slice((u + 1) % 2 * TGT, ((u + 1) % 2 + 1) * TGT)
                        for k in range(KD):
                            w = slice(k * P, (k + 1) * P)
                            ins = matmul_split(pe, p_ps[b % 2][:, 0:TGT], wi_hi[:, b, w], wi_lo[:, b, w],
                                               keep.xt_hi[:, k, a], keep.xt_lo[:, k, a], k == 0, k == KD - 1)
                        ins.then_inc(proj_done, 1)
                    if scan:
                        if b == 0:
                            pe.wait_ge(drained, 4 * (G + 1))
                            pe.wait_ge(silu_done, 2 * (G + 1))
                        wait(pe, y_gated, U)
                        wait(pe, x_skip_done, U)
                        for i, src in enumerate((xs, zs)):
                            for j in range(GJ):
                                o = (i * GJ + j) * P
                                ins = pe.transpose(xz_ps[0:T, o:o + P], src[:, u % 2, j, b * T:(b + 1) * T], keep.ident[:])
                        ins.then_inc(xz_done, 1)
                    if product and b == 1:
                        pe.wait_ge(y_normed, 4 * G)
                        pe.wait_ge(yt_lo_done, 2 * G)
                        for j in range(GJ):
                            for i in range(TGB):
                                ins = pe.transpose(t_ps[j][:, i * T:(i + 1) * T], y[:, (u - 1) % 2, i, j * P:(j + 1) * P], keep.ident[0:T, 0:T])
                            ins.then_inc(yt_done, 1)
                    if product and b == 2:
                        pe.wait_ge(yt_lo_done, 2 * G + 2)
                        pe.wait_ge(wo_lo_done, g + (u - 1) // 2 + 1)
                        output(0)
                    if product and b == 3:
                        output(2)
                    if scan:
                        pe.wait_ge(mix_done, U + 1)
                        pe.wait_ge(x_dt_done, U + 1)
                        wait(pe, y_skip_done, U)
                        for h in range(NH):
                            o = h * HP
                            ins = pe.matmul(y_ps[0:T, o:o + HP], mix[:, b % 2, h, :], x_dt[:, b % 2, h, :], start=True, stop=True)
                        ins.then_inc(y_done, 1)
                    if product and b >= 2:
                        output(2 * (b - 2) + 1)

            slots(pe, slot)

        @block.scalar
        def _(act):
            def split(c, i):
                act.wait_ge(wi_in[c], 16 * (i + 1))
                wait(act, proj_done, 8 * i - 4 + c + 1 if not (isinstance(i, int) and i == 0) else 0)
                act.activation(wi_hi[:, c, :], wi_raw[:, c, :], ACT.Copy).then_inc(wi_hi_done[c], 1)

            def slot(g, u, last):
                scan, project, product = parts(u, last)
                G = 2 * g + u
                Q = G + 1
                if product and u == 1:
                    act.wait_ge(wo_in, 16 * (g + 1))
                    act.wait_ge(added, 4 * (G - 1) + 1)
                    act.activation(wo_hi[:], wo_raw[:], ACT.Copy).then_inc(wo_hi_done, 1)
                for b in range(TGB):
                    U = 4 * G + b
                    if scan:
                        act.wait_ge(seg_done, U + 1)
                        wait(act, mix_done, U - 1)
                        act.activation(decay[:, b % 2].rearrange("s h t -> s (h t)"), seg_ps[0:T, 0:NH * T], ACT.Exp).then_inc(decay_done, 1)
                    if project and b < GJ:
                        if b == 0:
                            act.wait_ge(par_done, 2 * (g + (u + 1) // 2) + 2)
                        act.wait_ge(proj_done, 4 * Q + b + 1)
                        wait(act, conv_done, 2 * TAPS * (Q - 1) + TAPS * (b + 1))
                        act.activation(pad[:, b, :, TAPS - 1:], p_ps[b % 2][:, 0:TGT].rearrange("p (b t) -> p b t", b=TGB),
                                       ACT.Identity, bias=bias[:, b:b + 1], scale=par[:, b, MUP_:MUP_ + 1]).then_inc(drained, 1)
                    if product and b == 2:
                        for j in range(GJ):
                            act.wait_ge(yt_done, 2 * (G - 1) + j + 1)
                            act.wait_ge(added, 4 * (G - 1) + 1)
                            act.wait_ge(norm_w_done, g + (u - 1) // 2 + 1)
                            act.activation(yt_hi[:, j, :], t_ps[j][:, 0:TGT], ACT.Copy, scale=norm_w[:, j:j + 1]).then_inc(yt_hi_done, 1)
                    if scan and b >= 1:
                        squares(g, u, b - 1)
                if project:
                    wait(act, xz_done, 4 * (Q - 1))
                    for j in range(GJ):
                        act.wait_ge(proj_done, 4 * Q + GJ + j + 1)
                        act.activation(zs[:, (u + 1) % 2, j, :], p_ps[j % 2][:, 0:TGT], ACT.Silu,
                                       bias=bias[:, GJ + j:GJ + j + 1], scale=par[:, GJ + j, MUP_:MUP_ + 1]).then_inc(drained, 1)
                    for j in range(GJ):
                        act.wait_ge(conv_done, 2 * TAPS * Q + TAPS * (j + 1))
                        act.activation(xs[:, (u + 1) % 2, j, :], conv[:, j].rearrange("p b t -> p (b t)"), ACT.Silu).then_inc(silu_done, 1)
                if scan:
                    squares(g, u, TGB - 1)
                    act.wait_ge(var_done, G + 1)
                    act.activation(std[:, u % 2, :], std[:, u % 2, :], ACT.Sqrt).then_inc(std_done, 1)
                if project and (u + 1) % 2 == 1:
                    for c in range(4):
                        split(c, g + (u + 1) // 2 + 1)

            def squares(g, u, b):
                U = 8 * g + 4 * u + b
                act.wait_ge(y_gated, U + 1)
                wait(act, square_done, U)
                act.activation(square[:], y[:, u % 2, b, :], ACT.Square, accum_out=power[:, u % 2, b:b + 1]).then_inc(square_done, 1)

            for c in range(4):
                split(c, 0)
            act.wait_ge(zeroed, 1)
            slots(act, slot)

        @block.gpsimd
        def _(pool):
            pool.memset(pad[:, :, :, 0:TAPS - 1], 0.0).then_inc(zeroed, 1)

            def steps(g, tg, b, U):
                wait(pool, seg_done, U - 1)
                pool.sem_inc(held_pool, 1)
                for out, src in ((steps_hi, keep.da_hi), (steps_lo, keep.da_lo)):
                    pool.tensor_tensor(out[:, b % 2], src[:, tg * TGB + b, bass.ds(g * NH, NH)].bitcast(F32).unsqueeze(2).to_broadcast([T, NH, T]),
                                       keep.tri[:].unsqueeze(1).to_broadcast([T, NH, T]), ALU.mult).then_inc(steps_done, 1)

            def slot(g, u, last):
                scan, project, product = parts(u, last)
                if not scan:
                    return
                G = 2 * g + u
                for b in range(TGB):
                    U = 4 * G + b
                    if b + 1 < TGB:
                        steps(g + u // 2, u % 2, b + 1, U + 1)
                    elif not (last and u == 1):
                        steps(g + (u + 1) // 2, (u + 1) % 2, 0, U + 1)
                    pool.wait_ge(decay_done, U + 1)
                    wait(pool, y_done, U - 1)
                    pool.sem_inc(held_pool, 1)
                    pool.tensor_tensor(mix[:, b % 2], decay[:, b % 2],
                                       keep.cb[:, u % 2 * TGB + b, bass.ds(g + u // 2, 1), :].to_broadcast([T, NH, T]), ALU.mult).then_inc(mix_done, 1)

            steps(0, 0, 0, 0)
            slots(pool, slot)

        @block.vector
        def _(dve):
            dve.sem_inc(added, 1)
            dve.sem_inc(yt_lo_done, 2)

            def split(c, i):
                dve.wait_ge(wi_hi_done[c], i + 1)
                dve.tensor_tensor(wi_lo[:, c, :], wi_raw[:, c, :], wi_hi[:, c, :].bitcast(F32), ALU.subtract).then_inc(wi_lo_done[c], 1)

            def slot(g, u, last):
                scan, project, product = parts(u, last)
                G = 2 * g + u
                Q = G + 1
                if product:
                    dve.wait_ge(std_done, G)
                    dve.reciprocal(rstd[:, (u - 1) % 2, :], std[:, (u - 1) % 2, :]).then_inc(rstd_done, 1)
                    dve.wait_ge(rstd_done, G)
                    for b in range(TGB):
                        dve.tensor_scalar(y[:, (u - 1) % 2, b, :], y[:, (u - 1) % 2, b, :], rstd[:, (u - 1) % 2, b:b + 1], None,
                                          ALU.mult).then_inc(y_normed, 1)
                if u % 2 == 1:
                    if product:
                        dve.tensor_copy(norm_w[:], par[:, 4, 0:GJ]).then_inc(norm_w_done, 1)
                        dve.wait_ge(wo_hi_done, g + 1)
                        dve.tensor_tensor(wo_lo[:], wo_raw[:], wo_hi[:].bitcast(F32), ALU.subtract).then_inc(wo_lo_done, 1)
                    if project:
                        i = g + (u + 1) // 2
                        dve.wait_ge(par_in, 16 * (i + 1))
                        wait(dve, silu_done, 2 * Q)
                        wait(dve, norm_w_done, i)
                        dve.tensor_copy(par[:], par_raw[:]).then_inc(par_done, 1)
                        dve.wait_ge(par_done, 2 * i + 1)
                        dve.tensor_tensor(bias[:], par[:, 0:4, BIAS_], par[:, 0:4, MUP_], ALU.mult).then_inc(par_done, 1)
                for b in range(TGB):
                    U = 4 * G + b
                    if project and b < GJ:
                        dve.wait_ge(drained, 4 * Q + b + 1)
                        wait(dve, silu_done, 2 * (Q - 1) + b + 1)
                        convolve(dve, conv[:, b], pad[:, b], par[:, b, :], conv_done, 2 * TAPS * Q + TAPS * b)
                    if scan:
                        p = b % 2
                        heads = bass.ds((g + u // 2) * NH, NH)
                        dve.wait_ge(xz_done, U + 1)
                        wait(dve, y_done, U - 1)
                        x_tok = xz_ps[0:T, 0:GC].rearrange("t (h p) -> t h p", h=NH)
                        dve.tensor_tensor(x_dt[:, p], x_tok, keep.dt[:, u % 2 * TGB + b, heads].unsqueeze(2).to_broadcast([T, NH, HP]),
                                          ALU.mult).then_inc(x_dt_done, 1)
                        dve.tensor_tensor(x_skip[:, p, :].rearrange("t (h p) -> t h p", h=NH), x_tok,
                                          keep.skip[:, heads].unsqueeze(2).to_broadcast([T, NH, HP]), ALU.mult).then_inc(x_skip_done, 1)
                    if product and b == 2:
                        for j in range(GJ):
                            dve.wait_ge(yt_hi_done, 2 * (G - 1) + j + 1)
                            dve.scalar_tensor_tensor(yt_lo[:, j, :], t_ps[j][:, 0:TGT], norm_w[:, j:j + 1], yt_hi[:, j, :].bitcast(F32),
                                                     ALU.mult, ALU.subtract).then_inc(yt_lo_done, 1)
                    if product and b >= 2:
                        add(G, u, 2 * (b - 2))
                    if scan:
                        dve.wait_ge(y_done, U + 1)
                        dve.wait_ge(x_skip_done, U + 1)
                        dve.tensor_tensor(y[:, u % 2, b, :], y_ps[0:T, 0:GC], x_skip[:, p, :], ALU.add).then_inc(y_skip_done, 1)
                        dve.wait_ge(y_skip_done, U + 1)
                        dve.tensor_tensor(y[:, u % 2, b, :], y[:, u % 2, b, :], xz_ps[0:T, GC:2 * GC], ALU.mult).then_inc(y_gated, 1)
                    if product and b >= 2:
                        add(G, u, 2 * (b - 2) + 1)
                if scan:
                    dve.wait_ge(square_done, 4 * G + 4)
                    dve.tensor_scalar(std[:, u % 2, :], power[:, u % 2, :], 1.0 / GC, LN_EPS, ALU.mult, ALU.add).then_inc(var_done, 1)
                if project and (u + 1) % 2 == 1:
                    for c in range(4):
                        split(c, g + (u + 1) // 2 + 1)

            def add(G, u, b):
                m = (u - 1) % 2 * TGB + b
                dve.wait_ge(r_done, 4 * (G - 1) + b + 1)
                dve.tensor_tensor(keep.x[:, m, :], r_ps[0:T, :], keep.x[:, m, :], ALU.add).then_inc(added, 1)

            for c in range(4):
                split(c, 0)
            slots(dve, slot)


def attn_phase(nc, x_dram, d, out_dram):
    for half in range(2):
        with ExitStack() as ctx:
            sb, ps, sem = opener(nc, ctx, f"ak{half}")
            keep = Kept(sb)
            attn_prepare(nc, half, x_dram, d, keep)
            attn_main(nc, half, d, out_dram, keep)


B = 16
T = 112
S = 375
SE = S + 1
DC = 256
KC = DC // P
SCH = 3
SL = S // SCH
HD = 128
NKV = 8
QH = 2
HB = B // 2
HT = HB * T
TGB = 4
TGT = TGB * T
WQ, WKV, WO = KD * QH * HD, 2 * KC * HD, QH * DM
PAIR = 2 * HB
NPAIR = NKV // 2
MASKED = 1e30


def xattn_half(nc, half, x_dram, ctx_dram, mask_dram, w_dram, ident_dram, out_dram):
    with ExitStack() as ctx:
        sb, ps, sem = opener(nc, ctx, f"xa{half}")
        x = sb("x", [T, HB, DM])
        xt_hi = sb("xt_hi", [P, KD, HT], F32R)
        xt_lo = sb("xt_lo", [P, KD, HT], F32R)
        c_raw = sb("c_raw", [P, 2, KC, SE])
        c_hi = sb("c_hi", [P, HB, KC, SE], F32R)
        c_lo = sb("c_lo", [P, HB, KC, SE], F32R)
        ident = sb("ident", [P, P])
        mask_raw = sb("mask_raw", [T, HB, S], mybir.dt.uint8)
        bias = sb("bias", [T, HB, S])
        valid = sb("valid", [T, HB])
        wq_raw = sb("wq_raw", [P, WQ])
        wkv_raw = sb("wkv_raw", [P, WKV])
        wo_raw = sb("wo_raw", [P, WO])
        wq_hi = sb("wq_hi", [P, WQ], F32R)
        wq_lo = sb("wq_lo", [P, WQ], F32R)
        wkv_hi = sb("wkv_hi", [P, 2, WKV], F32R)
        wkv_lo = sb("wkv_lo", [P, 2, WKV], F32R)
        wo_hi = sb("wo_hi", [P, WO], F32R)
        wo_lo = sb("wo_lo", [P, WO], F32R)
        q_hi = sb("q_hi", [P, 2, QH, TGT], F32R)
        q_lo = sb("q_lo", [P, 2, QH, TGT], F32R)
        k_hi = sb("k_hi", [P, 2, SE], F32R)
        k_lo = sb("k_lo", [P, 2, SE], F32R)
        v_hi = sb("v_hi", [SL, 2, SCH * HD], F32R)
        v_lo = sb("v_lo", [SL, 2, SCH * HD], F32R)
        prob = sb("prob", [T, 2, QH, S])
        least = sb("least", [T, 2, QH])
        total = sb("total", [T, 2, QH])
        recip = sb("recip", [T, 2, QH])
        pt_hi = sb("pt_hi", [SL, 2, SCH, QH, T], F32R)
        pt_lo = sb("pt_lo", [SL, 2, SCH, QH, T], F32R)
        o_hi = sb("o_hi", [P, 2, QH * T], F32R)
        o_lo = sb("o_lo", [P, 2, QH * T], F32R)

        k_ps = ps("k", [P, 512])
        v_ps = ps("v", [P, 512])
        s_ps = [ps(f"s{h}", [P, 512]) for h in range(QH)]
        t_ps = [ps(f"t{h}", [P, 512]) for h in range(QH)]
        o_ps = ps("o", [P, 512])
        r_ps = ps("r", [P, 512])

        ln = Norm(sb, sem, T, HB, x, xt_hi, xt_lo, ident, s_ps + t_ps, [(0, 2), (2, 5), (5, 8)])
        mask_in, bias_done = sem("mask_in"), sem("bias_done")
        c_in = [sem(f"c_in{i}") for i in range(2)]
        c_hi_done, c_lo_done = sem("c_hi_done"), sem("c_lo_done")
        wq_in, wkv_in, wo_in = sem("wq_in"), sem("wkv_in"), sem("wo_in")
        wq_hi_done, wkv_hi_done, wo_hi_done = sem("wq_hi_done"), sem("wkv_hi_done"), sem("wo_hi_done")
        wq_lo_done, wkv_lo_done, wo_lo_done = sem("wq_lo_done"), sem("wkv_lo_done"), sem("wo_lo_done")
        q_done, q_hi_done, q_lo_done = sem("q_done"), sem("q_hi_done"), sem("q_lo_done")
        k_done, k_hi_done, k_lo_done = sem("k_done"), sem("k_hi_done"), sem("k_lo_done")
        v_done, v_hi_done, v_lo_done = sem("v_done"), sem("v_hi_done"), sem("v_lo_done")
        s_done, max_done, exp_done = sem("s_done"), sem("max_done"), sem("exp_done")
        recip_done, norm_done = sem("recip_done"), sem("norm_done")
        t_done, pt_hi_done, pt_lo_done = sem("t_done"), sem("pt_hi_done"), sem("pt_lo_done")
        o_done, o_hi_done, o_lo_done = sem("o_done"), sem("o_hi_done"), sem("o_lo_done")
        r_done = sem("r_done")
        added = sem("added")
        stored = sem("stored")
        held_dve, held_pool = sem("held_dve"), sem("held_pool")

        def slots(eng, slot):
            for u in (-2, -1, 0):
                slot(0, u, False)
            with eng.Fori(0, NPAIR - 1) as b:
                for u in range(1, PAIR + 1):
                    slot(b, u, False)
            for u in range(1, PAIR + 1):
                slot(NPAIR - 1, u, True)

        def parts(u, last):
            return (u >= 0 and not (last and u >= PAIR), u >= -1 and not (last and u + 1 >= PAIR),
                    u >= 1, not (last and u + 2 >= PAIR))

        def wait(eng, sem_, value):
            if not isinstance(value, int) or value > 0:
                eng.wait_ge(sem_, value)

        def splits(u, last):
            if u < 0 or (last and u >= HB + 1):
                return None, 0
            return {3: "q", 4: "kv", 0: "o" if u else None}.get(u % HB), (u - 1) // HB + 1

        block = ctx.enter_context(nc.Block())

        @block.sync
        def _(sp):
            norm_load(ln, sp, x_dram.rearrange("(b t) d -> t b d", t=T)[:, half * HB:(half + 1) * HB, :], ident_dram)

            def load_w(i):
                w = w_dram[bass.ds(i, 1)].rearrange("o p n -> p (o n)")
                wait(sp, wq_lo_done, i)
                sp.dma_start(wq_raw[:], w[:, 0:WQ]).then_inc(wq_in, 16)
                wait(sp, wkv_lo_done, i)
                sp.dma_start(wkv_raw[:], w[:, WQ:WQ + WKV]).then_inc(wkv_in, 16)
                wait(sp, wo_lo_done, i)
                sp.dma_start(wo_raw[:], w[:, WQ + WKV:]).then_inc(wo_in, 16)

            load_w(0)
            sp.dma_start(mask_raw[:], mask_dram[half:half + 1].to_broadcast([T, HB, S])).then_inc(mask_in, 16)
            for b in range(HB):
                if b >= 2:
                    sp.wait_ge(c_lo_done, b - 1)
                sp.dma_start(c_raw[:, b % 2], ctx_dram[half * HB + b].rearrange("(k p) s -> p k s", p=P)).then_inc(c_in[b % 2], 16)
            with sp.Fori(1, NKV) as i:
                load_w(i)
            out_v = out_dram.rearrange("(b t) d -> t b d", t=T)[:, half * HB:(half + 1) * HB, :]
            for a in range(0, HB, 2):
                sp.wait_ge(added, 1 + (NKV - 1) * HB + a + 2)
                sp.dma_start(out_v[:, a:a + 2, :], x[:, a:a + 2, :]).then_inc(stored, 16)
            sp.wait_ge(stored, 16 * HB // 2)

        @block.tensor
        def _(pe):
            norm_tensor(ln, pe)
            pe.wait_ge(ln.lo_done, HB)
            pe.wait_ge(c_lo_done, HB)

            def slot(b, u, last):
                turn, score, product, keys = parts(u, last)
                n = b * PAIR + u
                if turn:
                    for h in range(QH):
                        wait(pe, norm_done, 2 * n + h + 1)
                        wait(pe, pt_lo_done, 2 * n - 1 + h)
                        view = t_ps[h][0:SL, 0:SCH * T].rearrange("s (c t) -> s c t", c=SCH)
                        for c in range(SCH):
                            ins = pe.transpose(view[:, c, :], prob[:, u % 2, h, c * SL:(c + 1) * SL], ident[0:T, 0:T])
                        ins.then_inc(t_done, 1)
                if score:
                    w, g = u + 1, (u + 1) % PAIR // TGB
                    pe.wait_ge(k_lo_done, n + 2)
                    if w % TGB == 0:
                        pe.wait_ge(q_lo_done, b * (PAIR // TGB * QH) + w // TGB * QH + QH)
                    a = slice(w % TGB * T, (w % TGB + 1) * T)
                    for h in range(QH):
                        wait(pe, max_done, 2 * n + h + 1)
                        ins = matmul_split(pe, s_ps[h][0:T, 0:SE], q_hi[:, g % 2, h, a], q_lo[:, g % 2, h, a],
                                           k_hi[:, w % 2, :], k_lo[:, w % 2, :], True, True)
                        ins.then_inc(s_done, 1)
                if product:
                    m = u - 1
                    pe.wait_ge(o_lo_done, n)
                    if m % HB == 0:
                        pe.wait_ge(wo_lo_done, 2 * b + m // HB + 1)
                    pe.wait_ge(added, n)
                    for h in range(QH):
                        a, w = slice(h * T, (h + 1) * T), slice(h * DM, (h + 1) * DM)
                        ins = matmul_split(pe, r_ps[0:T, :], o_hi[:, m % 2, a], o_lo[:, m % 2, a],
                                           wo_hi[:, w], wo_lo[:, w], h == 0, h == QH - 1)
                    ins.then_inc(r_done, 1)
                if keys:
                    w, i = u + 2, (u + 2) // HB
                    wait(pe, k_lo_done, n + 2)
                    wait(pe, v_lo_done, n + 2)
                    if w % TGB == 0:
                        if w % HB == 0:
                            pe.wait_ge(wq_lo_done, 2 * b + i + 1)
                        for h, bank in enumerate((k_ps, v_ps)):
                            for k in range(KD):
                                c = slice((k * QH + h) * HD, (k * QH + h + 1) * HD)
                                a = slice(w // TGB % 2 * TGT, (w // TGB % 2 + 1) * TGT)
                                ins = matmul_split(pe, bank[:, 0:TGT], wq_hi[:, c], wq_lo[:, c],
                                                   xt_hi[:, k, a], xt_lo[:, k, a], k == 0, k == KD - 1)
                            ins.then_inc(q_done, 1)
                        pe.wait_ge(q_lo_done, b * (PAIR // TGB * QH) + w // TGB * QH + 1)
                    if w % HB == 0:
                        pe.wait_ge(wkv_lo_done, 2 * b + i + 1)
                    for k in range(KC):
                        c = slice(k * HD, (k + 1) * HD)
                        ins = matmul_split(pe, k_ps[:, 0:SE], wkv_hi[:, i % 2, c], wkv_lo[:, i % 2, c],
                                           c_hi[:, w % HB, k, :], c_lo[:, w % HB, k, :], k == 0, k == KC - 1)
                    ins.then_inc(k_done, 1)
                    if w % TGB == 0:
                        pe.wait_ge(q_lo_done, b * (PAIR // TGB * QH) + w // TGB * QH + QH)
                    for c in range(SCH):
                        for k in range(KC):
                            a, d = slice(c * SL, (c + 1) * SL), slice((KC + k) * HD, (KC + k + 1) * HD)
                            ins = matmul_split(pe, v_ps[0:SL, c * HD:(c + 1) * HD], c_hi[:, w % HB, k, a], c_lo[:, w % HB, k, a],
                                               wkv_hi[:, i % 2, d], wkv_lo[:, i % 2, d], k == 0, k == KC - 1)
                    ins.then_inc(v_done, 1)
                if turn:
                    pe.wait_ge(pt_lo_done, 2 * n + 2)
                    pe.wait_ge(v_lo_done, n + 1)
                    wait(pe, o_lo_done, n)
                    for c in range(SCH):
                        d = slice(c * HD, (c + 1) * HD)
                        ins = matmul_split(pe, o_ps[:, 0:QH * T], v_hi[:, u % 2, d], v_lo[:, u % 2, d],
                                           pt_hi[:, u % 2, c].rearrange("s h t -> s (h t)"),
                                           pt_lo[:, u % 2, c].rearrange("s h t -> s (h t)"), c == 0, c == SCH - 1)
                    ins.then_inc(o_done, 1)

            slots(pe, slot)

        @block.scalar
        def _(act):
            norm_scalar(ln, act)
            for b in range(HB):
                act.wait_ge(c_in[b % 2], 16 * (b // 2 + 1))
                act.activation(c_hi[:, b], c_raw[:, b % 2], ACT.Copy).then_inc(c_hi_done, 1)

            def split(kind, i, j):
                if kind == "q":
                    act.wait_ge(wq_in, 16 * (i + 1))
                    wait(act, q_done, i * (HB // TGB * QH))
                    act.activation(wq_hi[:], wq_raw[:], ACT.Copy).then_inc(wq_hi_done, 1)
                if kind == "kv":
                    act.wait_ge(wkv_in, 16 * (i + 1))
                    wait(act, v_done, i * HB - TGB)
                    act.activation(wkv_hi[:, j], wkv_raw[:], ACT.Copy).then_inc(wkv_hi_done, 1)
                if kind == "o":
                    act.wait_ge(wo_in, 16 * (i + 1))
                    wait(act, r_done, i * HB)
                    act.activation(wo_hi[:], wo_raw[:], ACT.Copy).then_inc(wo_hi_done, 1)

            def slot(b, u, last):
                turn, score, product, keys = parts(u, last)
                n = b * PAIR + u
                if turn:
                    for h in range(QH):
                        act.wait_ge(t_done, 2 * n + h + 1)
                        wait(act, o_done, n)
                        act.activation(pt_hi[:, u % 2, :, h, :], t_ps[h][0:SL, 0:SCH * T].rearrange("s (c t) -> s c t", c=SCH),
                                       ACT.Copy).then_inc(pt_hi_done, 1)
                if score:
                    w = (u + 1) % 2
                    for h in range(QH):
                        act.wait_ge(max_done, 2 * n + h + 3)
                        act.activation(prob[:, w, h, :], prob[:, w, h, :], ACT.Exp, bias=least[:, w, h:h + 1], scale=-1.0,
                                       accum_out=total[:, w, h:h + 1]).then_inc(exp_done, 1)
                if keys:
                    w = u + 2
                    wait(act, s_done, 2 * n + 2)
                    if w % TGB == 0:
                        for h, bank in enumerate((k_ps, v_ps)):
                            act.wait_ge(q_done, b * (PAIR // TGB * QH) + w // TGB * QH + h + 1)
                            act.activation(q_hi[:, w // TGB % 2, h, :], bank[:, 0:TGT], ACT.Copy).then_inc(q_hi_done, 1)
                    act.wait_ge(k_done, n + 3)
                    act.activation(k_hi[:, w % 2, :], k_ps[:, 0:SE], ACT.Copy).then_inc(k_hi_done, 1)
                if turn:
                    act.wait_ge(o_done, n + 1)
                    wait(act, r_done, n)
                    act.activation(o_hi[:, u % 2, :], o_ps[:, 0:QH * T], ACT.Copy).then_inc(o_hi_done, 1)
                if keys:
                    act.wait_ge(v_done, n + 3)
                    wait(act, o_done, n + 1)
                    act.activation(v_hi[:, w % 2, :], v_ps[0:SL, 0:SCH * HD], ACT.Copy).then_inc(v_hi_done, 1)
                kind, i = splits(u, last)
                if kind:
                    split(kind, 2 * b + i, i % 2)

            for kind in ("q", "kv", "o"):
                split(kind, 0, 0)
            slots(act, slot)

        @block.gpsimd
        def _(pool):
            pool.wait_ge(mask_in, 16)
            pool.tensor_scalar(bias[:], mask_raw[:], MASKED, -MASKED, ALU.mult, ALU.add).then_inc(bias_done, 1)
            for b in range(HB):
                pool.wait_ge(c_hi_done, b + 1)
                pool.tensor_tensor(c_lo[:, b], c_raw[:, b % 2], c_hi[:, b].bitcast(F32), ALU.subtract).then_inc(c_lo_done, 1)

            def split(kind, i, j):
                if kind == "q":
                    pool.wait_ge(wq_hi_done, i + 1)
                    pool.tensor_tensor(wq_lo[:], wq_raw[:], wq_hi[:].bitcast(F32), ALU.subtract).then_inc(wq_lo_done, 1)
                if kind == "kv":
                    pool.wait_ge(wkv_hi_done, i + 1)
                    pool.tensor_tensor(wkv_lo[:, j], wkv_raw[:], wkv_hi[:, j].bitcast(F32), ALU.subtract).then_inc(wkv_lo_done, 1)
                if kind == "o":
                    pool.wait_ge(wo_hi_done, i + 1)
                    pool.tensor_tensor(wo_lo[:], wo_raw[:], wo_hi[:].bitcast(F32), ALU.subtract).then_inc(wo_lo_done, 1)

            def slot(b, u, last):
                turn, score, product, keys = parts(u, last)
                n = b * PAIR + u
                if score:
                    w = (u + 1) % 2
                    pool.wait_ge(recip_done, n + 2)
                    pool.sem_inc(held_pool, 1)
                    for h in range(QH):
                        pool.tensor_scalar(prob[:, w, h, :], prob[:, w, h, :], recip[:, w, h:h + 1],
                                           valid[:, (u + 1) % HB:(u + 1) % HB + 1], ALU.mult, ALU.mult).then_inc(norm_done, 1)
                kind, i = splits(u, last)
                if kind:
                    split(kind, 2 * b + i, i % 2)

            for kind in ("q", "kv", "o"):
                split(kind, 0, 0)
            slots(pool, slot)

        @block.vector
        def _(dve):
            dve.sem_inc(added, 1)
            norm_vector(ln, dve)
            dve.wait_ge(mask_in, 16)
            dve.tensor_reduce(valid[:], mask_raw[:], AX.X, ALU.max).then_inc(bias_done, 1)
            dve.wait_ge(bias_done, 2)

            def slot(b, u, last):
                turn, score, product, keys = parts(u, last)
                n = b * PAIR + u
                if turn:
                    for h in range(QH):
                        dve.wait_ge(pt_hi_done, 2 * n + h + 1)
                        dve.tensor_tensor(pt_lo[:, u % 2, :, h, :], t_ps[h][0:SL, 0:SCH * T].rearrange("s (c t) -> s c t", c=SCH),
                                          pt_hi[:, u % 2, :, h, :].bitcast(F32), ALU.subtract).then_inc(pt_lo_done, 1)
                if score:
                    w = (u + 1) % 2
                    for h in range(QH):
                        dve.wait_ge(s_done, 2 * n + h + 3)
                        wait(dve, t_done, 2 * n - 1 + h)
                        dve.sem_inc(held_dve, 1)
                        dve.tensor_tensor_reduce(prob[:, w, h, :], s_ps[h][0:T, 0:S], bias[:, (u + 1) % HB, :],
                                                 -(HD ** -0.5), 3e38, ALU.add, ALU.min,
                                                 least[:, w, h:h + 1]).then_inc(max_done, 1)
                if product:
                    m = (u - 1) % HB
                    dve.wait_ge(r_done, n)
                    dve.tensor_tensor(x[:, m, :], r_ps[0:T, :], x[:, m, :], ALU.add).then_inc(added, 1)
                if score:
                    dve.wait_ge(exp_done, 2 * n + 4)
                    wait(dve, norm_done, 2 * n)
                    dve.reciprocal(recip[:, w, :], total[:, w, :]).then_inc(recip_done, 1)
                if keys:
                    w = u + 2
                    if w % TGB == 0:
                        for h, bank in enumerate((k_ps, v_ps)):
                            dve.wait_ge(q_hi_done, b * (PAIR // TGB * QH) + w // TGB * QH + h + 1)
                            dve.tensor_tensor(q_lo[:, w // TGB % 2, h, :], bank[:, 0:TGT], q_hi[:, w // TGB % 2, h, :].bitcast(F32),
                                              ALU.subtract).then_inc(q_lo_done, 1)
                    dve.wait_ge(k_hi_done, n + 3)
                    dve.tensor_tensor(k_lo[:, w % 2, :], k_ps[:, 0:SE], k_hi[:, w % 2, :].bitcast(F32), ALU.subtract).then_inc(k_lo_done, 1)
                if turn:
                    dve.wait_ge(o_hi_done, n + 1)
                    dve.tensor_tensor(o_lo[:, u % 2, :], o_ps[:, 0:QH * T], o_hi[:, u % 2, :].bitcast(F32), ALU.subtract).then_inc(o_lo_done, 1)
                if keys:
                    dve.wait_ge(v_hi_done, n + 3)
                    dve.tensor_tensor(v_lo[:, w % 2, :], v_ps[0:SL, 0:SCH * HD], v_hi[:, w % 2, :].bitcast(F32),
                                      ALU.subtract).then_inc(v_lo_done, 1)

            slots(dve, slot)


def xattn_phase(nc, x_dram, ctx_dram, mask_dram, w_dram, ident_dram, out_dram):
    for half in range(2):
        xattn_half(nc, half, x_dram, ctx_dram, mask_dram, w_dram, ident_dram, out_dram)

E_N = 8
I_N = 352
IS_N = 1408
FT = TOKENS // P
FCH = (E_N * I_N + IS_N) // P
BCH = 3
NBLK = FCH // BCH
GU = 2 * KD * P
WCH = GU + DM
PIECE = 32
NPIECE = FCH * P // PIECE
EPIECE = I_N // PIECE
TG = [(0, 2), (2, 4), (6, 4), (10, 4)]
STEPS = len(TG) * BCH


def ffn_phase(nc, x_dram, w_dram, router_dram, rank_dram, ident_dram, c_dram, cexp_dram, out_dram):
    with ExitStack() as ctx:
        sb, ps, sem = opener(nc, ctx, "ff")
        x = sb("x", [P, FT, DM])
        xt_hi = sb("xt_hi", [P, KD, TOKENS], F32R)
        xt_lo = sb("xt_lo", [P, KD, TOKENS], F32R)
        w_raw = sb("w_raw", [P, BCH, WCH])
        w_hi = sb("w_hi", [P, BCH, WCH], F32R)
        w_lo = sb("w_lo", [P, BCH, WCH], F32R)
        scale = sb("scale", [P, BCH, TOKENS])
        silu = sb("silu", [P, 2, 512])
        scaled = sb("scaled", [P, 2, 512])
        h = sb("h", [P, 2, 512])
        h_hi = sb("h_hi", [P, 2, 512], F32R)
        h_lo = sb("h_lo", [P, 2, 512], F32R)
        ident = sb("ident", [P, P])
        r_raw = sb("r_raw", [P, KD, E_N + 2])
        r_hi = sb("r_hi", [P, KD, E_N + 2], F32R)
        r_lo = sb("r_lo", [P, KD, E_N + 2], F32R)
        rank = sb("rank", [P, FT, E_N])
        logits = sb("logits", [P, FT, E_N + 2])
        prob = sb("prob", [P, FT, E_N])
        rest = sb("rest", [P, FT, E_N])
        key = sb("key", [P, FT, E_N])
        first = sb("first", [P, FT, E_N])
        stat = sb("stat", [P, 4, FT])
        comb = sb("comb", [P, FT, E_N + 1])
        comb_t = sb("comb_t", [E_N + 1, TOKENS])

        gate_ps = [ps(f"gate{i}", [P, 512]) for i in range(2)]
        up_ps = [ps(f"up{i}", [P, 512]) for i in range(2)]
        acc = [ps(f"acc{i}", [P, 512]) for i in range(4)]

        ln = Norm(sb, sem, P, FT, x, xt_hi, xt_lo, ident, acc, [(0, 2), (2, 6), (6, 10), (10, 14)])
        router_in = sem("router_in")
        r_split = sem("r_split")
        logits_ps = sem("logits_ps")
        routed = sem("routed")
        exp_done = sem("exp_done")
        comb_turned = sem("comb_turned")
        comb_out = sem("comb_out")
        c_stored = sem("c_stored")
        w_in = [sem(f"w_in{j}") for j in range(BCH)]
        scale_in = [sem(f"scale_in{j}") for j in range(BCH)]
        gu_hi = [sem(f"gu_hi{j}") for j in range(BCH)]
        gu_lo = [sem(f"gu_lo{j}") for j in range(BCH)]
        dn_hi = [sem(f"dn_hi{j}") for j in range(BCH)]
        dn_lo = [sem(f"dn_lo{j}") for j in range(BCH)]
        gu_done = sem("gu_done")
        silu_done = sem("silu_done")
        scaled_done = sem("scaled_done")
        h_done = sem("h_done")
        h_hi_done = sem("h_hi_done")
        h_lo_done = sem("h_lo_done")
        down_done = sem("down_done")
        acc_done = sem("acc_done")
        added = sem("added")
        stored = sem("stored")

        def n_tok(s):
            return TG[s // BCH][1] * P

        def tok(s):
            return TG[s // BCH][0] * P

        block = ctx.enter_context(nc.Block())

        @block.sync
        def _(sp):
            norm_load(ln, sp, x_dram.rearrange("(t p) d -> p t d", p=P), ident_dram)
            sp.dma_start(r_raw[:], router_dram).then_inc(router_in, 16)
            sp.dma_start(rank[:], rank_dram).then_inc(router_in, 16)
            for j in range(BCH):
                sp.dma_start(w_raw[:, j, :], w_dram[j]).then_inc(w_in[j], 16)
            sp.wait_ge(comb_out, 4)
            sp.dma_start(c_dram, comb_t[:]).then_inc(c_stored, 16)
            sp.wait_ge(c_stored, 16)
            sp.dma_start(cexp_dram[0:E_N * EPIECE, :].rearrange("(e r) t -> e r t", r=EPIECE),
                         c_dram[0:E_N, :].unsqueeze(1).to_broadcast([E_N, EPIECE, TOKENS])).then_inc(c_stored, 16)
            sp.dma_start(cexp_dram[E_N * EPIECE:NPIECE, :],
                         c_dram[E_N:E_N + 1, :].to_broadcast([NPIECE - E_N * EPIECE, TOKENS])).then_inc(c_stored, 16)
            sp.wait_ge(c_stored, 48)

            def load_scale(b, j):
                for r in range(P // PIECE):
                    q = (b * BCH + j) * (P // PIECE) + r
                    sp.dma_start(scale[r * PIECE:(r + 1) * PIECE, j, :],
                                 cexp_dram[bass.ds(q, 1), :].to_broadcast([PIECE, TOKENS])).then_inc(scale_in[j], 16)

            def load_weights(b, j):
                sp.wait_ge(gu_lo[j], b)
                sp.wait_ge(dn_lo[j], b)
                sp.dma_start(w_raw[:, j, :], w_dram[bass.ds(b * BCH + j, 1)].rearrange("o p n -> p (o n)")).then_inc(w_in[j], 16)

            for j in range(BCH):
                load_scale(0, j)
            for j in range(BCH):
                load_weights(1, j)
            with sp.Fori(1, NBLK - 1) as b:
                for j in range(BCH):
                    sp.wait_ge(scaled_done, (b - 1) * STEPS + STEPS - BCH + j + 3)
                    load_scale(b, j)
                    load_weights(b + 1, j)
            for j in range(BCH):
                sp.wait_ge(scaled_done, (NBLK - 2) * STEPS + STEPS - BCH + j + 3)
                load_scale(NBLK - 1, j)
            out_v = out_dram.rearrange("(t p) d -> p t d", p=P)
            for g, (t, n) in enumerate(TG):
                sp.wait_ge(added, NBLK * FT + t + n)
                sp.dma_start(out_v[:, t:t + n, :], x[:, t:t + n, :]).then_inc(stored, 16)
            sp.wait_ge(stored, 16 * len(TG))

        @block.tensor
        def _(pe):
            norm_tensor(ln, pe)
            pe.wait_ge(r_split, 2)
            pe.wait_ge(ln.lo_done, FT)
            for t in range(FT):
                for k in range(KD):
                    a = slice(t * P, (t + 1) * P)
                    ins = matmul_split(pe, gate_ps[0][:, t * (E_N + 2):(t + 1) * (E_N + 2)], xt_hi[:, k, a], xt_lo[:, k, a],
                                       r_hi[:, k, :], r_lo[:, k, :], k == 0, k == KD - 1)
            ins.then_inc(logits_ps, 1)
            pe.wait_ge(r_split, 5)
            for t in range(FT):
                ins = pe.transpose(acc[t // 4][0:E_N + 1, (t % 4) * P:(t % 4 + 1) * P], comb[:, t, :], ident[:])
                if t % 4 == 3 or t == FT - 1:
                    ins.then_inc(comb_turned, 1)
            pe.wait_ge(comb_out, 4)

            def gate_up(b, s, first=False):
                j, n, a = s % BCH, n_tok(s), tok(s)
                if s < BCH:
                    pe.wait_ge(gu_lo[j], b + 1)
                if not first:
                    pe.wait_ge(h_done, b * STEPS + s + 1)
                for bank, o in ((gate_ps[s % 2], 0), (up_ps[s % 2], KD * P)):
                    for k in range(KD):
                        w = slice(o + k * P, o + (k + 1) * P)
                        ins = matmul_split(pe, bank[:, 0:n], w_hi[:, j, w], w_lo[:, j, w],
                                           xt_hi[:, k, a:a + n], xt_lo[:, k, a:a + n], k == 0, k == KD - 1)
                ins.then_inc(gu_done, 1)

            def down(b, s):
                j, (t0, nt) = s % BCH, TG[s // BCH]
                if s < BCH:
                    pe.wait_ge(dn_lo[j], b + 1)
                pe.wait_ge(h_lo_done, b * STEPS + s + 1)
                for m in range(nt):
                    if j == 0:
                        g = s // BCH - 1
                        if g >= 0:
                            pe.wait_ge(added, (b + 1) * FT + TG[g][0] + min(m + 1, TG[g][1]))
                        else:
                            pe.wait_ge(added, b * FT + TG[-1][0] + m + 1)
                    a, w = slice(m * P, (m + 1) * P), slice(GU, WCH)
                    ins = matmul_split(pe, acc[m][:], h_hi[:, s % 2, a], h_lo[:, s % 2, a],
                                       w_hi[:, j, w], w_lo[:, j, w], j == 0, j == BCH - 1)
                    if j == BCH - 1:
                        ins.then_inc(acc_done, 1)
                if j < BCH - 1:
                    ins.then_inc(down_done, 1)

            def one_block(b, last):
                for s in range(1, STEPS):
                    gate_up(b, s)
                    down(b, s - 1)
                if not last:
                    gate_up(b + 1, 0)
                down(b, STEPS - 1)

            gate_up(0, 0, first=True)
            with pe.Fori(0, NBLK - 1) as b:
                one_block(b, False)
            one_block(NBLK - 1, True)

        @block.scalar
        def _(act):
            norm_scalar(ln, act)
            act.wait_ge(routed, 1)
            act.activation(prob[:], rest[:], ACT.Exp).then_inc(exp_done, 1)
            act.activation(comb[:, :, E_N], logits[:, :, E_N], ACT.Sigmoid).then_inc(exp_done, 1)

            def split_gu(b, j, first=False):
                act.wait_ge(w_in[j], 16 * (b + 1))
                if not first:
                    act.wait_ge(gu_done, b * STEPS - BCH + j + 1)
                act.activation(w_hi[:, j, 0:GU], w_raw[:, j, 0:GU], ACT.Copy).then_inc(gu_hi[j], 1)

            def split_dn(b, j, first=False):
                if not first and j < BCH - 1:
                    act.wait_ge(down_done, b * len(TG) * (BCH - 1) - (BCH - 1) + j + 1)
                elif not first:
                    act.wait_ge(acc_done, b * FT)
                act.activation(w_hi[:, j, GU:WCH], w_raw[:, j, GU:WCH], ACT.Copy).then_inc(dn_hi[j], 1)

            def step(b, s, first=False):
                n = n_tok(s)
                act.wait_ge(gu_done, b * STEPS + s + 1)
                if not first:
                    act.wait_ge(scaled_done, b * STEPS + s + 1)
                act.activation(silu[:, s % 2, 0:n], gate_ps[s % 2][:, 0:n], ACT.Silu).then_inc(silu_done, 1)
                act.wait_ge(h_done, b * STEPS + s + 3)
                act.activation(h_hi[:, s % 2, 0:n], h[:, s % 2, 0:n], ACT.Copy).then_inc(h_hi_done, 1)

            def one_block(b, last):
                for s in range(1, STEPS + 1):
                    if s < STEPS:
                        step(b, s)
                    elif not last:
                        step(b + 1, 0)
                    if s >= STEPS - BCH and s < STEPS and not last:
                        split_gu(b + 1, s - (STEPS - BCH))
                    if s > STEPS - BCH and not last:
                        split_dn(b + 1, s - (STEPS - BCH) - 1)

            for j in range(BCH):
                split_gu(0, j, first=True)
                split_dn(0, j, first=True)
            step(0, 0, first=True)
            with act.Fori(0, NBLK - 1) as b:
                one_block(b, False)
            one_block(NBLK - 1, True)

        @block.gpsimd
        def _(pool):
            def split_gu(b, j):
                pool.wait_ge(gu_hi[j], b + 1)
                pool.tensor_tensor(w_lo[:, j, 0:GU], w_raw[:, j, 0:GU], w_hi[:, j, 0:GU].bitcast(F32),
                                   ALU.subtract).then_inc(gu_lo[j], 1)

            def split_dn(b, j):
                pool.wait_ge(dn_hi[j], b + 1)
                pool.tensor_tensor(w_lo[:, j, GU:WCH], w_raw[:, j, GU:WCH], w_hi[:, j, GU:WCH].bitcast(F32),
                                   ALU.subtract).then_inc(dn_lo[j], 1)

            def step(b, s, first=False):
                n, a, j = n_tok(s), tok(s), s % BCH
                if s < BCH:
                    pool.wait_ge(scale_in[j], 16 * (P // PIECE) * (b + 1))
                pool.wait_ge(silu_done, b * STEPS + s + 1)
                if not first:
                    pool.wait_ge(h_done, b * STEPS + s + 1)
                pool.tensor_tensor(scaled[:, s % 2, 0:n], silu[:, s % 2, 0:n], scale[:, j, a:a + n],
                                   ALU.mult).then_inc(scaled_done, 1)

            def one_block(b, last):
                for s in range(1, STEPS + 1):
                    if s < STEPS:
                        step(b, s)
                    elif not last:
                        step(b + 1, 0)
                    if s >= STEPS - BCH and s < STEPS and not last:
                        split_gu(b + 1, s - (STEPS - BCH))
                    if s > STEPS - BCH and not last:
                        split_dn(b + 1, s - (STEPS - BCH) - 1)

            for j in range(BCH):
                split_gu(0, j)
                split_dn(0, j)
            step(0, 0, first=True)
            with pool.Fori(0, NBLK - 1) as b:
                one_block(b, False)
            one_block(NBLK - 1, True)

        @block.vector
        def _(dve):
            dve.sem_inc(added, FT)
            dve.sem_inc(h_done, 2)
            dve.sem_inc(scaled_done, 2)
            norm_vector(ln, dve)
            dve.wait_ge(router_in, 32)
            dve.tensor_copy(r_hi[:], r_raw[:]).then_inc(r_split, 1)
            dve.wait_ge(r_split, 1)
            dve.tensor_tensor(r_lo[:], r_raw[:], r_hi[:].bitcast(F32), ALU.subtract).then_inc(r_split, 1)

            chain = [0]

            def link(ins):
                chain[0] += 1
                ins.then_inc(routed, 1)
                dve.wait_ge(routed, chain[0])

            def wide(a):
                return a.unsqueeze(2).to_broadcast([P, FT, E_N])

            top, total, top1, top2 = (stat[:, i, :] for i in range(4))
            dve.wait_ge(logits_ps, 1)
            dve.tensor_copy(logits[:], gate_ps[0][:, 0:FT * (E_N + 2)].rearrange("p (t e) -> p t e", e=E_N + 2)).then_inc(r_split, 1)
            dve.wait_ge(r_split, 3)
            dve.tensor_reduce(top, logits[:, :, 0:E_N], AX.X, ALU.max).then_inc(r_split, 1)
            dve.wait_ge(r_split, 4)
            link(dve.tensor_tensor(rest[:], logits[:, :, 0:E_N], wide(top), ALU.subtract))
            dve.wait_ge(exp_done, 2)
            link(dve.tensor_reduce(total, prob[:], AX.X, ALU.add))
            link(dve.reciprocal(total, total))
            link(dve.tensor_tensor(prob[:], prob[:], wide(total), ALU.mult))

            def choose(out, of, best):
                link(dve.tensor_reduce(best, of, AX.X, ALU.max))
                link(dve.tensor_tensor(key[:], of, wide(best), ALU.is_equal))
                link(dve.tensor_tensor(key[:], key[:], rank[:], ALU.mult))
                link(dve.tensor_reduce(top, key[:], AX.X, ALU.max))
                link(dve.tensor_tensor(out, key[:], wide(top), ALU.is_equal))

            choose(first[:], prob[:], top1)
            link(dve.scalar_tensor_tensor(rest[:], first[:], -2.0, prob[:], ALU.mult, ALU.add))
            choose(key[:], rest[:], top2)
            link(dve.tensor_tensor(first[:], first[:], key[:], ALU.add))
            link(dve.tensor_tensor(first[:], first[:], prob[:], ALU.mult))
            link(dve.tensor_tensor(total, top1, top2, ALU.add))
            link(dve.reciprocal(total, total))
            dve.tensor_tensor(comb[:, :, 0:E_N], first[:], wide(total), ALU.mult).then_inc(r_split, 1)
            for i in range(4):
                dve.wait_ge(comb_turned, i + 1)
                n = min(4, FT - 4 * i) * P
                dve.tensor_copy(comb_t[:, 512 * i:512 * i + n], acc[i][0:E_N + 1, 0:n]).then_inc(comb_out, 1)

            def step(b, s):
                n = n_tok(s)
                dve.wait_ge(scaled_done, b * STEPS + s + 3)
                dve.tensor_tensor(h[:, s % 2, 0:n], up_ps[s % 2][:, 0:n], scaled[:, s % 2, 0:n],
                                  ALU.mult).then_inc(h_done, 1)
                dve.wait_ge(h_hi_done, b * STEPS + s + 1)
                dve.tensor_tensor(h_lo[:, s % 2, 0:n], h[:, s % 2, 0:n], h_hi[:, s % 2, 0:n].bitcast(F32),
                                  ALU.subtract).then_inc(h_lo_done, 1)

            def one_block(b, last):
                for s in range(1, STEPS + 1):
                    if s < STEPS:
                        step(b, s)
                    elif not last:
                        step(b + 1, 0)
                    if s % BCH == 0:
                        t0, nt = TG[s // BCH - 1]
                        for m in range(nt):
                            dve.wait_ge(acc_done, b * FT + t0 + m + 1)
                            dve.tensor_tensor(x[:, t0 + m, :], acc[m][:], x[:, t0 + m, :], ALU.add).then_inc(added, 1)

            step(0, 0)
            with dve.Fori(0, NBLK - 1) as b:
                one_block(b, False)
            one_block(NBLK - 1, True)


def build(nc, d, out):
    x1 = nc.dram_tensor("x1", (TOKENS, DM), F32, kind="Internal").ap()
    attn_phase(nc, d["x"], d, x1)
    x2 = nc.dram_tensor("x2", (TOKENS, DM), F32, kind="Internal").ap()
    xattn_phase(nc, x1, d["ctx_t"], d["mask"], d["w_xattn"], d["ident"], x2)
    c = nc.dram_tensor("c_scratch", (E_N + 1, TOKENS), F32, kind="Internal").ap()
    cexp = nc.dram_tensor("c_spread", (NPIECE, TOKENS), F32, kind="Internal").ap()
    ffn_phase(nc, x2, d["w_ffn"], d["router"], d["rank"], d["ident"], c, cexp, out)



def kernel(x, ctx_1024, mask_BxS2_bf1, L0_attn_W_in, L0_attn_b_in, L0_attn_conv_w, L0_attn_conv_b, L0_attn_A_log,
           L0_attn_D_param, L0_attn_dt_bias, L0_attn_norm_w, L0_attn_W_out, L0_attn_b_out, L0_attn_mup_vector,
           L0_xattn_Wq, L0_xattn_Wk, L0_xattn_Wv, L0_xattn_Wo, L0_ffn_gate_w, L0_ffn_w_gate, L0_ffn_w_up,
           L0_ffn_w_down, L0_ffn_sw_gate, L0_ffn_sw_up, L0_ffn_sw_down, L0_ffn_shared_gate_w):
    import numpy as np
    import concourse.bacc as bacc
    from concourse import mybir
    from concourse.bass_utils import run_bass_kernel_spmd

    f = lambda a: np.ascontiguousarray(a)

    def feature_chunks(w, width=128):
        k, n = w.shape
        return w.reshape(k // 128, 128, n // width, width).transpose(2, 1, 0, 3)

    arrays = {
        "x": f(x).reshape(1792, 512),
        "ident": np.eye(128, dtype=np.float32),
    }
    gate = np.concatenate([f(L0_ffn_w_gate).transpose(1, 0, 2).reshape(512, 2816), f(L0_ffn_sw_gate)], 1)
    up = np.concatenate([f(L0_ffn_w_up).transpose(1, 0, 2).reshape(512, 2816), f(L0_ffn_sw_up)], 1)
    down = np.concatenate([f(L0_ffn_w_down).reshape(2816, 512), f(L0_ffn_sw_down)], 0)
    arrays["w_ffn"] = np.concatenate([feature_chunks(gate).reshape(33, 128, 512), feature_chunks(up).reshape(33, 128, 512),
                                      down.reshape(33, 128, 512)], 2)
    router = np.concatenate([f(L0_ffn_gate_w).T, f(L0_ffn_shared_gate_w), np.zeros((512, 1), np.float32)], 1)
    arrays["router"] = router.reshape(4, 128, 10).transpose(1, 0, 2)
    arrays["rank"] = np.broadcast_to(np.arange(8, 0, -1, dtype=np.float32), (128, 14, 8))
    ctx_t = f(ctx_1024).transpose(0, 2, 1)
    arrays["ctx_t"] = np.concatenate([ctx_t, np.zeros((16, 256, 1), np.float32)], 2)
    arrays["mask"] = f(mask_BxS2_bf1).view(np.uint8).reshape(2, 8, 375)
    wq = f(L0_xattn_Wq).reshape(4, 128, 8, 256).transpose(2, 1, 0, 3).reshape(8, 128, 1024)
    wk = f(L0_xattn_Wk).reshape(2, 128, 8, 128).transpose(2, 1, 0, 3).reshape(8, 128, 256)
    wv = f(L0_xattn_Wv).reshape(2, 128, 8, 128).transpose(2, 1, 0, 3).reshape(8, 128, 256)
    wo = f(L0_xattn_Wo).reshape(8, 2, 128, 512).transpose(0, 2, 1, 3).reshape(8, 128, 1024)
    arrays["w_xattn"] = np.concatenate([wq, wk, wv, wo], 2)
    w_in = f(L0_attn_W_in)
    xz = np.concatenate([w_in[:, 2048:4096], w_in[:, 0:2048]], 1)
    xz = feature_chunks(xz).reshape(2, 8, 2, 128, 512).transpose(1, 3, 0, 2, 4).reshape(8, 128, 2048)
    w_out = f(L0_attn_W_out).reshape(8, 2, 128, 512).transpose(0, 2, 1, 3).reshape(8, 128, 1024)
    arrays["w_mix"] = np.concatenate([xz, w_out], 2)
    bcdt = np.concatenate([w_in[:, 4096:4640], np.zeros((512, 96), np.float32)], 1)
    arrays["w_bcdt"] = bcdt.reshape(4, 128, 640).transpose(1, 0, 2)

    def channels(a, first, n):
        return f(a)[first:first + n]

    def params(first, n):
        p = np.zeros((n, 8), np.float32)
        p[:, 0], p[:, 1] = channels(L0_attn_b_in, first, n), channels(L0_attn_mup_vector, first, n)
        if first >= 2048:
            p[:, 2:6], p[:, 6] = channels(L0_attn_conv_w, first - 2048, n), channels(L0_attn_conv_b, first - 2048, n)
        return p

    par_x = params(2048, 2048).reshape(8, 2, 128, 8)
    par_z = params(0, 2048).reshape(8, 2, 128, 8)
    par_n = np.zeros((8, 1, 128, 8), np.float32)
    par_n[:, 0, :, 0:2] = f(L0_attn_norm_w).reshape(8, 2, 128).transpose(0, 2, 1)
    arrays["par_mix"] = np.concatenate([par_x, par_z, par_n], 1).transpose(0, 2, 1, 3)
    par_dt = np.zeros((128, 8), np.float32)
    par_dt[0:32, 0], par_dt[0:32, 1] = channels(L0_attn_b_in, 4608, 32), channels(L0_attn_mup_vector, 4608, 32)
    par_dt[0:32, 2], par_dt[0:32, 7] = f(L0_attn_A_log), f(L0_attn_dt_bias)
    arrays["par_bcdt"] = np.concatenate([params(4096, 512).reshape(4, 128, 8), par_dt.reshape(1, 128, 8)], 0).transpose(1, 0, 2)
    arrays["tri"] = np.triu(np.ones((112, 112), np.float32))
    arrays["below"] = np.tril(np.ones((112, 112), np.float32), -1)
    arrays["skip"] = f(L0_attn_D_param).reshape(1, 32)
    arrays["b_out"] = f(L0_attn_b_out).reshape(1, 512)

    nc = bacc.Bacc("TRN2", target_bir_lowering=False, num_devices=1)
    arrays = {f"in_{k}_dram": f(a) for k, a in arrays.items()}
    given = {k: nc.dram_tensor(k, a.shape, mybir.dt.from_np(a.dtype), kind="ExternalInput").ap()
             for k, a in arrays.items()}
    out = nc.dram_tensor("out_0_dram", (1792, 512), mybir.dt.float32, kind="ExternalOutput").ap()
    build(nc, {k[3:-5]: a for k, a in given.items()}, out)
    r = run_bass_kernel_spmd(nc, [arrays], core_ids=[0])
    return r.results[0]["out_0_dram"].reshape(16, 112, 512)
```

```python
from contextlib import ExitStack

import concourse.bass as bass
from concourse import mybir

F32 = mybir.dt.float32
F32R = mybir.dt.float32r
ALU = mybir.AluOpType
ACT = mybir.ActivationFunctionType
AX = mybir.AxisListType

P = 128
DM = 512
KD = DM // P
LN_EPS = 1e-5
TOKENS = 16 * 112


def opener(nc, ctx, prefix):
    def sb(name, shape, dt=F32):
        return ctx.enter_context(nc.sbuf_tensor(f"{prefix}_{name}", shape, dt))

    def ps(name, shape):
        return ctx.enter_context(nc.psum_tensor(f"{prefix}_ps_{name}", shape, F32))

    used = []

    def sem(name):
        used.append(nc.alloc_semaphore(f"{prefix}_{name}"))
        return used[-1]

    def give_back():
        if used:
            nc.clear_and_free_semaphores(used)
            nc.all_engine_barrier()

    ctx.callback(give_back)

    return sb, ps, sem


def matmul_split(pe, out, w_hi, w_lo, x_hi, x_lo, start, stop):
    pe.matmul(out, w_hi, x_hi, start=start, stop=False)
    pe.matmul(out, w_hi, x_lo, start=False, stop=False)
    return pe.matmul(out, w_lo, x_hi, start=False, stop=stop)



class Norm:

    def __init__(self, sb, sem, rows, tiles, x, xt_hi, xt_lo, ident, banks, loads):
        self.rows, self.tiles, self.x, self.xt_hi, self.xt_lo = rows, tiles, x, xt_hi, xt_lo
        self.ident, self.banks, self.loads = ident, banks, loads
        self.stats = sb("ln_stats", [rows, tiles, 6])
        self.mv = sb("ln_mv", [rows, tiles, 2])
        self.std = sb("ln_std", [rows, tiles])
        self.rstd = sb("ln_rstd", [rows, tiles])
        self.shift = sb("ln_shift", [rows, tiles])
        self.xn = sb("ln_xn", [rows, 2, DM])
        self.x_in = [sem(f"ln_x_in{n}") for n in range(len(loads))]
        self.ident_in = sem("ln_ident_in")
        self.stats_done = sem("ln_stats_done")
        self.moments = sem("ln_moments")
        self.std_done = sem("ln_std_done")
        self.rstd_done = sem("ln_rstd_done")
        self.xn_done = sem("ln_xn_done")
        self.turned = sem("ln_turned")
        self.hi_done = sem("ln_hi_done")
        self.lo_done = sem("ln_lo_done")


def norm_load(s, eng, x_dram, ident_dram):
    eng.dma_start(s.ident[:], ident_dram).then_inc(s.ident_in, 16)
    for n, (a, b) in enumerate(s.loads):
        eng.dma_start(s.x[:, a:b, :], x_dram[:, a:b, :]).then_inc(s.x_in[n], 16)


def norm_vector(s, dve):

    def low(t):
        dve.wait_ge(s.hi_done, t + 1)
        cols = slice(t * s.rows, (t + 1) * s.rows)
        dve.tensor_tensor(s.xt_lo[:, :, cols], turned_view(s, s.banks[t % len(s.banks)]),
                          s.xt_hi[:, :, cols].bitcast(F32), ALU.subtract).then_inc(s.lo_done, 1)

    turned = 0
    for n, (a, b) in enumerate(s.loads):
        dve.wait_ge(s.x_in[n], 16)
        for t in range(a, b):
            dve.bn_stats(s.stats[:, t, :], s.x[:, t, :]).then_inc(s.stats_done, 1)
        for t in range(a, b):
            dve.wait_ge(s.stats_done, t + 1)
            dve.bn_aggr(s.mv[:, t, :], s.stats[:, t, :]).then_inc(s.moments, 1)
        dve.wait_ge(s.moments, b + n)
        dve.tensor_scalar(s.std[:, a:b], s.mv[:, a:b, 1], LN_EPS, None, ALU.add).then_inc(s.moments, 1)
        for t in range(turned, a - 1):
            low(t)
        turned = max(a - 1, 0)
        dve.wait_ge(s.std_done, n + 1)
        dve.reciprocal(s.rstd[:, a:b], s.std[:, a:b]).then_inc(s.rstd_done, 1)
        dve.wait_ge(s.rstd_done, 2 * n + 1)
        dve.scalar_tensor_tensor(s.shift[:, a:b], s.mv[:, a:b, 0], -1.0, s.rstd[:, a:b],
                                 ALU.mult, ALU.mult).then_inc(s.rstd_done, 1)
    for t in range(turned, s.tiles):
        low(t)


def turned_view(s, bank):
    return bank[:, 0:KD * s.rows].rearrange("p (k t) -> p k t", k=KD)


def norm_scalar(s, act):
    def high(t):
        act.wait_ge(s.turned, t + 1)
        act.activation(s.xt_hi[:, :, t * s.rows:(t + 1) * s.rows],
                       turned_view(s, s.banks[t % len(s.banks)]), ACT.Copy).then_inc(s.hi_done, 1)

    for n, (a, b) in enumerate(s.loads):
        act.wait_ge(s.moments, b + n + 1)
        act.activation(s.std[:, a:b], s.std[:, a:b], ACT.Sqrt).then_inc(s.std_done, 1)
        act.wait_ge(s.rstd_done, 2 * n + 2)
        for t in range(a, b):
            if t >= 2:
                act.wait_ge(s.turned, t - 1)
            act.activation(s.xn[:, t % 2, :], s.x[:, t, :], ACT.Identity, bias=s.shift[:, t:t + 1],
                           scale=s.rstd[:, t:t + 1]).then_inc(s.xn_done, 1)
            if t >= 1:
                high(t - 1)
    high(s.tiles - 1)


def norm_tensor(s, pe):
    pe.wait_ge(s.ident_in, 16)
    for t in range(s.tiles):
        pe.wait_ge(s.xn_done, t + 1)
        if t >= len(s.banks):
            pe.wait_ge(s.lo_done, t - len(s.banks) + 1)
        view = turned_view(s, s.banks[t % len(s.banks)])
        for k in range(KD):
            ins = pe.transpose(view[:, k, :], s.xn[:, t % 2, k * P:(k + 1) * P],
                               s.ident[0:s.rows, 0:s.rows])
        ins.then_inc(s.turned, 1)


B = 16
T = 112
HB = B // 2
HT = HB * T
TGB = 4
TGT = TGB * T
NG = 8
NH = 4
HP = 64
ST = 32
GC = NH * HP
GJ = GC // P
HEADS = NG * NH
TAPS = 4
PADT = T + TAPS - 1
WIN = 2 * GJ * DM
WOUT = GJ * DM
NBC = 5
LEAST_LOG = -200.0
MOST_LOG_A = 88.0
SCALED_A = 1024.0
BIAS_, MUP_, TAP_, CONVB_, EXTRA_ = 0, 1, 2, 6, 7
NPAR = 8
NSLOT = 2 * NG


def convolve(dve, out, padded, par, done, base, taps=range(TAPS)):
    for k in taps:
        if k == 0:
            dve.tensor_scalar(out, padded[:, :, 0:T], par[:, TAP_:TAP_ + 1], par[:, CONVB_:CONVB_ + 1],
                              ALU.mult, ALU.add).then_inc(done, 1)
            continue
        dve.wait_ge(done, base + k)
        dve.scalar_tensor_tensor(out, padded[:, :, k:k + T], par[:, TAP_ + k:TAP_ + k + 1], out,
                                 ALU.mult, ALU.add).then_inc(done, 1)


class Kept:

    def __init__(self, sb):
        self.x = sb("x", [T, HB, DM])
        self.xt_hi = sb("xt_hi", [P, KD, HT], F32R)
        self.xt_lo = sb("xt_lo", [P, KD, HT], F32R)
        self.ident = sb("ident", [P, P])
        self.below_raw = sb("below_raw", [T, T])
        self.below = sb("below", [T, T], F32R)
        self.tri = sb("tri", [T, T])
        self.skip = sb("skip", [T, HEADS])
        self.b_out = sb("b_out", [T, DM])
        self.cb = sb("cb", [T, HB, NG, T])
        self.dt = sb("dt", [T, HB, HEADS])
        self.da_hi = sb("da_hi", [T, HB, HEADS], F32R)
        self.da_lo = sb("da_lo", [T, HB, HEADS], F32R)


def attn_prepare(nc, half, x_dram, d, keep):
    with ExitStack() as ctx:
        sb, ps, sem = opener(nc, ctx, f"ap{half}")
        w_raw = sb("w_raw", [P, KD, NBC * P])
        w_hi = sb("w_hi", [P, KD, NBC * P], F32R)
        w_lo = sb("w_lo", [P, KD, NBC * P], F32R)
        par = sb("par", [P, NBC, NPAR])
        bias = sb("bias", [P, NBC])
        a_log = sb("a_log", [T, HEADS])
        rate = sb("rate", [T, HEADS])
        pad = sb("pad", [P, 2, TGB, PADT])
        conv = sb("conv", [P, 2, TGB, T])
        bc = sb("bc", [P, NBC - 1, HT])
        tri = sb("tri", [T, T])
        u_heads = sb("u_heads", [HEADS, HT])
        u, e, w1, lnw, rest, da = (sb(n, [T, HB, HEADS]) for n in ("u", "e", "w1", "lnw", "rest", "da"))
        banks = [ps(f"bank{i}", [P, 512]) for i in range(4)]
        proj = [ps(f"proj{i}", [P, 512]) for i in range(2)]
        ln = Norm(sb, sem, T, HB, keep.x, keep.xt_hi, keep.xt_lo, keep.ident, banks, [(0, 2), (2, 5), (5, 8)])
        w_in, w_hi_done, w_lo_done = sem("w_in"), sem("w_hi_done"), sem("w_lo_done")
        par_in, bias_done = sem("par_in"), sem("bias_done")
        const_in, const_done = sem("const_in"), sem("const_done")
        zeroed = sem("zeroed")
        proj_done, drained, conv_done, silu_done = sem("proj_done"), sem("drained"), sem("conv_done"), sem("silu_done")
        cb_done, cb_out = sem("cb_done"), sem("cb_out")
        soft, exp_done = sem("soft"), sem("exp_done")
        u_turned, u_out = sem("u_turned"), sem("u_out")
        x_biased = sem("x_biased")
        NC4 = NBC - 1
        products = [(g, NC4) for g in range(2)] + [(g, c) for g in range(2) for c in range(NC4)]
        block = ctx.enter_context(nc.Block())

        @block.sync
        def _(sp):
            norm_load(ln, sp, x_dram.rearrange("(b t) d -> t b d", t=T)[:, half * HB:(half + 1) * HB, :], d["ident"])
            sp.dma_start(par[:], d["par_bcdt"]).then_inc(par_in, 16)
            sp.dma_start(a_log[:], d["a_log"].to_broadcast([T, HEADS])).then_inc(par_in, 16)
            sp.dma_start(w_raw[:], d["w_bcdt"]).then_inc(w_in, 16)
            sp.dma_start(tri[:], d["tri"]).then_inc(const_in, 16)
            sp.dma_start(keep.below_raw[:], d["below"]).then_inc(const_in, 16)
            sp.dma_start(keep.skip[:], d["skip"].to_broadcast([T, HEADS])).then_inc(const_in, 16)
            sp.dma_start(keep.b_out[:], d["b_out"].to_broadcast([T, DM])).then_inc(const_in, 16)

        @block.gpsimd
        def _(pool):
            pool.memset(pad[:, :, :, 0:TAPS - 1], 0.0).then_inc(zeroed, 1)
            pool.wait_ge(w_in, 16)
            for i, c in enumerate((NC4, 0, 1, 2, 3)):
                w = slice(c * P, (c + 1) * P)
                pool.tensor_copy(w_hi[:, :, w], w_raw[:, :, w]).then_inc(w_hi_done, 1)
                pool.wait_ge(w_hi_done, i + 1)
                pool.tensor_tensor(w_lo[:, :, w], w_raw[:, :, w], w_hi[:, :, w].bitcast(F32), ALU.subtract).then_inc(w_lo_done, 1)
            pool.wait_ge(const_in, 64)
            pool.tensor_copy(keep.tri[:], tri[:]).then_inc(const_done, 1)
            pool.wait_ge(ln.xn_done, HB)
            for b in range(HB):
                pool.tensor_tensor(keep.x[:, b, :], keep.x[:, b, :], keep.b_out[:], ALU.add).then_inc(x_biased, 1)

        @block.tensor
        def _(pe):
            norm_tensor(ln, pe)
            pe.wait_ge(ln.lo_done, HB)
            for n, (g, c) in enumerate(products):
                if n < 2 or c != products[n - 1][1]:
                    pe.wait_ge(w_lo_done, min(n, NBC) if n else 1)
                if n >= 2:
                    pe.wait_ge(drained, n - 1)
                a = slice(g * TGT, (g + 1) * TGT)
                for k in range(KD):
                    w = slice(c * P, (c + 1) * P)
                    ins = matmul_split(pe, proj[n % 2][:, 0:TGT], w_hi[:, k, w], w_lo[:, k, w],
                                       keep.xt_hi[:, k, a], keep.xt_lo[:, k, a], k == 0, k == KD - 1)
                ins.then_inc(proj_done, 1)
                if n == 2:
                    pe.wait_ge(drained, 2)
                    for b in range(HB):
                        ins = pe.transpose(banks[0][0:T, b * HEADS:(b + 1) * HEADS], u_heads[:, b * T:(b + 1) * T], keep.ident[0:HEADS, 0:HEADS])
                    ins.then_inc(u_turned, 1)
            pe.wait_ge(silu_done, 2 * NC4)
            for b in range(0, HB, 2):
                for r in range(4):
                    if b:
                        pe.wait_ge(cb_out, (b // 2 - 1) * 4 + r + 1)
                    elif r == 0:
                        pe.wait_ge(u_out, 1)
                    rows = slice(r * ST, (r + 1) * ST)
                    for i in range(2):
                        for q in range(2):
                            o = (i * 2 + q) * T
                            a = slice((b + i) * T, (b + i + 1) * T)
                            ins = pe.matmul(banks[r][0:T, o:o + T], bc[rows, q, a], bc[rows, 2 + q, a], start=True, stop=True)
                    ins.then_inc(cb_done, 1)

        def silu(act, m):
            g, c = m // NC4, m % NC4
            act.wait_ge(conv_done, TAPS * (m + 1))
            act.activation(bc[:, c, g * TGT:(g + 1) * TGT].rearrange("p (b t) -> p b t", b=TGB), conv[:, c % 2], ACT.Silu).then_inc(silu_done, 1)

        @block.scalar
        def _(act):
            norm_scalar(ln, act)
            act.wait_ge(bias_done, 3)
            act.activation(rate[:], a_log[:], ACT.Exp).then_inc(exp_done, 1)
            act.wait_ge(zeroed, 1)
            for n, (g, c) in enumerate(products):
                act.wait_ge(proj_done, n + 1)
                if c == NC4:
                    act.activation(u_heads[:, g * TGT:(g + 1) * TGT], proj[n % 2][0:HEADS, 0:TGT], ACT.Identity,
                                   bias=bias[0:HEADS, c:c + 1], scale=par[0:HEADS, c, MUP_:MUP_ + 1]).then_inc(drained, 1)
                    continue
                m = n - 2
                if m >= 2:
                    act.wait_ge(conv_done, TAPS * (m - 1))
                act.activation(pad[:, m % 2, :, TAPS - 1:], proj[n % 2][:, 0:TGT].rearrange("p (b t) -> p b t", b=TGB),
                               ACT.Identity, bias=bias[:, c:c + 1], scale=par[:, c, MUP_:MUP_ + 1]).then_inc(drained, 1)
                if m == 0:
                    act.wait_ge(u_turned, 1)
                    act.activation(u[:].rearrange("t b h -> t (b h)"), banks[0][0:T, 0:HB * HEADS], ACT.Copy).then_inc(u_out, 1)
                    act.wait_ge(soft, 1)
                    act.activation(e[:], e[:], ACT.Exp, scale=-1.0).then_inc(exp_done, 1)
                    act.wait_ge(soft, 2)
                    act.activation(lnw[:], w1[:], ACT.Ln).then_inc(exp_done, 1)
                else:
                    silu(act, m - 1)
            silu(act, 2 * NC4 - 1)

        @block.vector
        def _(dve):
            norm_vector(ln, dve)
            dve.wait_ge(par_in, 32)
            dve.tensor_tensor(bias[:], par[:, :, BIAS_], par[:, :, MUP_], ALU.mult).then_inc(bias_done, 1)
            dve.wait_ge(bias_done, 1)
            dve.tensor_tensor(bias[:, NC4:NBC], bias[:, NC4:NBC], par[:, NC4, EXTRA_:EXTRA_ + 1], ALU.add).then_inc(bias_done, 1)
            dve.tensor_scalar(a_log[:], a_log[:], MOST_LOG_A, None, ALU.min).then_inc(bias_done, 1)
            dve.wait_ge(const_in, 64)
            dve.tensor_copy(keep.below[:], keep.below_raw[:]).then_inc(const_done, 1)

            chain = [0]

            def link(ins):
                chain[0] += 1
                ins.then_inc(soft, 1)
                dve.wait_ge(soft, chain[0])

            dve.wait_ge(u_out, 1)
            link(dve.scalar_tensor_tensor(e[:], u[:], -1.0, u[:], ALU.mult, ALU.max))
            dve.wait_ge(exp_done, 2)
            link(dve.tensor_scalar(w1[:], e[:], 1.0, None, ALU.add))
            for m in range(2 * NC4):
                dve.wait_ge(drained, m + 3)
                if m >= 2:
                    dve.wait_ge(silu_done, m - 1)
                convolve(dve, conv[:, m % 2], pad[:, m % 2], par[:, m % NC4, :], conv_done, TAPS * m)
            dve.wait_ge(exp_done, 3)

            def soften(n):
                if n == 0:
                    link(dve.tensor_scalar(rest[:], w1[:], 1.0, None, ALU.subtract))
                elif n == 1:
                    link(dve.tensor_tensor(rest[:], e[:], rest[:], ALU.subtract))
                elif n == 2:
                    link(dve.reciprocal(e[:], w1[:]))
                elif n == 3:
                    link(dve.tensor_tensor(rest[:], rest[:], e[:], ALU.mult))
                elif n == 4:
                    link(dve.tensor_tensor(rest[:], rest[:], lnw[:], ALU.add))
                elif n == 5:
                    link(dve.scalar_tensor_tensor(keep.dt[:], u[:], 0.0, rest[:], ALU.max, ALU.add))
                elif n == 6:
                    link(dve.scalar_tensor_tensor(da[:], keep.dt[:], 1.0 / SCALED_A, rate[:].unsqueeze(1).to_broadcast([T, HB, HEADS]),
                                                  ALU.mult, ALU.mult))
                elif n == 7:
                    link(dve.tensor_scalar(da[:], da[:], -LEAST_LOG / SCALED_A, -SCALED_A, ALU.min, ALU.mult))
                elif n == 8:
                    link(dve.tensor_copy(keep.da_hi[:], da[:]))
                elif n == 9:
                    link(dve.tensor_tensor(keep.da_lo[:], da[:], keep.da_hi[:].bitcast(F32), ALU.subtract))

            for n in range(HB // 2 * 4):
                b, r = n // 4 * 2, n % 4
                dve.wait_ge(cb_done, n + 1)
                for i in range(2):
                    ins = dve.tensor_tensor(keep.cb[:, b + i, r:NG:4, :], banks[r][0:T, 2 * i * T:2 * (i + 1) * T].rearrange("s (q t) -> s q t", q=2),
                                            tri[:].unsqueeze(1).to_broadcast([T, 2, T]), ALU.mult)
                ins.then_inc(cb_out, 1)
                soften(n)


def attn_main(nc, half, d, out_dram, keep):
    with ExitStack() as ctx:
        sb, ps, sem = opener(nc, ctx, f"am{half}")
        wi_raw = sb("wi_raw", [P, 4, KD * P])
        wi_hi = sb("wi_hi", [P, 4, KD * P], F32R)
        wi_lo = sb("wi_lo", [P, 4, KD * P], F32R)
        wo_raw = sb("wo_raw", [P, WOUT])
        wo_hi = sb("wo_hi", [P, WOUT], F32R)
        wo_lo = sb("wo_lo", [P, WOUT], F32R)
        par_raw = sb("par_raw", [P, 5, NPAR])
        par = sb("par", [P, 5, NPAR])
        bias = sb("bias", [P, 4])
        norm_w = sb("norm_w", [P, GJ])
        pad = sb("pad", [P, GJ, TGB, PADT])
        conv = sb("conv", [P, GJ, TGB, T])
        xs = sb("xs", [P, 2, GJ, TGT])
        zs = sb("zs", [P, 2, GJ, TGT])
        steps_hi = sb("steps_hi", [T, 2, NH, T], F32R)
        steps_lo = sb("steps_lo", [T, 2, NH, T], F32R)
        decay = sb("decay", [T, 2, NH, T])
        mix = sb("mix", [T, 2, NH, T])
        x_dt = sb("x_dt", [T, 2, NH, HP])
        x_skip = sb("x_skip", [T, 2, GC])
        y = sb("y", [T, 2, TGB, GC])
        square = sb("square", [T, GC])
        power = sb("power", [T, 2, TGB])
        log_ms = sb("log_ms", [T, 2, TGB])
        ms = sb("ms", [T, TGB])
        part = sb("part", [T, TGB])
        eps = sb("eps", [T, 1])
        rstd = sb("rstd", [T, 2, TGB])
        yt_hi = sb("yt_hi", [P, GJ, TGT], F32R)
        yt_lo = sb("yt_lo", [P, GJ, TGT], F32R)
        p_ps = [ps(f"p{i}", [P, 512]) for i in range(2)]
        xz_ps, seg_ps, y_ps, r_ps = ps("xz", [P, 512]), ps("seg", [P, 512]), ps("y", [P, 512]), ps("r", [P, 512])
        t_ps = [ps(f"t{j}", [P, 512]) for j in range(GJ)]

        wi_in = [sem(f"wi_in{c}") for c in range(4)]
        wi_hi_done = [sem(f"wi_hi_done{c}") for c in range(4)]
        wi_lo_done = [sem(f"wi_lo_done{c}") for c in range(4)]
        wo_in, wo_hi_done, wo_lo_done = sem("wo_in"), sem("wo_hi_done"), sem("wo_lo_done")
        par_in, par_done, norm_w_done = sem("par_in"), sem("par_done"), sem("norm_w_done")
        zeroed = sem("zeroed")
        proj_done = sem("proj_done")
        drained = sem("drained")
        conv_done = sem("conv_done")
        silu_done = sem("silu_done")
        xz_done = sem("xz_done")
        steps_done = sem("steps_done")
        seg_done, decay_done, mix_done = sem("seg_done"), sem("decay_done"), sem("mix_done")
        x_dt_done, x_skip_done = sem("x_dt_done"), sem("x_skip_done")
        y_done, y_skip_done, y_gated = sem("y_done"), sem("y_skip_done"), sem("y_gated")
        square_done, log_done, rstd_done = sem("square_done"), sem("log_done"), sem("rstd_done")
        newton = sem("newton")
        y_normed = sem("y_normed")
        yt_done, yt_hi_done, yt_lo_done = sem("yt_done"), sem("yt_hi_done"), sem("yt_lo_done")
        r_done, added = sem("r_done"), sem("added")
        stored = sem("stored")
        held_pool = sem("held_pool")

        def slots(eng, slot):
            for u in (-1, 0):
                slot(0, u, False)
            with eng.Fori(0, NG - 1) as g:
                for u in (1, 2):
                    slot(g, u, False)
            for u in (1, 2):
                slot(NG - 1, u, True)

        def parts(u, last):
            return u >= 0 and not (last and u == 2), not last, u >= 1

        def wait(eng, sem_, value):
            if not isinstance(value, int) or value > 0:
                eng.wait_ge(sem_, value)

        def next_split(u, b, last):
            if u % 2 == 0 and not last and b >= 1:
                return b - 1, u // 2 + 1
            if u % 2 == 1 and u > 0 and b == 0:
                return 3, (u + 1) // 2
            return None, 0

        block = ctx.enter_context(nc.Block())

        @block.sync
        def _(sp):
            def load(i, g):
                for c in range(4):
                    wait(sp, wi_lo_done[c], i)
                    sp.dma_start(wi_raw[:, c, :], d["w_mix"][bass.ds(g, 1), :, c * DM:(c + 1) * DM].rearrange("o p n -> p (o n)")).then_inc(wi_in[c], 16)
                if isinstance(i, int) and i == NG:
                    return
                wait(sp, par_done, 2 * i)
                sp.dma_start(par_raw[:], d["par_mix"][bass.ds(g, 1)].rearrange("o p r n -> p (o r) n")).then_inc(par_in, 16)
                wait(sp, wo_lo_done, i)
                sp.dma_start(wo_raw[:], d["w_mix"][bass.ds(g, 1), :, 4 * DM:].rearrange("o p n -> p (o n)")).then_inc(wo_in, 16)

            load(0, 0)
            with sp.Fori(1, NG) as g:
                load(g, g)
            load(NG, NG - 1)
            out_v = out_dram.rearrange("(b t) d -> t b d", t=T)[:, half * HB:(half + 1) * HB, :]
            for a in range(0, HB, TGB):
                sp.wait_ge(added, 1 + (NG - 1) * HB + a + TGB)
                sp.dma_start(out_v[:, a:a + TGB, :], keep.x[:, a:a + TGB, :]).then_inc(stored, 16)
            sp.wait_ge(stored, 32)

        @block.tensor
        def _(pe):
            def slot(g, u, last):
                scan, project, product = parts(u, last)
                G = 2 * g + u

                def output(b):
                    a = slice(b * T, (b + 1) * T)
                    pe.wait_ge(added, 4 * (G - 1) + b + 1)
                    for j in range(GJ):
                        w = slice(j * DM, (j + 1) * DM)
                        ins = matmul_split(pe, r_ps[0:T, :], yt_hi[:, j, a], yt_lo[:, j, a], wo_hi[:, w], wo_lo[:, w],
                                           j == 0, j == GJ - 1)
                    ins.then_inc(r_done, 1)

                def chunk(u, b, ks):
                    a = slice((u + 1) % 2 * TGT, ((u + 1) % 2 + 1) * TGT)
                    for k in ks:
                        w = slice(k * P, (k + 1) * P)
                        ins = matmul_split(pe, p_ps[b % 2][:, 0:TGT], wi_hi[:, b, w], wi_lo[:, b, w],
                                           keep.xt_hi[:, k, a], keep.xt_lo[:, k, a], k == 0, k == KD - 1)
                    return ins

                for b in range(TGB):
                    U = 4 * G + b
                    if scan:
                        pe.wait_ge(steps_done, 2 * U + 2)
                        wait(pe, decay_done, U)
                        pe.matmul(seg_ps[0:T, 0:NH * T], keep.below[:], steps_hi[:, b % 2].rearrange("s h t -> s (h t)"), start=True, stop=False)
                        pe.matmul(seg_ps[0:T, 0:NH * T], keep.below[:], steps_lo[:, b % 2].rearrange("s h t -> s (h t)"), start=False, stop=True).then_inc(seg_done, 1)
                    if project:
                        if (u + 1) % 2 == 0:
                            pe.wait_ge(wi_lo_done[b], g + (u + 1) // 2 + 1)
                        wait(pe, drained, 4 * (G + 1) + b - 1)
                        chunk(u, b, range(KD // 2))
                    if scan:
                        if b == 0:
                            pe.wait_ge(drained, 4 * (G + 1))
                            pe.wait_ge(silu_done, 2 * (G + 1))
                        wait(pe, y_gated, U)
                        wait(pe, x_skip_done, U)
                        for i, src in enumerate((xs, zs)):
                            for j in range(GJ):
                                o = (i * GJ + j) * P
                                ins = pe.transpose(xz_ps[0:T, o:o + P], src[:, u % 2, j, b * T:(b + 1) * T], keep.ident[:])
                        ins.then_inc(xz_done, 1)
                    if project:
                        chunk(u, b, range(KD // 2, KD)).then_inc(proj_done, 1)
                    if product and b == 1:
                        pe.wait_ge(y_normed, 4 * G)
                        pe.wait_ge(yt_lo_done, 2 * G)
                        for j in range(GJ):
                            for i in range(TGB):
                                ins = pe.transpose(t_ps[j][:, i * T:(i + 1) * T], y[:, (u - 1) % 2, i, j * P:(j + 1) * P], keep.ident[0:T, 0:T])
                            ins.then_inc(yt_done, 1)
                    if product and b == 2:
                        pe.wait_ge(yt_lo_done, 2 * G + 2)
                        pe.wait_ge(wo_lo_done, g + (u - 1) // 2 + 1)
                        output(0)
                    if product and b == 3:
                        output(2)
                    if scan:
                        pe.wait_ge(mix_done, U + 1)
                        pe.wait_ge(x_dt_done, U + 1)
                        wait(pe, y_skip_done, U)
                        for h in range(NH):
                            o = h * HP
                            ins = pe.matmul(y_ps[0:T, o:o + HP], mix[:, b % 2, h, :], x_dt[:, b % 2, h, :], start=True, stop=True)
                        ins.then_inc(y_done, 1)
                    if product and b >= 2:
                        output(2 * (b - 2) + 1)

            slots(pe, slot)

        @block.scalar
        def _(act):
            def split(c, i):
                act.wait_ge(wi_in[c], 16 * (i + 1))
                wait(act, proj_done, 8 * i - 4 + c + 1 if not (isinstance(i, int) and i == 0) else 0)
                act.activation(wi_hi[:, c, :], wi_raw[:, c, :], ACT.Copy).then_inc(wi_hi_done[c], 1)

            def slot(g, u, last):
                scan, project, product = parts(u, last)
                G = 2 * g + u
                Q = G + 1
                for b in range(TGB):
                    U = 4 * G + b
                    if scan:
                        act.wait_ge(seg_done, U + 1)
                        wait(act, mix_done, U - 1)
                        act.activation(decay[:, b % 2].rearrange("s h t -> s (h t)"), seg_ps[0:T, 0:NH * T], ACT.Exp).then_inc(decay_done, 1)
                    if project and b < GJ:
                        if b == 0:
                            act.wait_ge(par_done, 2 * (g + (u + 1) // 2) + 2)
                        act.wait_ge(proj_done, 4 * Q + b + 1)
                        wait(act, conv_done, 2 * TAPS * (Q - 1) + TAPS * (b + 1))
                        act.activation(pad[:, b, :, TAPS - 1:], p_ps[b % 2][:, 0:TGT].rearrange("p (b t) -> p b t", b=TGB),
                                       ACT.Identity, bias=bias[:, b:b + 1], scale=par[:, b, MUP_:MUP_ + 1]).then_inc(drained, 1)
                    if product and b == 1:
                        for j in range(GJ):
                            act.wait_ge(yt_done, 2 * (G - 1) + j + 1)
                            act.wait_ge(added, 4 * (G - 1) + 1)
                            act.wait_ge(norm_w_done, g + (u - 1) // 2 + 1)
                            act.activation(yt_hi[:, j, :], t_ps[j][:, 0:TGT], ACT.Copy, scale=norm_w[:, j:j + 1]).then_inc(yt_hi_done, 1)
                    if scan and b >= 1:
                        squares(g, u, b - 1)
                    if product and u == 1 and b == 0:
                        act.wait_ge(wo_in, 16 * (g + 1))
                        act.wait_ge(added, 4 * (G - 1) + 1)
                        act.activation(wo_hi[:], wo_raw[:], ACT.Copy).then_inc(wo_hi_done, 1)
                    c, i = next_split(u, b, last)
                    if c is not None:
                        split(c, g + i)
                if project:
                    wait(act, xz_done, 4 * (Q - 1))
                    for j in range(GJ):
                        act.wait_ge(proj_done, 4 * Q + GJ + j + 1)
                        act.activation(zs[:, (u + 1) % 2, j, :], p_ps[j % 2][:, 0:TGT], ACT.Silu,
                                       bias=bias[:, GJ + j:GJ + j + 1], scale=par[:, GJ + j, MUP_:MUP_ + 1]).then_inc(drained, 1)
                    for j in range(GJ):
                        act.wait_ge(conv_done, 2 * TAPS * Q + TAPS * (j + 1))
                        act.activation(xs[:, (u + 1) % 2, j, :], conv[:, j].rearrange("p b t -> p (b t)"), ACT.Silu).then_inc(silu_done, 1)
                if scan:
                    act.preload_act_table_set("natural_log_exp_and_others")
                    squares(g, u, TGB - 1)
                    act.wait_ge(square_done, 4 * G + 4)
                    act.activation(log_ms[:, u % 2, :], power[:, u % 2, :], ACT.Ln, bias=eps[:], scale=1.0 / GC).then_inc(log_done, 1)
                    act.wait_ge(log_done, G + 1)
                    act.activation(rstd[:, u % 2, :], log_ms[:, u % 2, :], ACT.Exp, scale=-0.5).then_inc(rstd_done, 1)

            def squares(g, u, b):
                U = 8 * g + 4 * u + b
                act.wait_ge(y_gated, U + 1)
                wait(act, square_done, U)
                act.activation(square[:], y[:, u % 2, b, :], ACT.Square, accum_out=power[:, u % 2, b:b + 1]).then_inc(square_done, 1)

            for c in range(4):
                split(c, 0)
            act.wait_ge(zeroed, 2)
            slots(act, slot)

        @block.gpsimd
        def _(pool):
            pool.memset(pad[:, :, :, 0:TAPS - 1], 0.0).then_inc(zeroed, 1)
            pool.memset(eps[:], LN_EPS).then_inc(zeroed, 1)

            def split(c, i):
                pool.wait_ge(wi_hi_done[c], i + 1)
                pool.tensor_tensor(wi_lo[:, c, :], wi_raw[:, c, :], wi_hi[:, c, :].bitcast(F32), ALU.subtract).then_inc(wi_lo_done[c], 1)

            def steps(g, tg, b, U):
                wait(pool, seg_done, U - 1)
                pool.sem_inc(held_pool, 1)
                for out, src in ((steps_hi, keep.da_hi), (steps_lo, keep.da_lo)):
                    pool.tensor_tensor(out[:, b % 2], src[:, tg * TGB + b, bass.ds(g * NH, NH)].bitcast(F32).unsqueeze(2).to_broadcast([T, NH, T]),
                                       keep.tri[:].unsqueeze(1).to_broadcast([T, NH, T]), ALU.mult).then_inc(steps_done, 1)

            def slot(g, u, last):
                scan, project, product = parts(u, last)
                if not scan:
                    return
                G = 2 * g + u
                for b in range(TGB):
                    U = 4 * G + b
                    if b + 1 < TGB:
                        steps(g + u // 2, u % 2, b + 1, U + 1)
                    elif not (last and u == 1):
                        steps(g + (u + 1) // 2, (u + 1) % 2, 0, U + 1)
                    if product and u == 1 and b == 1:
                        pool.wait_ge(wo_hi_done, g + 1)
                        pool.tensor_tensor(wo_lo[:], wo_raw[:], wo_hi[:].bitcast(F32), ALU.subtract).then_inc(wo_lo_done, 1)
                    if b >= 1:
                        c, i = next_split(u, b - 1, last)
                        if c is not None:
                            split(c, g + i)
                    pool.wait_ge(decay_done, U + 1)
                    wait(pool, y_done, U - 1)
                    pool.sem_inc(held_pool, 1)
                    pool.tensor_tensor(mix[:, b % 2], decay[:, b % 2],
                                       keep.cb[:, u % 2 * TGB + b, bass.ds(g + u // 2, 1), :].to_broadcast([T, NH, T]), ALU.mult).then_inc(mix_done, 1)
                c, i = next_split(u, TGB - 1, last)
                if c is not None:
                    split(c, g + i)

            for c in range(4):
                split(c, 0)
            steps(0, 0, 0, 0)
            slots(pool, slot)

        @block.vector
        def _(dve):
            dve.sem_inc(added, 1)
            dve.sem_inc(yt_lo_done, 2)

            def slot(g, u, last):
                scan, project, product = parts(u, last)
                G = 2 * g + u
                Q = G + 1
                if u % 2 == 1:
                    if product:
                        dve.tensor_copy(norm_w[:], par[:, 4, 0:GJ]).then_inc(norm_w_done, 1)
                    if project:
                        i = g + (u + 1) // 2
                        dve.wait_ge(par_in, 16 * (i + 1))
                        wait(dve, silu_done, 2 * Q)
                        wait(dve, norm_w_done, i)
                        dve.tensor_copy(par[:], par_raw[:]).then_inc(par_done, 1)
                        dve.wait_ge(par_done, 2 * i + 1)
                        dve.tensor_tensor(bias[:], par[:, 0:4, BIAS_], par[:, 0:4, MUP_], ALU.mult).then_inc(par_done, 1)
                for b in range(TGB):
                    U = 4 * G + b
                    if scan:
                        p = b % 2
                        heads = bass.ds((g + u // 2) * NH, NH)
                        dve.wait_ge(xz_done, U + 1)
                        wait(dve, y_done, U - 1)
                        x_tok = xz_ps[0:T, 0:GC].rearrange("t (h p) -> t h p", h=NH)
                        dve.tensor_tensor(x_dt[:, p], x_tok, keep.dt[:, u % 2 * TGB + b, heads].unsqueeze(2).to_broadcast([T, NH, HP]),
                                          ALU.mult).then_inc(x_dt_done, 1)
                        dve.tensor_tensor(x_skip[:, p, :].rearrange("t (h p) -> t h p", h=NH), x_tok,
                                          keep.skip[:, heads].unsqueeze(2).to_broadcast([T, NH, HP]), ALU.mult).then_inc(x_skip_done, 1)
                    if product and b >= 2:
                        add(G, u, 2 * (b - 2))
                    if project and 1 <= b <= GJ:
                        j = b - 1
                        dve.wait_ge(drained, 4 * Q + j + 1)
                        wait(dve, silu_done, 2 * (Q - 1) + j + 1)
                        convolve(dve, conv[:, j], pad[:, j], par[:, j, :], conv_done, 2 * TAPS * Q + TAPS * j, range(TAPS // 2))
                    if scan:
                        dve.wait_ge(y_done, U + 1)
                        dve.wait_ge(x_skip_done, U + 1)
                        dve.tensor_tensor(y[:, u % 2, b, :], y_ps[0:T, 0:GC], x_skip[:, p, :], ALU.add).then_inc(y_skip_done, 1)
                        dve.wait_ge(y_skip_done, U + 1)
                        dve.tensor_tensor(y[:, u % 2, b, :], y[:, u % 2, b, :], xz_ps[0:T, GC:2 * GC], ALU.mult).then_inc(y_gated, 1)
                    if product and b == 0:
                        v = (u - 1) % 2
                        dve.wait_ge(rstd_done, G)
                        dve.tensor_scalar(ms[:], power[:, v, :], 1.0 / GC, LN_EPS, ALU.mult, ALU.add).then_inc(newton, 1)
                        dve.wait_ge(newton, 4 * G - 3)
                        dve.tensor_tensor(part[:], ms[:], rstd[:, v, :], ALU.mult).then_inc(newton, 1)
                        dve.wait_ge(newton, 4 * G - 2)
                        dve.scalar_tensor_tensor(part[:], part[:], -0.5, rstd[:, v, :], ALU.mult, ALU.mult).then_inc(newton, 1)
                        dve.wait_ge(newton, 4 * G - 1)
                        dve.scalar_tensor_tensor(rstd[:, v, :], part[:], 1.5, rstd[:, v, :], ALU.add, ALU.mult).then_inc(newton, 1)
                        dve.wait_ge(newton, 4 * G)
                        for i in range(TGB):
                            dve.tensor_scalar(y[:, (u - 1) % 2, i, :], y[:, (u - 1) % 2, i, :], rstd[:, (u - 1) % 2, i:i + 1], None,
                                              ALU.mult).then_inc(y_normed, 1)
                    if product and b == 1:
                        for j in range(GJ):
                            dve.wait_ge(yt_hi_done, 2 * (G - 1) + j + 1)
                            dve.scalar_tensor_tensor(yt_lo[:, j, :], t_ps[j][:, 0:TGT], norm_w[:, j:j + 1], yt_hi[:, j, :].bitcast(F32),
                                                     ALU.mult, ALU.subtract).then_inc(yt_lo_done, 1)
                    if project and 1 <= b <= GJ:
                        convolve(dve, conv[:, b - 1], pad[:, b - 1], par[:, b - 1, :], conv_done, 2 * TAPS * Q + TAPS * (b - 1), range(TAPS // 2, TAPS))
                    if product and b >= 2:
                        add(G, u, 2 * (b - 2) + 1)

            def add(G, u, b):
                m = (u - 1) % 2 * TGB + b
                dve.wait_ge(r_done, 4 * (G - 1) + b + 1)
                dve.tensor_tensor(keep.x[:, m, :], r_ps[0:T, :], keep.x[:, m, :], ALU.add).then_inc(added, 1)

            slots(dve, slot)


def attn_phase(nc, x_dram, d, out_dram):
    for half in range(2):
        with ExitStack() as ctx:
            sb, ps, sem = opener(nc, ctx, f"ak{half}")
            keep = Kept(sb)
            attn_prepare(nc, half, x_dram, d, keep)
            attn_main(nc, half, d, out_dram, keep)


B = 16
T = 112
S = 375
SE = S + 1
DC = 256
KC = DC // P
SCH = 3
SL = S // SCH
HD = 128
NKV = 8
QH = 2
HB = B // 2
HT = HB * T
TGB = 4
TGT = TGB * T
WQ, WKV, WO = KD * QH * HD, 2 * KC * HD, QH * DM
PAIR = 2 * HB
NPAIR = NKV // 2
MASKED = 1e30


def xattn_half(nc, half, x_dram, ctx_dram, mask_dram, w_dram, ident_dram, out_dram):
    with ExitStack() as ctx:
        sb, ps, sem = opener(nc, ctx, f"xa{half}")
        x = sb("x", [T, HB, DM])
        xt_hi = sb("xt_hi", [P, KD, HT], F32R)
        xt_lo = sb("xt_lo", [P, KD, HT], F32R)
        c_raw = sb("c_raw", [P, 2, KC, SE])
        c_hi = sb("c_hi", [P, HB, KC, SE], F32R)
        c_lo = sb("c_lo", [P, HB, KC, SE], F32R)
        ident = sb("ident", [P, P])
        mask_raw = sb("mask_raw", [T, HB, S], mybir.dt.uint8)
        bias = sb("bias", [T, HB, S])
        valid = sb("valid", [T, HB])
        wq_raw = sb("wq_raw", [P, WQ])
        wkv_raw = sb("wkv_raw", [P, WKV])
        wo_raw = sb("wo_raw", [P, WO])
        wq_hi = sb("wq_hi", [P, WQ], F32R)
        wq_lo = sb("wq_lo", [P, WQ], F32R)
        wkv_hi = sb("wkv_hi", [P, 2, WKV], F32R)
        wkv_lo = sb("wkv_lo", [P, 2, WKV], F32R)
        wo_hi = sb("wo_hi", [P, WO], F32R)
        wo_lo = sb("wo_lo", [P, WO], F32R)
        q_hi = sb("q_hi", [P, 2, QH, TGT], F32R)
        q_lo = sb("q_lo", [P, 2, QH, TGT], F32R)
        k_hi = sb("k_hi", [P, 2, SE], F32R)
        k_lo = sb("k_lo", [P, 2, SE], F32R)
        v_hi = sb("v_hi", [SL, 2, SCH * HD], F32R)
        v_lo = sb("v_lo", [SL, 2, SCH * HD], F32R)
        prob = sb("prob", [T, 2, QH, S])
        least = sb("least", [T, 2, QH])
        total = sb("total", [T, 2, QH])
        recip = sb("recip", [T, 2, QH])
        pt_hi = sb("pt_hi", [SL, 2, SCH, QH, T], F32R)
        pt_lo = sb("pt_lo", [SL, 2, SCH, QH, T], F32R)
        o_hi = sb("o_hi", [P, 2, QH * T], F32R)
        o_lo = sb("o_lo", [P, 2, QH * T], F32R)

        k_ps = ps("k", [P, 512])
        v_ps = ps("v", [P, 512])
        s_ps = [ps(f"s{h}", [P, 512]) for h in range(QH)]
        t_ps = [ps(f"t{h}", [P, 512]) for h in range(QH)]
        o_ps = ps("o", [P, 512])
        r_ps = ps("r", [P, 512])

        ln = Norm(sb, sem, T, HB, x, xt_hi, xt_lo, ident, s_ps + t_ps, [(0, 2), (2, 5), (5, 8)])
        mask_in, bias_done = sem("mask_in"), sem("bias_done")
        c_in = [sem(f"c_in{i}") for i in range(2)]
        c_hi_done = sem("c_hi_done")
        c_lo_done = [sem(f"c_lo_done{i}") for i in range(2)]
        wq_in, wkv_in, wo_in = sem("wq_in"), sem("wkv_in"), sem("wo_in")
        wq_hi_done, wkv_hi_done, wo_hi_done = sem("wq_hi_done"), sem("wkv_hi_done"), sem("wo_hi_done")
        wq_lo_done, wkv_lo_done, wo_lo_done = sem("wq_lo_done"), sem("wkv_lo_done"), sem("wo_lo_done")
        q_done, q_hi_done, q_lo_done = sem("q_done"), sem("q_hi_done"), sem("q_lo_done")
        k_done, k_hi_done, k_lo_done = sem("k_done"), sem("k_hi_done"), sem("k_lo_done")
        v_done, v_hi_done, v_lo_done = sem("v_done"), sem("v_hi_done"), sem("v_lo_done")
        s_done, max_done, exp_done = sem("s_done"), sem("max_done"), sem("exp_done")
        recip_done, norm_done = sem("recip_done"), sem("norm_done")
        t_done, pt_hi_done, pt_lo_done = sem("t_done"), sem("pt_hi_done"), sem("pt_lo_done")
        o_done, o_hi_done, o_lo_done = sem("o_done"), sem("o_hi_done"), sem("o_lo_done")
        r_done = sem("r_done")
        added = sem("added")
        stored = sem("stored")
        held_dve, held_pool = sem("held_dve"), sem("held_pool")

        def slots(eng, slot, split_context=None):
            for u in (-2, -1, 0):
                slot(0, u, False)
                if split_context:
                    split_context(2 * u + 6)
            with eng.Fori(0, NPAIR - 1) as b:
                for u in range(1, PAIR + 1):
                    slot(b, u, False)
            for u in range(1, PAIR + 1):
                slot(NPAIR - 1, u, True)

        def parts(u, last):
            return (u >= 0 and not (last and u >= PAIR), u >= -1 and not (last and u + 1 >= PAIR),
                    u >= 1, not (last and u + 2 >= PAIR))

        def wait(eng, sem_, value):
            if not isinstance(value, int) or value > 0:
                eng.wait_ge(sem_, value)

        def splits(u, last):
            if u < 0 or (last and u >= HB + 1):
                return None, 0
            return {3: "q", 4: "kv", 0: "o" if u else None}.get(u % HB), (u - 1) // HB + 1

        block = ctx.enter_context(nc.Block())

        @block.sync
        def _(sp):
            norm_load(ln, sp, x_dram.rearrange("(b t) d -> t b d", t=T)[:, half * HB:(half + 1) * HB, :], ident_dram)

            def load_w(i):
                w = w_dram[bass.ds(i, 1)].rearrange("o p n -> p (o n)")
                wait(sp, wq_lo_done, i)
                sp.dma_start(wq_raw[:], w[:, 0:WQ]).then_inc(wq_in, 16)
                wait(sp, wkv_lo_done, i)
                sp.dma_start(wkv_raw[:], w[:, WQ:WQ + WKV]).then_inc(wkv_in, 16)
                wait(sp, wo_lo_done, i)
                sp.dma_start(wo_raw[:], w[:, WQ + WKV:]).then_inc(wo_in, 16)

            load_w(0)
            sp.dma_start(mask_raw[:], mask_dram[half:half + 1].to_broadcast([T, HB, S])).then_inc(mask_in, 16)
            for b in range(HB):
                if b >= 2:
                    sp.wait_ge(c_lo_done[b % 2], b // 2)
                sp.dma_start(c_raw[:, b % 2], ctx_dram[half * HB + b].rearrange("(k p) s -> p k s", p=P)).then_inc(c_in[b % 2], 16)
            with sp.Fori(1, NKV) as i:
                load_w(i)
            out_v = out_dram.rearrange("(b t) d -> t b d", t=T)[:, half * HB:(half + 1) * HB, :]
            for a in range(0, HB, 2):
                sp.wait_ge(added, 1 + (NKV - 1) * HB + a + 2)
                sp.dma_start(out_v[:, a:a + 2, :], x[:, a:a + 2, :]).then_inc(stored, 16)
            sp.wait_ge(stored, 16 * HB // 2)

        @block.tensor
        def _(pe):
            norm_tensor(ln, pe)
            pe.wait_ge(ln.lo_done, HB)

            def slot(b, u, last):
                turn, score, product, keys = parts(u, last)
                n = b * PAIR + u
                if turn:
                    for h in range(QH):
                        wait(pe, norm_done, 2 * n + h + 1)
                        wait(pe, pt_lo_done, 2 * n - 1 + h)
                        view = t_ps[h][0:SL, 0:SCH * T].rearrange("s (c t) -> s c t", c=SCH)
                        for c in range(SCH):
                            ins = pe.transpose(view[:, c, :], prob[:, u % 2, h, c * SL:(c + 1) * SL], ident[0:T, 0:T])
                        ins.then_inc(t_done, 1)
                if score:
                    w, g = u + 1, (u + 1) % PAIR // TGB
                    pe.wait_ge(k_lo_done, n + 2)
                    if w % TGB == 0:
                        pe.wait_ge(q_lo_done, b * (PAIR // TGB * QH) + w // TGB * QH + QH)
                    a = slice(w % TGB * T, (w % TGB + 1) * T)
                    for h in range(QH):
                        wait(pe, max_done, 2 * n + h + 1)
                        ins = matmul_split(pe, s_ps[h][0:T, 0:SE], q_hi[:, g % 2, h, a], q_lo[:, g % 2, h, a],
                                           k_hi[:, w % 2, :], k_lo[:, w % 2, :], True, True)
                        ins.then_inc(s_done, 1)
                if product:
                    m = u - 1
                    pe.wait_ge(o_lo_done, n)
                    if m % HB == 0:
                        pe.wait_ge(wo_lo_done, 2 * b + m // HB + 1)
                    pe.wait_ge(added, n)
                    for h in range(QH):
                        a, w = slice(h * T, (h + 1) * T), slice(h * DM, (h + 1) * DM)
                        ins = matmul_split(pe, r_ps[0:T, :], o_hi[:, m % 2, a], o_lo[:, m % 2, a],
                                           wo_hi[:, w], wo_lo[:, w], h == 0, h == QH - 1)
                    ins.then_inc(r_done, 1)
                if keys:
                    w, i = u + 2, (u + 2) // HB
                    wait(pe, k_lo_done, n + 2)
                    wait(pe, v_lo_done, n + 2)
                    if w % TGB == 0:
                        if w % HB == 0:
                            pe.wait_ge(wq_lo_done, 2 * b + i + 1)
                        for h, bank in enumerate((k_ps, v_ps)):
                            for k in range(KD):
                                c = slice((k * QH + h) * HD, (k * QH + h + 1) * HD)
                                a = slice(w // TGB % 2 * TGT, (w // TGB % 2 + 1) * TGT)
                                ins = matmul_split(pe, bank[:, 0:TGT], wq_hi[:, c], wq_lo[:, c],
                                                   xt_hi[:, k, a], xt_lo[:, k, a], k == 0, k == KD - 1)
                            ins.then_inc(q_done, 1)
                        pe.wait_ge(q_lo_done, b * (PAIR // TGB * QH) + w // TGB * QH + 1)
                    if w % HB == 0:
                        pe.wait_ge(wkv_lo_done, 2 * b + i + 1)
                    if w < HB:
                        pe.wait_ge(c_lo_done[w % 2], w // 2 + 1)
                    for k in range(KC):
                        c = slice(k * HD, (k + 1) * HD)
                        ins = matmul_split(pe, k_ps[:, 0:SE], wkv_hi[:, i % 2, c], wkv_lo[:, i % 2, c],
                                           c_hi[:, w % HB, k, :], c_lo[:, w % HB, k, :], k == 0, k == KC - 1)
                    ins.then_inc(k_done, 1)
                    if w % TGB == 0:
                        pe.wait_ge(q_lo_done, b * (PAIR // TGB * QH) + w // TGB * QH + QH)
                    for c in range(SCH):
                        for k in range(KC):
                            a, d = slice(c * SL, (c + 1) * SL), slice((KC + k) * HD, (KC + k + 1) * HD)
                            ins = matmul_split(pe, v_ps[0:SL, c * HD:(c + 1) * HD], c_hi[:, w % HB, k, a], c_lo[:, w % HB, k, a],
                                               wkv_hi[:, i % 2, d], wkv_lo[:, i % 2, d], k == 0, k == KC - 1)
                    ins.then_inc(v_done, 1)
                if turn:
                    pe.wait_ge(pt_lo_done, 2 * n + 2)
                    pe.wait_ge(v_lo_done, n + 1)
                    wait(pe, o_lo_done, n)
                    for c in range(SCH):
                        d = slice(c * HD, (c + 1) * HD)
                        ins = matmul_split(pe, o_ps[:, 0:QH * T], v_hi[:, u % 2, d], v_lo[:, u % 2, d],
                                           pt_hi[:, u % 2, c].rearrange("s h t -> s (h t)"),
                                           pt_lo[:, u % 2, c].rearrange("s h t -> s (h t)"), c == 0, c == SCH - 1)
                    ins.then_inc(o_done, 1)

            slots(pe, slot)

        @block.scalar
        def _(act):
            norm_scalar(ln, act)

            def split(kind, i, j):
                if kind == "q":
                    act.wait_ge(wq_in, 16 * (i + 1))
                    wait(act, q_done, i * (HB // TGB * QH))
                    act.activation(wq_hi[:], wq_raw[:], ACT.Copy).then_inc(wq_hi_done, 1)
                if kind == "kv":
                    act.wait_ge(wkv_in, 16 * (i + 1))
                    wait(act, v_done, i * HB - TGB)
                    act.activation(wkv_hi[:, j], wkv_raw[:], ACT.Copy).then_inc(wkv_hi_done, 1)
                if kind == "o":
                    act.wait_ge(wo_in, 16 * (i + 1))
                    wait(act, r_done, i * HB)
                    act.activation(wo_hi[:], wo_raw[:], ACT.Copy).then_inc(wo_hi_done, 1)

            def slot(b, u, last):
                turn, score, product, keys = parts(u, last)
                n = b * PAIR + u
                if turn:
                    for h in range(QH):
                        act.wait_ge(t_done, 2 * n + h + 1)
                        wait(act, o_done, n)
                        act.activation(pt_hi[:, u % 2, :, h, :], t_ps[h][0:SL, 0:SCH * T].rearrange("s (c t) -> s c t", c=SCH),
                                       ACT.Copy).then_inc(pt_hi_done, 1)
                if score:
                    w = (u + 1) % 2
                    for h in range(QH):
                        act.wait_ge(max_done, 2 * n + h + 3)
                        act.activation(prob[:, w, h, :], prob[:, w, h, :], ACT.Exp, bias=least[:, w, h:h + 1], scale=-1.0,
                                       accum_out=total[:, w, h:h + 1]).then_inc(exp_done, 1)
                kind, i = splits(u, last)
                if kind == "o":
                    split(kind, 2 * b + i, i % 2)
                if keys:
                    w = u + 2
                    wait(act, s_done, 2 * n + 2)
                    if w % TGB == 0:
                        for h, bank in enumerate((k_ps, v_ps)):
                            act.wait_ge(q_done, b * (PAIR // TGB * QH) + w // TGB * QH + h + 1)
                            act.activation(q_hi[:, w // TGB % 2, h, :], bank[:, 0:TGT], ACT.Copy).then_inc(q_hi_done, 1)
                    act.wait_ge(k_done, n + 3)
                    act.activation(k_hi[:, w % 2, :], k_ps[:, 0:SE], ACT.Copy).then_inc(k_hi_done, 1)
                if turn:
                    act.wait_ge(o_done, n + 1)
                    wait(act, r_done, n)
                    act.activation(o_hi[:, u % 2, :], o_ps[:, 0:QH * T], ACT.Copy).then_inc(o_hi_done, 1)
                if keys:
                    act.wait_ge(v_done, n + 3)
                    wait(act, o_done, n + 1)
                    act.activation(v_hi[:, w % 2, :], v_ps[0:SL, 0:SCH * HD], ACT.Copy).then_inc(v_hi_done, 1)
                if kind and kind != "o":
                    split(kind, 2 * b + i, i % 2)

            def split_context(first):
                for b in (first, first + 1):
                    act.wait_ge(c_in[b % 2], 16 * (b // 2 + 1))
                    act.activation(c_hi[:, b], c_raw[:, b % 2], ACT.Copy).then_inc(c_hi_done, 1)
                if first == 2:
                    split("o", 0, 0)

            split("kv", 0, 0)
            split_context(0)
            slots(act, slot, split_context)

        @block.gpsimd
        def _(pool):

            def split(kind, i, j):
                if kind == "q":
                    pool.wait_ge(wq_hi_done, i + 1)
                    pool.tensor_tensor(wq_lo[:], wq_raw[:], wq_hi[:].bitcast(F32), ALU.subtract).then_inc(wq_lo_done, 1)
                if kind == "kv":
                    pool.wait_ge(wkv_hi_done, i + 1)
                    pool.tensor_tensor(wkv_lo[:, j], wkv_raw[:], wkv_hi[:, j].bitcast(F32), ALU.subtract).then_inc(wkv_lo_done, 1)
                if kind == "o":
                    pool.wait_ge(wo_hi_done, i + 1)
                    pool.tensor_tensor(wo_lo[:], wo_raw[:], wo_hi[:].bitcast(F32), ALU.subtract).then_inc(wo_lo_done, 1)

            def slot(b, u, last):
                turn, score, product, keys = parts(u, last)
                n = b * PAIR + u
                if score:
                    w = (u + 1) % 2
                    pool.wait_ge(recip_done, n + 2)
                    pool.sem_inc(held_pool, 1)
                    for h in range(QH):
                        pool.tensor_scalar(prob[:, w, h, :], prob[:, w, h, :], recip[:, w, h:h + 1],
                                           valid[:, (u + 1) % HB:(u + 1) % HB + 1], ALU.mult, ALU.mult).then_inc(norm_done, 1)
                kind, i = splits(u, last)
                if kind:
                    split(kind, 2 * b + i, i % 2)

            def split_context(b):
                pool.wait_ge(c_hi_done, b + 1)
                pool.tensor_tensor(c_lo[:, b], c_raw[:, b % 2], c_hi[:, b].bitcast(F32), ALU.subtract).then_inc(c_lo_done[0], 1)
                if b == 2:
                    split("o", 0, 0)

            pool.wait_ge(wq_in, 16)
            pool.tensor_copy(wq_hi[:], wq_raw[:]).then_inc(wq_hi_done, 1)
            split("q", 0, 0)
            pool.wait_ge(mask_in, 16)
            pool.tensor_scalar(bias[:], mask_raw[:], MASKED, -MASKED, ALU.mult, ALU.add).then_inc(bias_done, 1)
            split("kv", 0, 0)
            split_context(0)
            slots(pool, slot, split_context)

        @block.vector
        def _(dve):
            dve.sem_inc(added, 1)
            norm_vector(ln, dve)
            dve.wait_ge(mask_in, 16)
            dve.tensor_reduce(valid[:], mask_raw[:], AX.X, ALU.max).then_inc(bias_done, 1)
            dve.wait_ge(bias_done, 2)

            def slot(b, u, last):
                turn, score, product, keys = parts(u, last)
                n = b * PAIR + u
                if turn:
                    for h in range(QH):
                        dve.wait_ge(pt_hi_done, 2 * n + h + 1)
                        dve.tensor_tensor(pt_lo[:, u % 2, :, h, :], t_ps[h][0:SL, 0:SCH * T].rearrange("s (c t) -> s c t", c=SCH),
                                          pt_hi[:, u % 2, :, h, :].bitcast(F32), ALU.subtract).then_inc(pt_lo_done, 1)
                if score:
                    w = (u + 1) % 2
                    for h in range(QH):
                        dve.wait_ge(s_done, 2 * n + h + 3)
                        wait(dve, t_done, 2 * n - 1 + h)
                        dve.sem_inc(held_dve, 1)
                        dve.tensor_tensor_reduce(prob[:, w, h, :], s_ps[h][0:T, 0:S], bias[:, (u + 1) % HB, :],
                                                 -(HD ** -0.5), 3e38, ALU.add, ALU.min,
                                                 least[:, w, h:h + 1]).then_inc(max_done, 1)
                if product:
                    m = (u - 1) % HB
                    dve.wait_ge(r_done, n)
                    dve.tensor_tensor(x[:, m, :], r_ps[0:T, :], x[:, m, :], ALU.add).then_inc(added, 1)
                if score:
                    dve.wait_ge(exp_done, 2 * n + 4)
                    wait(dve, norm_done, 2 * n)
                    dve.reciprocal(recip[:, w, :], total[:, w, :]).then_inc(recip_done, 1)
                if keys:
                    w = u + 2
                    if w % TGB == 0:
                        for h, bank in enumerate((k_ps, v_ps)):
                            dve.wait_ge(q_hi_done, b * (PAIR // TGB * QH) + w // TGB * QH + h + 1)
                            dve.tensor_tensor(q_lo[:, w // TGB % 2, h, :], bank[:, 0:TGT], q_hi[:, w // TGB % 2, h, :].bitcast(F32),
                                              ALU.subtract).then_inc(q_lo_done, 1)
                    dve.wait_ge(k_hi_done, n + 3)
                    dve.tensor_tensor(k_lo[:, w % 2, :], k_ps[:, 0:SE], k_hi[:, w % 2, :].bitcast(F32), ALU.subtract).then_inc(k_lo_done, 1)
                if turn:
                    dve.wait_ge(o_hi_done, n + 1)
                    dve.tensor_tensor(o_lo[:, u % 2, :], o_ps[:, 0:QH * T], o_hi[:, u % 2, :].bitcast(F32), ALU.subtract).then_inc(o_lo_done, 1)
                if keys:
                    dve.wait_ge(v_hi_done, n + 3)
                    dve.tensor_tensor(v_lo[:, w % 2, :], v_ps[0:SL, 0:SCH * HD], v_hi[:, w % 2, :].bitcast(F32),
                                      ALU.subtract).then_inc(v_lo_done, 1)

            def split_context(b):
                dve.wait_ge(c_hi_done, b + 2)
                dve.tensor_tensor(c_lo[:, b + 1], c_raw[:, (b + 1) % 2], c_hi[:, b + 1].bitcast(F32), ALU.subtract).then_inc(c_lo_done[1], 1)

            split_context(0)
            slots(dve, slot, split_context)


def xattn_phase(nc, x_dram, ctx_dram, mask_dram, w_dram, ident_dram, out_dram):
    for half in range(2):
        xattn_half(nc, half, x_dram, ctx_dram, mask_dram, w_dram, ident_dram, out_dram)

E_N = 8
I_N = 352
IS_N = 1408
FT = TOKENS // P
FCH = (E_N * I_N + IS_N) // P
BCH = 3
NBLK = FCH // BCH
GU = 2 * KD * P
WCH = GU + DM
PIECE = 32
NPIECE = FCH * P // PIECE
EPIECE = I_N // PIECE
TG = [(0, 2), (2, 4), (6, 4), (10, 4)]
STEPS = len(TG) * BCH


def ffn_phase(nc, x_dram, w_dram, router_dram, rank_dram, ident_dram, c_dram, cexp_dram, out_dram):
    with ExitStack() as ctx:
        sb, ps, sem = opener(nc, ctx, "ff")
        x = sb("x", [P, FT, DM])
        xt_hi = sb("xt_hi", [P, KD, TOKENS], F32R)
        xt_lo = sb("xt_lo", [P, KD, TOKENS], F32R)
        w_raw = sb("w_raw", [P, BCH, WCH])
        w_hi = sb("w_hi", [P, BCH, WCH], F32R)
        w_lo = sb("w_lo", [P, BCH, WCH], F32R)
        scale = sb("scale", [P, BCH, TOKENS])
        silu = sb("silu", [P, 2, 512])
        scaled = sb("scaled", [P, 2, 512])
        h = sb("h", [P, 2, 512])
        h_hi = sb("h_hi", [P, 2, 512], F32R)
        h_lo = sb("h_lo", [P, 2, 512], F32R)
        ident = sb("ident", [P, P])
        r_raw = sb("r_raw", [P, KD, E_N + 2])
        r_hi = sb("r_hi", [P, KD, E_N + 2], F32R)
        r_lo = sb("r_lo", [P, KD, E_N + 2], F32R)
        rank = sb("rank", [P, FT, E_N])
        logits = sb("logits", [P, FT, E_N + 2])
        prob = sb("prob", [P, FT, E_N])
        rest = sb("rest", [P, FT, E_N])
        key = sb("key", [P, FT, E_N])
        first = sb("first", [P, FT, E_N])
        stat = sb("stat", [P, 4, FT])
        comb = sb("comb", [P, FT, E_N + 1])
        comb_t = sb("comb_t", [E_N + 1, TOKENS])

        gate_ps = [ps(f"gate{i}", [P, 512]) for i in range(2)]
        up_ps = [ps(f"up{i}", [P, 512]) for i in range(2)]
        acc = [ps(f"acc{i}", [P, 512]) for i in range(4)]

        ln = Norm(sb, sem, P, FT, x, xt_hi, xt_lo, ident, acc, [(0, 2), (2, 6), (6, 10), (10, 14)])
        router_in = sem("router_in")
        r_split = sem("r_split")
        logits_ps = sem("logits_ps")
        routed = sem("routed")
        exp_done = sem("exp_done")
        comb_turned = sem("comb_turned")
        comb_out = sem("comb_out")
        c_stored = sem("c_stored")
        w_in = [sem(f"w_in{j}") for j in range(BCH)]
        scale_in = [sem(f"scale_in{j}") for j in range(BCH)]
        gu_hi = [sem(f"gu_hi{j}") for j in range(BCH)]
        gu_lo = [sem(f"gu_lo{j}") for j in range(BCH)]
        dn_hi = [sem(f"dn_hi{j}") for j in range(BCH)]
        dn_lo = [sem(f"dn_lo{j}") for j in range(BCH)]
        gu_done = sem("gu_done")
        silu_done = sem("silu_done")
        scaled_done = sem("scaled_done")
        h_done = sem("h_done")
        h_hi_done = sem("h_hi_done")
        h_lo_done = sem("h_lo_done")
        down_done = sem("down_done")
        acc_done = sem("acc_done")
        added = sem("added")
        stored = sem("stored")

        def n_tok(s):
            return TG[s // BCH][1] * P

        def tok(s):
            return TG[s // BCH][0] * P

        block = ctx.enter_context(nc.Block())

        @block.sync
        def _(sp):
            norm_load(ln, sp, x_dram.rearrange("(t p) d -> p t d", p=P), ident_dram)
            sp.dma_start(r_raw[:], router_dram).then_inc(router_in, 16)
            sp.dma_start(rank[:], rank_dram).then_inc(router_in, 16)
            for j in range(BCH):
                sp.dma_start(w_raw[:, j, :], w_dram[j]).then_inc(w_in[j], 16)
            sp.wait_ge(comb_out, 4)
            sp.dma_start(c_dram, comb_t[:]).then_inc(c_stored, 16)
            sp.wait_ge(c_stored, 16)
            sp.dma_start(cexp_dram[0:E_N * EPIECE, :].rearrange("(e r) t -> e r t", r=EPIECE),
                         c_dram[0:E_N, :].unsqueeze(1).to_broadcast([E_N, EPIECE, TOKENS])).then_inc(c_stored, 16)
            sp.dma_start(cexp_dram[E_N * EPIECE:NPIECE, :],
                         c_dram[E_N:E_N + 1, :].to_broadcast([NPIECE - E_N * EPIECE, TOKENS])).then_inc(c_stored, 16)
            sp.wait_ge(c_stored, 48)

            def load_scale(b, j):
                for r in range(P // PIECE):
                    q = (b * BCH + j) * (P // PIECE) + r
                    sp.dma_start(scale[r * PIECE:(r + 1) * PIECE, j, :],
                                 cexp_dram[bass.ds(q, 1), :].to_broadcast([PIECE, TOKENS])).then_inc(scale_in[j], 16)

            def load_weights(b, j):
                sp.wait_ge(gu_lo[j], b)
                sp.wait_ge(dn_lo[j], b)
                sp.dma_start(w_raw[:, j, :], w_dram[bass.ds(b * BCH + j, 1)].rearrange("o p n -> p (o n)")).then_inc(w_in[j], 16)

            for j in range(BCH):
                load_scale(0, j)
            for j in range(BCH):
                load_weights(1, j)
            with sp.Fori(1, NBLK - 1) as b:
                for j in range(BCH):
                    sp.wait_ge(scaled_done, (b - 1) * STEPS + STEPS - BCH + j + 3)
                    load_scale(b, j)
                    load_weights(b + 1, j)
            for j in range(BCH):
                sp.wait_ge(scaled_done, (NBLK - 2) * STEPS + STEPS - BCH + j + 3)
                load_scale(NBLK - 1, j)
            out_v = out_dram.rearrange("(t p) d -> p t d", p=P)
            for g, (t, n) in enumerate(TG):
                sp.wait_ge(added, NBLK * FT + t + n)
                sp.dma_start(out_v[:, t:t + n, :], x[:, t:t + n, :]).then_inc(stored, 16)
            sp.wait_ge(stored, 16 * len(TG))

        @block.tensor
        def _(pe):
            norm_tensor(ln, pe)
            pe.wait_ge(r_split, 2)
            pe.wait_ge(ln.lo_done, FT)
            for t in range(FT):
                for k in range(KD):
                    a = slice(t * P, (t + 1) * P)
                    ins = matmul_split(pe, gate_ps[0][:, t * (E_N + 2):(t + 1) * (E_N + 2)], xt_hi[:, k, a], xt_lo[:, k, a],
                                       r_hi[:, k, :], r_lo[:, k, :], k == 0, k == KD - 1)
            ins.then_inc(logits_ps, 1)
            pe.wait_ge(r_split, 5)
            for t in range(FT):
                ins = pe.transpose(acc[t // 4][0:E_N + 1, (t % 4) * P:(t % 4 + 1) * P], comb[:, t, :], ident[:])
                if t % 4 == 3 or t == FT - 1:
                    ins.then_inc(comb_turned, 1)
            pe.wait_ge(comb_out, 4)

            def gate_up(b, s, first=False):
                j, n, a = s % BCH, n_tok(s), tok(s)
                if s < BCH:
                    pe.wait_ge(gu_lo[j], b + 1)
                if not first:
                    pe.wait_ge(h_done, b * STEPS + s + 1)
                for bank, o in ((gate_ps[s % 2], 0), (up_ps[s % 2], KD * P)):
                    for k in range(KD):
                        w = slice(o + k * P, o + (k + 1) * P)
                        ins = matmul_split(pe, bank[:, 0:n], w_hi[:, j, w], w_lo[:, j, w],
                                           xt_hi[:, k, a:a + n], xt_lo[:, k, a:a + n], k == 0, k == KD - 1)
                ins.then_inc(gu_done, 1)

            def down(b, s):
                j, (t0, nt) = s % BCH, TG[s // BCH]
                if s < BCH:
                    pe.wait_ge(dn_lo[j], b + 1)
                pe.wait_ge(h_lo_done, b * STEPS + s + 1)
                for m in range(nt):
                    if j == 0:
                        g = s // BCH - 1
                        if g >= 0:
                            pe.wait_ge(added, (b + 1) * FT + TG[g][0] + min(m + 1, TG[g][1]))
                        else:
                            pe.wait_ge(added, b * FT + TG[-1][0] + m + 1)
                    a, w = slice(m * P, (m + 1) * P), slice(GU, WCH)
                    ins = matmul_split(pe, acc[m][:], h_hi[:, s % 2, a], h_lo[:, s % 2, a],
                                       w_hi[:, j, w], w_lo[:, j, w], j == 0, j == BCH - 1)
                    if j == BCH - 1:
                        ins.then_inc(acc_done, 1)
                if j < BCH - 1:
                    ins.then_inc(down_done, 1)

            def one_block(b, last):
                for s in range(1, STEPS):
                    gate_up(b, s)
                    down(b, s - 1)
                if not last:
                    gate_up(b + 1, 0)
                down(b, STEPS - 1)

            gate_up(0, 0, first=True)
            with pe.Fori(0, NBLK - 1) as b:
                one_block(b, False)
            one_block(NBLK - 1, True)

        @block.scalar
        def _(act):
            norm_scalar(ln, act)
            act.wait_ge(routed, 1)
            act.activation(prob[:], rest[:], ACT.Exp).then_inc(exp_done, 1)
            act.activation(comb[:, :, E_N], logits[:, :, E_N], ACT.Sigmoid).then_inc(exp_done, 1)

            def split_gu(b, j, first=False):
                act.wait_ge(w_in[j], 16 * (b + 1))
                if not first:
                    act.wait_ge(gu_done, b * STEPS - BCH + j + 1)
                act.activation(w_hi[:, j, 0:GU], w_raw[:, j, 0:GU], ACT.Copy).then_inc(gu_hi[j], 1)

            def split_dn(b, j, first=False):
                if not first and j < BCH - 1:
                    act.wait_ge(down_done, b * len(TG) * (BCH - 1) - (BCH - 1) + j + 1)
                elif not first:
                    act.wait_ge(acc_done, b * FT)
                act.activation(w_hi[:, j, GU:WCH], w_raw[:, j, GU:WCH], ACT.Copy).then_inc(dn_hi[j], 1)

            def step(b, s, first=False):
                n = n_tok(s)
                act.wait_ge(gu_done, b * STEPS + s + 1)
                if not first:
                    act.wait_ge(scaled_done, b * STEPS + s + 1)
                act.activation(silu[:, s % 2, 0:n], gate_ps[s % 2][:, 0:n], ACT.Silu).then_inc(silu_done, 1)
                act.wait_ge(h_done, b * STEPS + s + 3)
                act.activation(h_hi[:, s % 2, 0:n], h[:, s % 2, 0:n], ACT.Copy).then_inc(h_hi_done, 1)

            def one_block(b, last):
                for s in range(1, STEPS + 1):
                    if s < STEPS:
                        step(b, s)
                    elif not last:
                        step(b + 1, 0)
                    if s >= STEPS - BCH and s < STEPS and not last:
                        split_gu(b + 1, s - (STEPS - BCH))
                    if s > STEPS - BCH and not last:
                        split_dn(b + 1, s - (STEPS - BCH) - 1)

            for j in range(BCH):
                split_gu(0, j, first=True)
                split_dn(0, j, first=True)
            step(0, 0, first=True)
            with act.Fori(0, NBLK - 1) as b:
                one_block(b, False)
            one_block(NBLK - 1, True)

        @block.gpsimd
        def _(pool):
            def split_gu(b, j):
                pool.wait_ge(gu_hi[j], b + 1)
                pool.tensor_tensor(w_lo[:, j, 0:GU], w_raw[:, j, 0:GU], w_hi[:, j, 0:GU].bitcast(F32),
                                   ALU.subtract).then_inc(gu_lo[j], 1)

            def split_dn(b, j):
                pool.wait_ge(dn_hi[j], b + 1)
                pool.tensor_tensor(w_lo[:, j, GU:WCH], w_raw[:, j, GU:WCH], w_hi[:, j, GU:WCH].bitcast(F32),
                                   ALU.subtract).then_inc(dn_lo[j], 1)

            def step(b, s, first=False):
                n, a, j = n_tok(s), tok(s), s % BCH
                if s < BCH:
                    pool.wait_ge(scale_in[j], 16 * (P // PIECE) * (b + 1))
                pool.wait_ge(silu_done, b * STEPS + s + 1)
                if not first:
                    pool.wait_ge(h_done, b * STEPS + s + 1)
                pool.tensor_tensor(scaled[:, s % 2, 0:n], silu[:, s % 2, 0:n], scale[:, j, a:a + n],
                                   ALU.mult).then_inc(scaled_done, 1)

            def one_block(b, last):
                for s in range(1, STEPS + 1):
                    if s < STEPS:
                        step(b, s)
                    elif not last:
                        step(b + 1, 0)
                    if s >= STEPS - BCH and s < STEPS and not last:
                        split_gu(b + 1, s - (STEPS - BCH))
                    if s > STEPS - BCH and not last:
                        split_dn(b + 1, s - (STEPS - BCH) - 1)

            for j in range(BCH):
                split_gu(0, j)
                split_dn(0, j)
            step(0, 0, first=True)
            with pool.Fori(0, NBLK - 1) as b:
                one_block(b, False)
            one_block(NBLK - 1, True)

        @block.vector
        def _(dve):
            dve.sem_inc(added, FT)
            dve.sem_inc(h_done, 2)
            dve.sem_inc(scaled_done, 2)
            norm_vector(ln, dve)
            dve.wait_ge(router_in, 32)
            dve.tensor_copy(r_hi[:], r_raw[:]).then_inc(r_split, 1)
            dve.wait_ge(r_split, 1)
            dve.tensor_tensor(r_lo[:], r_raw[:], r_hi[:].bitcast(F32), ALU.subtract).then_inc(r_split, 1)

            chain = [0]

            def link(ins):
                chain[0] += 1
                ins.then_inc(routed, 1)
                dve.wait_ge(routed, chain[0])

            def wide(a):
                return a.unsqueeze(2).to_broadcast([P, FT, E_N])

            top, total, top1, top2 = (stat[:, i, :] for i in range(4))
            dve.wait_ge(logits_ps, 1)
            dve.tensor_copy(logits[:], gate_ps[0][:, 0:FT * (E_N + 2)].rearrange("p (t e) -> p t e", e=E_N + 2)).then_inc(r_split, 1)
            dve.wait_ge(r_split, 3)
            dve.tensor_reduce(top, logits[:, :, 0:E_N], AX.X, ALU.max).then_inc(r_split, 1)
            dve.wait_ge(r_split, 4)
            link(dve.tensor_tensor(rest[:], logits[:, :, 0:E_N], wide(top), ALU.subtract))
            dve.wait_ge(exp_done, 2)
            link(dve.tensor_reduce(total, prob[:], AX.X, ALU.add))
            link(dve.reciprocal(total, total))
            link(dve.tensor_tensor(prob[:], prob[:], wide(total), ALU.mult))

            def choose(out, of, best):
                link(dve.tensor_reduce(best, of, AX.X, ALU.max))
                link(dve.tensor_tensor(key[:], of, wide(best), ALU.is_equal))
                link(dve.tensor_tensor(key[:], key[:], rank[:], ALU.mult))
                link(dve.tensor_reduce(top, key[:], AX.X, ALU.max))
                link(dve.tensor_tensor(out, key[:], wide(top), ALU.is_equal))

            choose(first[:], prob[:], top1)
            link(dve.scalar_tensor_tensor(rest[:], first[:], -2.0, prob[:], ALU.mult, ALU.add))
            choose(key[:], rest[:], top2)
            link(dve.tensor_tensor(first[:], first[:], key[:], ALU.add))
            link(dve.tensor_tensor(first[:], first[:], prob[:], ALU.mult))
            link(dve.tensor_tensor(total, top1, top2, ALU.add))
            link(dve.reciprocal(total, total))
            dve.tensor_tensor(comb[:, :, 0:E_N], first[:], wide(total), ALU.mult).then_inc(r_split, 1)
            for i in range(4):
                dve.wait_ge(comb_turned, i + 1)
                n = min(4, FT - 4 * i) * P
                dve.tensor_copy(comb_t[:, 512 * i:512 * i + n], acc[i][0:E_N + 1, 0:n]).then_inc(comb_out, 1)

            def step(b, s):
                n = n_tok(s)
                dve.wait_ge(scaled_done, b * STEPS + s + 3)
                dve.tensor_tensor(h[:, s % 2, 0:n], up_ps[s % 2][:, 0:n], scaled[:, s % 2, 0:n],
                                  ALU.mult).then_inc(h_done, 1)
                dve.wait_ge(h_hi_done, b * STEPS + s + 1)
                dve.tensor_tensor(h_lo[:, s % 2, 0:n], h[:, s % 2, 0:n], h_hi[:, s % 2, 0:n].bitcast(F32),
                                  ALU.subtract).then_inc(h_lo_done, 1)

            def one_block(b, last):
                for s in range(1, STEPS + 1):
                    if s < STEPS:
                        step(b, s)
                    elif not last:
                        step(b + 1, 0)
                    if s % BCH == 0:
                        t0, nt = TG[s // BCH - 1]
                        for m in range(nt):
                            dve.wait_ge(acc_done, b * FT + t0 + m + 1)
                            dve.tensor_tensor(x[:, t0 + m, :], acc[m][:], x[:, t0 + m, :], ALU.add).then_inc(added, 1)

            step(0, 0)
            with dve.Fori(0, NBLK - 1) as b:
                one_block(b, False)
            one_block(NBLK - 1, True)


def build(nc, d, out):
    x1 = nc.dram_tensor("x1", (TOKENS, DM), F32, kind="Internal").ap()
    attn_phase(nc, d["x"], d, x1)
    x2 = nc.dram_tensor("x2", (TOKENS, DM), F32, kind="Internal").ap()
    xattn_phase(nc, x1, d["ctx_t"], d["mask"], d["w_xattn"], d["ident"], x2)
    c = nc.dram_tensor("c_scratch", (E_N + 1, TOKENS), F32, kind="Internal").ap()
    cexp = nc.dram_tensor("c_spread", (NPIECE, TOKENS), F32, kind="Internal").ap()
    ffn_phase(nc, x2, d["w_ffn"], d["router"], d["rank"], d["ident"], c, cexp, out)



def kernel(x, ctx_1024, mask_BxS2_bf1, L0_attn_W_in, L0_attn_b_in, L0_attn_conv_w, L0_attn_conv_b, L0_attn_A_log,
           L0_attn_D_param, L0_attn_dt_bias, L0_attn_norm_w, L0_attn_W_out, L0_attn_b_out, L0_attn_mup_vector,
           L0_xattn_Wq, L0_xattn_Wk, L0_xattn_Wv, L0_xattn_Wo, L0_ffn_gate_w, L0_ffn_w_gate, L0_ffn_w_up,
           L0_ffn_w_down, L0_ffn_sw_gate, L0_ffn_sw_up, L0_ffn_sw_down, L0_ffn_shared_gate_w):
    import numpy as np
    import concourse.bacc as bacc
    from concourse import mybir
    from concourse.bass_utils import run_bass_kernel_spmd

    f = lambda a: np.ascontiguousarray(a)

    def feature_chunks(w, width=128):
        k, n = w.shape
        return w.reshape(k // 128, 128, n // width, width).transpose(2, 1, 0, 3)

    arrays = {
        "x": f(x).reshape(1792, 512),
        "ident": np.eye(128, dtype=np.float32),
    }
    gate = np.concatenate([f(L0_ffn_w_gate).transpose(1, 0, 2).reshape(512, 2816), f(L0_ffn_sw_gate)], 1)
    up = np.concatenate([f(L0_ffn_w_up).transpose(1, 0, 2).reshape(512, 2816), f(L0_ffn_sw_up)], 1)
    down = np.concatenate([f(L0_ffn_w_down).reshape(2816, 512), f(L0_ffn_sw_down)], 0)
    arrays["w_ffn"] = np.concatenate([feature_chunks(gate).reshape(33, 128, 512), feature_chunks(up).reshape(33, 128, 512),
                                      down.reshape(33, 128, 512)], 2)
    router = np.concatenate([f(L0_ffn_gate_w).T, f(L0_ffn_shared_gate_w), np.zeros((512, 1), np.float32)], 1)
    arrays["router"] = router.reshape(4, 128, 10).transpose(1, 0, 2)
    arrays["rank"] = np.broadcast_to(np.arange(8, 0, -1, dtype=np.float32), (128, 14, 8))
    ctx_t = f(ctx_1024).transpose(0, 2, 1)
    arrays["ctx_t"] = np.concatenate([ctx_t, np.zeros((16, 256, 1), np.float32)], 2)
    arrays["mask"] = f(mask_BxS2_bf1).view(np.uint8).reshape(2, 8, 375)
    wq = f(L0_xattn_Wq).reshape(4, 128, 8, 256).transpose(2, 1, 0, 3).reshape(8, 128, 1024)
    wk = f(L0_xattn_Wk).reshape(2, 128, 8, 128).transpose(2, 1, 0, 3).reshape(8, 128, 256)
    wv = f(L0_xattn_Wv).reshape(2, 128, 8, 128).transpose(2, 1, 0, 3).reshape(8, 128, 256)
    wo = f(L0_xattn_Wo).reshape(8, 2, 128, 512).transpose(0, 2, 1, 3).reshape(8, 128, 1024)
    arrays["w_xattn"] = np.concatenate([wq, wk, wv, wo], 2)
    w_in = f(L0_attn_W_in)
    xz = np.concatenate([w_in[:, 2048:4096], w_in[:, 0:2048]], 1)
    xz = feature_chunks(xz).reshape(2, 8, 2, 128, 512).transpose(1, 3, 0, 2, 4).reshape(8, 128, 2048)
    w_out = f(L0_attn_W_out).reshape(8, 2, 128, 512).transpose(0, 2, 1, 3).reshape(8, 128, 1024)
    arrays["w_mix"] = np.concatenate([xz, w_out], 2)
    bcdt = np.concatenate([w_in[:, 4096:4640], np.zeros((512, 96), np.float32)], 1)
    arrays["w_bcdt"] = bcdt.reshape(4, 128, 640).transpose(1, 0, 2)

    def channels(a, first, n):
        return f(a)[first:first + n]

    def params(first, n):
        p = np.zeros((n, 8), np.float32)
        p[:, 0], p[:, 1] = channels(L0_attn_b_in, first, n), channels(L0_attn_mup_vector, first, n)
        if first >= 2048:
            p[:, 2:6], p[:, 6] = channels(L0_attn_conv_w, first - 2048, n), channels(L0_attn_conv_b, first - 2048, n)
        return p

    par_x = params(2048, 2048).reshape(8, 2, 128, 8)
    par_z = params(0, 2048).reshape(8, 2, 128, 8)
    par_n = np.zeros((8, 1, 128, 8), np.float32)
    par_n[:, 0, :, 0:2] = f(L0_attn_norm_w).reshape(8, 2, 128).transpose(0, 2, 1)
    arrays["par_mix"] = np.concatenate([par_x, par_z, par_n], 1).transpose(0, 2, 1, 3)
    par_dt = np.zeros((128, 8), np.float32)
    par_dt[0:32, 0], par_dt[0:32, 1] = channels(L0_attn_b_in, 4608, 32), channels(L0_attn_mup_vector, 4608, 32)
    par_dt[0:32, 7] = f(L0_attn_dt_bias)
    arrays["par_bcdt"] = np.concatenate([params(4096, 512).reshape(4, 128, 8), par_dt.reshape(1, 128, 8)], 0).transpose(1, 0, 2)
    arrays["tri"] = np.triu(np.ones((112, 112), np.float32))
    arrays["below"] = np.tril(np.ones((112, 112), np.float32), -1)
    arrays["a_log"] = f(L0_attn_A_log).reshape(1, 32)
    arrays["skip"] = f(L0_attn_D_param).reshape(1, 32)
    arrays["b_out"] = f(L0_attn_b_out).reshape(1, 512)

    nc = bacc.Bacc("TRN2", target_bir_lowering=False, num_devices=1)
    arrays = {f"in_{k}_dram": f(a) for k, a in arrays.items()}
    given = {k: nc.dram_tensor(k, a.shape, mybir.dt.from_np(a.dtype), kind="ExternalInput").ap()
             for k, a in arrays.items()}
    out = nc.dram_tensor("out_0_dram", (1792, 512), mybir.dt.float32, kind="ExternalOutput").ap()
    build(nc, {k[3:-5]: a for k, a in given.items()}, out)
    r = run_bass_kernel_spmd(nc, [arrays], core_ids=[0])
    return r.results[0]["out_0_dram"].reshape(16, 112, 512)
```

```python
from contextlib import ExitStack

import concourse.bass as bass
from concourse import mybir

F32 = mybir.dt.float32
F32R = mybir.dt.float32r
ALU = mybir.AluOpType
ACT = mybir.ActivationFunctionType
AX = mybir.AxisListType

P = 128
DM = 512
KD = DM // P
LN_EPS = 1e-5
TOKENS = 16 * 112


def opener(nc, ctx, prefix):
    def sb(name, shape, dt=F32):
        return ctx.enter_context(nc.sbuf_tensor(f"{prefix}_{name}", shape, dt))

    def ps(name, shape):
        return ctx.enter_context(nc.psum_tensor(f"{prefix}_ps_{name}", shape, F32))

    used = []

    def sem(name):
        used.append(nc.alloc_semaphore(f"{prefix}_{name}"))
        return used[-1]

    def give_back():
        if used:
            nc.clear_and_free_semaphores(used)
            nc.all_engine_barrier()

    ctx.callback(give_back)

    return sb, ps, sem


def matmul_split(pe, out, w_hi, w_lo, x_hi, x_lo, start, stop):
    pe.matmul(out, w_hi, x_hi, start=start, stop=False)
    pe.matmul(out, w_hi, x_lo, start=False, stop=False)
    return pe.matmul(out, w_lo, x_hi, start=False, stop=stop)



class Norm:

    def __init__(self, sb, sem, rows, tiles, x, xt_hi, xt_lo, ident, banks, loads, xn=None):
        self.rows, self.tiles, self.x, self.xt_hi, self.xt_lo = rows, tiles, x, xt_hi, xt_lo
        self.ident, self.banks, self.loads = ident, banks, loads
        self.stats = sb("ln_stats", [rows, tiles, 6])
        self.mv = sb("ln_mv", [rows, tiles, 2])
        self.std = sb("ln_std", [rows, tiles])
        self.rstd = sb("ln_rstd", [rows, tiles])
        self.shift = sb("ln_shift", [rows, tiles])
        self.xn = sb("ln_xn", [rows, 2, DM]) if xn is None else xn
        self.x_in = [sem(f"ln_x_in{n}") for n in range(len(loads))]
        self.ident_in = sem("ln_ident_in")
        self.stats_done = sem("ln_stats_done")
        self.moments = sem("ln_moments")
        self.std_done = sem("ln_std_done")
        self.rstd_done = sem("ln_rstd_done")
        self.xn_done = sem("ln_xn_done")
        self.turned = sem("ln_turned")
        self.hi_done = sem("ln_hi_done")
        self.lo_done = sem("ln_lo_done")


def norm_load(s, eng, x_dram, ident_dram):
    eng.dma_start(s.ident[:], ident_dram).then_inc(s.ident_in, 16)
    for n, (a, b) in enumerate(s.loads):
        eng.dma_start(s.x[:, a:b, :], x_dram[:, a:b, :]).then_inc(s.x_in[n], 16)


def norm_vector(s, dve):

    def low(t):
        dve.wait_ge(s.hi_done, t + 1)
        cols = slice(t * s.rows, (t + 1) * s.rows)
        dve.tensor_tensor(s.xt_lo[:, :, cols], turned_view(s, s.banks[t % len(s.banks)]),
                          s.xt_hi[:, :, cols].bitcast(F32), ALU.subtract).then_inc(s.lo_done, 1)

    turned = 0
    for n, (a, b) in enumerate(s.loads):
        dve.wait_ge(s.x_in[n], 16)
        for t in range(a, b):
            dve.bn_stats(s.stats[:, t, :], s.x[:, t, :]).then_inc(s.stats_done, 1)
        for t in range(a, b):
            dve.wait_ge(s.stats_done, t + 1)
            dve.bn_aggr(s.mv[:, t, :], s.stats[:, t, :]).then_inc(s.moments, 1)
        dve.wait_ge(s.moments, b + n)
        dve.tensor_scalar(s.std[:, a:b], s.mv[:, a:b, 1], LN_EPS, None, ALU.add).then_inc(s.moments, 1)
        for t in range(turned, a - 1):
            low(t)
        turned = max(a - 1, 0)
        dve.wait_ge(s.std_done, n + 1)
        dve.reciprocal(s.rstd[:, a:b], s.std[:, a:b]).then_inc(s.rstd_done, 1)
        dve.wait_ge(s.rstd_done, 2 * n + 1)
        dve.scalar_tensor_tensor(s.shift[:, a:b], s.mv[:, a:b, 0], -1.0, s.rstd[:, a:b],
                                 ALU.mult, ALU.mult).then_inc(s.rstd_done, 1)
    for t in range(turned, s.tiles):
        low(t)


def turned_view(s, bank):
    return bank[:, 0:KD * s.rows].rearrange("p (k t) -> p k t", k=KD)


def norm_scalar(s, act):
    def high(t):
        act.wait_ge(s.turned, t + 1)
        act.activation(s.xt_hi[:, :, t * s.rows:(t + 1) * s.rows],
                       turned_view(s, s.banks[t % len(s.banks)]), ACT.Copy).then_inc(s.hi_done, 1)

    for n, (a, b) in enumerate(s.loads):
        act.wait_ge(s.moments, b + n + 1)
        act.activation(s.std[:, a:b], s.std[:, a:b], ACT.Sqrt).then_inc(s.std_done, 1)
        act.wait_ge(s.rstd_done, 2 * n + 2)
        for t in range(a, b):
            if t >= 2:
                act.wait_ge(s.turned, t - 1)
            act.activation(s.xn[:, t % 2, :], s.x[:, t, :], ACT.Identity, bias=s.shift[:, t:t + 1],
                           scale=s.rstd[:, t:t + 1]).then_inc(s.xn_done, 1)
            if t >= 1:
                high(t - 1)
    high(s.tiles - 1)


def norm_tensor(s, pe):
    pe.wait_ge(s.ident_in, 16)
    for t in range(s.tiles):
        pe.wait_ge(s.xn_done, t + 1)
        if t >= len(s.banks):
            pe.wait_ge(s.lo_done, t - len(s.banks) + 1)
        view = turned_view(s, s.banks[t % len(s.banks)])
        for k in range(KD):
            ins = pe.transpose(view[:, k, :], s.xn[:, t % 2, k * P:(k + 1) * P],
                               s.ident[0:s.rows, 0:s.rows])
        ins.then_inc(s.turned, 1)


B = 16
T = 112
HB = B // 2
HT = HB * T
TGB = 4
TGT = TGB * T
NG = 8
NH = 4
HP = 64
ST = 32
GC = NH * HP
GJ = GC // P
HEADS = NG * NH
TAPS = 4
PADT = T + TAPS - 1
WOUT = GJ * DM
NBC = 5
LEAST_LOG = -200.0
MOST_LOG_A = 88.0
SCALED_A = 1024.0
BIAS_, MUP_, TAP_, CONVB_, EXTRA_ = 0, 1, 2, 6, 7
NPAR = 8


def convolve(dve, out, padded, par, done, base, taps=range(TAPS)):
    for k in taps:
        if k == 0:
            dve.tensor_scalar(out, padded[:, :, 0:T], par[:, TAP_:TAP_ + 1], par[:, CONVB_:CONVB_ + 1],
                              ALU.mult, ALU.add).then_inc(done, 1)
            continue
        dve.wait_ge(done, base + k)
        dve.scalar_tensor_tensor(out, padded[:, :, k:k + T], par[:, TAP_ + k:TAP_ + k + 1], out,
                                 ALU.mult, ALU.add).then_inc(done, 1)


class Kept:

    def __init__(self, sb):
        self.x = sb("x", [T, HB, DM])
        self.wi_raw = sb("wi_raw", [P, 4, KD * P])
        self.wi_hi = sb("wi_hi", [P, 4, KD * P], F32R)
        self.wi_lo = sb("wi_lo", [P, 4, KD * P], F32R)
        self.xt_hi = sb("xt_hi", [P, KD, HT], F32R)
        self.xt_lo = sb("xt_lo", [P, KD, HT], F32R)
        self.ident = sb("ident", [P, P])
        self.below_raw = sb("below_raw", [T, T])
        self.below = sb("below", [T, T], F32R)
        self.tri = sb("tri", [T, T])
        self.skip = sb("skip", [T, HEADS])
        self.b_out = sb("b_out", [T, DM])
        self.cb = sb("cb", [T, HB, NG, T])
        self.dt = sb("dt", [T, HB, HEADS])
        self.da_hi = sb("da_hi", [T, HB, HEADS], F32R)
        self.da_lo = sb("da_lo", [T, HB, HEADS], F32R)


def attn_prepare(nc, half, x_dram, d, keep):
    with ExitStack() as ctx:
        sb, ps, sem = opener(nc, ctx, f"ap{half}")
        w_raw = sb("w_raw", [P, KD, NBC * P])
        w_hi = sb("w_hi", [P, KD, NBC * P], F32R)
        w_lo = sb("w_lo", [P, KD, NBC * P], F32R)
        par = sb("par", [P, NBC, NPAR])
        bias = sb("bias", [P, NBC])
        a_log = sb("a_log", [T, HEADS])
        rate = sb("rate", [T, HEADS])
        pad = sb("pad", [P, 2, TGB, PADT])
        conv = sb("conv", [P, 2, TGB, T])
        b_silu = sb("b_silu", [P, 2, HT])
        c_diag = sb("c_diag", [P, 2, HB, 4, T])
        tri = sb("tri", [T, T])
        u_heads = sb("u_heads", [HEADS, HT])
        u, e, w1, inverse, lnw, rest, da = (sb(n, [T, HB, HEADS]) for n in ("u", "e", "w1", "inverse", "lnw", "rest", "da"))
        banks = [ps(f"bank{i}", [P, 512]) for i in range(4)]
        proj = [ps(f"proj{i}", [P, 512]) for i in range(2)]
        ln = Norm(sb, sem, T, HB, keep.x, keep.xt_hi, keep.xt_lo, keep.ident, banks, [(0, 2), (2, 5), (5, 8)])
        w_in, w_hi_done, w_lo_done = sem("w_in"), sem("w_hi_done"), sem("w_lo_done")
        par_in, bias_done = sem("par_in"), sem("bias_done")
        const_in, const_done = sem("const_in"), sem("const_done")
        zeroed = sem("zeroed")
        proj_done, drained, conv_done, silu_done = sem("proj_done"), sem("drained"), sem("conv_done"), sem("silu_done")
        cb_done, cb_out = sem("cb_done"), sem("cb_out")
        soft, exp_done = sem("soft"), sem("exp_done")
        inverse_done, decay_step = sem("inverse_done"), sem("decay_step")
        u_turned, u_out = sem("u_turned"), sem("u_out")
        x_biased = sem("x_biased")
        wi_in, wi_hi_done, wi_lo_done = sem("wi_in"), sem("wi_hi_done"), sem("wi_lo_done")
        NC4 = NBC - 1
        products = [(g, NC4) for g in range(2)] + [(g, c) for g in range(2) for c in range(NC4)]
        block = ctx.enter_context(nc.Block())

        @block.sync
        def _(sp):
            norm_load(ln, sp, x_dram.rearrange("(b t) d -> t b d", t=T)[:, half * HB:(half + 1) * HB, :], d["ident"])
            sp.dma_start(par[:], d["par_bcdt"]).then_inc(par_in, 16)
            sp.dma_start(a_log[:], d["a_log"].to_broadcast([T, HEADS])).then_inc(par_in, 16)
            sp.dma_start(w_raw[:], d["w_bcdt"]).then_inc(w_in, 16)
            sp.dma_start(tri[:], d["tri"]).then_inc(const_in, 16)
            sp.dma_start(keep.below_raw[:], d["below"]).then_inc(const_in, 16)
            sp.dma_start(keep.skip[:], d["skip"].to_broadcast([T, HEADS])).then_inc(const_in, 16)
            sp.dma_start(keep.b_out[:], d["b_out"].to_broadcast([T, DM])).then_inc(const_in, 16)
            sp.dma_start(keep.wi_raw[:].rearrange("p c n -> p (c n)"), d["w_mix"][0, :, 0:4 * DM]).then_inc(wi_in, 16)

        @block.gpsimd
        def _(pool):
            pool.memset(pad[:, :, :, 0:TAPS - 1], 0.0).then_inc(zeroed, 1)
            pool.memset(c_diag[:, 0], 0.0).then_inc(zeroed, 1)
            pool.wait_ge(w_in, 16)
            for i, c in enumerate((NC4, 0, 1, 2, 3)):
                w = slice(c * P, (c + 1) * P)
                pool.tensor_copy(w_hi[:, :, w], w_raw[:, :, w]).then_inc(w_hi_done, 1)
                pool.wait_ge(w_hi_done, i + 1)
                pool.tensor_tensor(w_lo[:, :, w], w_raw[:, :, w], w_hi[:, :, w].bitcast(F32), ALU.subtract).then_inc(w_lo_done, 1)
            pool.wait_ge(const_in, 64)
            pool.tensor_copy(keep.tri[:], tri[:]).then_inc(const_done, 1)
            pool.memset(c_diag[:, 1], 0.0).then_inc(zeroed, 1)
            pool.wait_ge(ln.xn_done, HB)
            chain = [0]

            def link(ins):
                chain[0] += 1
                ins.then_inc(decay_step, 1)
                pool.wait_ge(decay_step, chain[0])

            pool.wait_ge(soft, 2)
            link(pool.tensor_scalar(rest[:], w1[:], 1.0, None, ALU.subtract))
            link(pool.tensor_tensor(rest[:], e[:], rest[:], ALU.subtract))
            pool.wait_ge(inverse_done, 1)
            link(pool.tensor_tensor(rest[:], rest[:], inverse[:], ALU.mult))
            pool.wait_ge(exp_done, 3)
            link(pool.tensor_tensor(rest[:], rest[:], lnw[:], ALU.add))
            link(pool.tensor_scalar(e[:], u[:], 0.0, None, ALU.max))
            link(pool.tensor_tensor(keep.dt[:], e[:], rest[:], ALU.add))
            link(pool.tensor_scalar(e[:], keep.dt[:], 1.0 / SCALED_A, None, ALU.mult))
            link(pool.tensor_tensor(da[:], e[:], rate[:].unsqueeze(1).to_broadcast([T, HB, HEADS]), ALU.mult))
            link(pool.tensor_scalar(da[:], da[:], -LEAST_LOG / SCALED_A, -SCALED_A, ALU.min, ALU.mult))
            link(pool.tensor_copy(keep.da_hi[:], da[:]))
            link(pool.tensor_tensor(keep.da_lo[:], da[:], keep.da_hi[:].bitcast(F32), ALU.subtract))
            for b in range(HB):
                pool.tensor_tensor(keep.x[:, b, :], keep.x[:, b, :], keep.b_out[:], ALU.add).then_inc(x_biased, 1)
            pool.wait_ge(wi_hi_done, 1)
            pool.tensor_tensor(keep.wi_lo[:], keep.wi_raw[:], keep.wi_hi[:].bitcast(F32), ALU.subtract).then_inc(wi_lo_done, 1)

        @block.tensor
        def _(pe):
            norm_tensor(ln, pe)
            pe.wait_ge(ln.lo_done, HB)
            for n, (g, c) in enumerate(products):
                if n < 2 or c != products[n - 1][1]:
                    pe.wait_ge(w_lo_done, min(n, NBC) if n else 1)
                if n >= 2:
                    pe.wait_ge(drained, n - 1)
                a = slice(g * TGT, (g + 1) * TGT)
                for k in range(KD):
                    w = slice(c * P, (c + 1) * P)
                    ins = matmul_split(pe, proj[n % 2][:, 0:TGT], w_hi[:, k, w], w_lo[:, k, w],
                                       keep.xt_hi[:, k, a], keep.xt_lo[:, k, a], k == 0, k == KD - 1)
                ins.then_inc(proj_done, 1)
                if n == 2:
                    pe.wait_ge(drained, 2)
                    for b in range(HB):
                        ins = pe.transpose(banks[0][0:T, b * HEADS:(b + 1) * HEADS], u_heads[:, b * T:(b + 1) * T], keep.ident[0:HEADS, 0:HEADS])
                    ins.then_inc(u_turned, 1)
            pe.wait_ge(u_out, 1)
            for b in range(HB):
                pe.wait_ge(silu_done, (b // TGB + 1) * NC4)
                for q in range(2):
                    n = 2 * b + q
                    if n >= 4:
                        pe.wait_ge(cb_out, n - 3)
                    pe.matmul(banks[n % 4][0:T, 0:4 * T], b_silu[:, q, b * T:(b + 1) * T],
                              c_diag[:, q, b].rearrange("p r t -> p (r t)"), start=True, stop=True).then_inc(cb_done, 1)

        def silu(act, m):
            g, c = m // NC4, m % NC4
            act.wait_ge(conv_done, TAPS * (m + 1))
            if c < 2:
                act.activation(b_silu[:, c, g * TGT:(g + 1) * TGT].rearrange("p (b t) -> p b t", b=TGB), conv[:, c % 2], ACT.Silu).then_inc(silu_done, 1)
                return
            act.wait_ge(zeroed, c)
            for r in range(4):
                rows = slice(r * ST, (r + 1) * ST)
                ins = act.activation(c_diag[rows, c - 2, g * TGB:(g + 1) * TGB, r, :], conv[rows, c % 2], ACT.Silu)
            ins.then_inc(silu_done, 1)

        @block.scalar
        def _(act):
            norm_scalar(ln, act)
            act.wait_ge(bias_done, 3)
            act.activation(rate[:], a_log[:], ACT.Exp).then_inc(exp_done, 1)
            act.wait_ge(wi_in, 16)
            act.activation(keep.wi_hi[:], keep.wi_raw[:], ACT.Copy).then_inc(wi_hi_done, 1)
            act.wait_ge(zeroed, 1)
            for n, (g, c) in enumerate(products):
                act.wait_ge(proj_done, n + 1)
                if c == NC4:
                    act.activation(u_heads[:, g * TGT:(g + 1) * TGT], proj[n % 2][0:HEADS, 0:TGT], ACT.Identity,
                                   bias=bias[0:HEADS, c:c + 1], scale=par[0:HEADS, c, MUP_:MUP_ + 1]).then_inc(drained, 1)
                    continue
                m = n - 2
                if m >= 2:
                    act.wait_ge(conv_done, TAPS * (m - 1))
                act.activation(pad[:, m % 2, :, TAPS - 1:], proj[n % 2][:, 0:TGT].rearrange("p (b t) -> p b t", b=TGB),
                               ACT.Identity, bias=bias[:, c:c + 1], scale=par[:, c, MUP_:MUP_ + 1]).then_inc(drained, 1)
                if m == 0:
                    act.wait_ge(u_turned, 1)
                    act.activation(u[:].rearrange("t b h -> t (b h)"), banks[0][0:T, 0:HB * HEADS], ACT.Copy).then_inc(u_out, 1)
                    act.wait_ge(soft, 1)
                    act.activation(e[:], e[:], ACT.Exp, scale=-1.0).then_inc(exp_done, 1)
                    act.wait_ge(soft, 2)
                    act.activation(lnw[:], w1[:], ACT.Ln).then_inc(exp_done, 1)
                else:
                    silu(act, m - 1)
            silu(act, 2 * NC4 - 1)

        @block.vector
        def _(dve):
            norm_vector(ln, dve)
            dve.wait_ge(par_in, 32)
            dve.tensor_tensor(bias[:], par[:, :, BIAS_], par[:, :, MUP_], ALU.mult).then_inc(bias_done, 1)
            dve.wait_ge(bias_done, 1)
            dve.tensor_tensor(bias[:, NC4:NBC], bias[:, NC4:NBC], par[:, NC4, EXTRA_:EXTRA_ + 1], ALU.add).then_inc(bias_done, 1)
            dve.tensor_scalar(a_log[:], a_log[:], MOST_LOG_A, None, ALU.min).then_inc(bias_done, 1)
            dve.wait_ge(const_in, 64)
            dve.tensor_copy(keep.below[:], keep.below_raw[:]).then_inc(const_done, 1)

            chain = [0]

            def link(ins):
                chain[0] += 1
                ins.then_inc(soft, 1)
                dve.wait_ge(soft, chain[0])

            dve.wait_ge(u_out, 1)
            link(dve.scalar_tensor_tensor(e[:], u[:], -1.0, u[:], ALU.mult, ALU.max))
            dve.wait_ge(exp_done, 2)
            link(dve.tensor_scalar(w1[:], e[:], 1.0, None, ALU.add))
            dve.reciprocal(inverse[:], w1[:]).then_inc(inverse_done, 1)
            for m in range(2 * NC4):
                dve.wait_ge(drained, m + 3)
                if m >= 2:
                    dve.wait_ge(silu_done, m - 1)
                convolve(dve, conv[:, m % 2], pad[:, m % 2], par[:, m % NC4, :], conv_done, TAPS * m)
            for n in range(2 * HB):
                b, q = n // 2, n % 2
                dve.wait_ge(cb_done, n + 1)
                dve.tensor_tensor(keep.cb[:, b, q * 4:(q + 1) * 4, :], banks[n % 4][0:T, 0:4 * T].rearrange("s (r t) -> s r t", r=4),
                                  tri[:].unsqueeze(1).to_broadcast([T, 4, T]), ALU.mult).then_inc(cb_out, 1)


def attn_main(nc, half, d, out_dram, keep):
    with ExitStack() as ctx:
        sb, ps, sem = opener(nc, ctx, f"am{half}")
        wi_raw, wi_hi, wi_lo = keep.wi_raw, keep.wi_hi, keep.wi_lo
        wo_raw = sb("wo_raw", [P, WOUT])
        wo_hi = sb("wo_hi", [P, WOUT], F32R)
        wo_lo = sb("wo_lo", [P, WOUT], F32R)
        par_raw = sb("par_raw", [P, 5, NPAR])
        par = sb("par", [P, 5, NPAR])
        bias = sb("bias", [P, 4])
        norm_w = sb("norm_w", [P, GJ])
        pad = sb("pad", [P, GJ, TGB, PADT])
        conv = sb("conv", [P, GJ, TGB, T])
        xs = sb("xs", [P, 2, GJ, TGT])
        zs = sb("zs", [P, 2, GJ, TGT])
        steps_hi = sb("steps_hi", [T, 2, NH, T], F32R)
        steps_lo = sb("steps_lo", [T, 2, NH, T], F32R)
        decay = sb("decay", [T, 2, NH, T])
        mix = sb("mix", [T, 2, NH, T])
        x_dt = sb("x_dt", [T, 2, NH, HP])
        x_skip = sb("x_skip", [T, 2, GC])
        y = sb("y", [T, 2, TGB, GC])
        square = sb("square", [T, GC])
        power = sb("power", [T, 2, TGB])
        log_ms = sb("log_ms", [T, 2, TGB])
        ms = sb("ms", [T, TGB])
        part = sb("part", [T, TGB])
        eps = sb("eps", [T, 1])
        rstd = sb("rstd", [T, 2, TGB])
        yt_hi = sb("yt_hi", [P, GJ, TGT], F32R)
        yt_lo = sb("yt_lo", [P, GJ, TGT], F32R)
        p_ps = [ps(f"p{i}", [P, 512]) for i in range(2)]
        xz_ps, seg_ps, y_ps, r_ps = ps("xz", [P, 512]), ps("seg", [P, 512]), ps("y", [P, 512]), ps("r", [P, 512])
        t_ps = [ps(f"t{j}", [P, 512]) for j in range(GJ)]

        wi_in = [sem(f"wi_in{c}") for c in range(4)]
        wi_hi_done = [sem(f"wi_hi_done{c}") for c in range(4)]
        wi_lo_done = [sem(f"wi_lo_done{c}") for c in range(4)]
        wo_in, wo_hi_done, wo_lo_done = sem("wo_in"), sem("wo_hi_done"), sem("wo_lo_done")
        par_in, par_done, norm_w_done = sem("par_in"), sem("par_done"), sem("norm_w_done")
        zeroed = sem("zeroed")
        proj_done = sem("proj_done")
        drained = sem("drained")
        conv_done = sem("conv_done")
        silu_done = sem("silu_done")
        xz_done = sem("xz_done")
        steps_done = sem("steps_done")
        seg_done, decay_done, mix_done = sem("seg_done"), sem("decay_done"), sem("mix_done")
        x_dt_done, x_skip_done = sem("x_dt_done"), sem("x_skip_done")
        y_done, y_skip_done, y_gated = sem("y_done"), sem("y_skip_done"), sem("y_gated")
        square_done, log_done, rstd_done = sem("square_done"), sem("log_done"), sem("rstd_done")
        newton = sem("newton")
        y_normed = sem("y_normed")
        yt_done, yt_hi_done, yt_lo_done = sem("yt_done"), sem("yt_hi_done"), sem("yt_lo_done")
        r_done, added = sem("r_done"), sem("added")
        stored = sem("stored")
        held_pool = sem("held_pool")

        def slots(eng, slot):
            for u in (-1, 0):
                slot(0, u, False)
            with eng.Fori(0, NG - 1) as g:
                for u in (1, 2):
                    slot(g, u, False)
            for u in (1, 2):
                slot(NG - 1, u, True)

        def r_bank(b):
            return r_ps if b % 2 == 0 else t_ps[0]

        def parts(u, last):
            return u >= 0 and not (last and u == 2), not last, u >= 1

        def wait(eng, sem_, value):
            if not isinstance(value, int) or value > 0:
                eng.wait_ge(sem_, value)

        def next_split(u, b, last):
            if u % 2 == 0 and not last and b >= 1:
                return b - 1, u // 2 + 1
            if u % 2 == 1 and u > 0 and b == 0:
                return 3, (u + 1) // 2
            return None, 0

        block = ctx.enter_context(nc.Block())

        @block.sync
        def _(sp):
            def load(i, g):
                for c in range(4):
                    if isinstance(i, int) and i == 0:
                        sp.sem_inc(wi_in[c], 16)
                        continue
                    wait(sp, wi_lo_done[c], i)
                    sp.dma_start(wi_raw[:, c, :], d["w_mix"][bass.ds(g, 1), :, c * DM:(c + 1) * DM].rearrange("o p n -> p (o n)")).then_inc(wi_in[c], 16)
                if isinstance(i, int) and i == NG:
                    return
                wait(sp, par_done, 2 * i)
                sp.dma_start(par_raw[:], d["par_mix"][bass.ds(g, 1)].rearrange("o p r n -> p (o r) n")).then_inc(par_in, 16)
                wait(sp, wo_lo_done, i)
                sp.dma_start(wo_raw[:], d["w_mix"][bass.ds(g, 1), :, 4 * DM:].rearrange("o p n -> p (o n)")).then_inc(wo_in, 16)

            load(0, 0)
            with sp.Fori(1, NG) as g:
                load(g, g)
            load(NG, NG - 1)
            out_v = out_dram.rearrange("(b t) d -> t b d", t=T)[:, half * HB:(half + 1) * HB, :]
            for a in range(0, HB, TGB):
                sp.wait_ge(added, 2 + (NG - 1) * HB + a + TGB)
                sp.dma_start(out_v[:, a:a + TGB, :], keep.x[:, a:a + TGB, :]).then_inc(stored, 16)
            sp.wait_ge(stored, 32)

        @block.tensor
        def _(pe):
            def slot(g, u, last):
                scan, project, product = parts(u, last)
                G = 2 * g + u

                def output(b):
                    a = slice(b * T, (b + 1) * T)
                    pe.wait_ge(added, 4 * (G - 1) + b + 1)
                    for j in range(GJ):
                        w = slice(j * DM, (j + 1) * DM)
                        ins = matmul_split(pe, r_bank(b)[0:T, :], yt_hi[:, j, a], yt_lo[:, j, a], wo_hi[:, w], wo_lo[:, w],
                                           j == 0, j == GJ - 1)
                    ins.then_inc(r_done, 1)

                def chunk(u, b, ks):
                    a = slice((u + 1) % 2 * TGT, ((u + 1) % 2 + 1) * TGT)
                    for k in ks:
                        w = slice(k * P, (k + 1) * P)
                        ins = matmul_split(pe, p_ps[b % 2][:, 0:TGT], wi_hi[:, b, w], wi_lo[:, b, w],
                                           keep.xt_hi[:, k, a], keep.xt_lo[:, k, a], k == 0, k == KD - 1)
                    return ins

                for b in range(TGB):
                    U = 4 * G + b
                    if scan:
                        pe.wait_ge(steps_done, 2 * U + 2)
                        wait(pe, decay_done, U)
                        pe.matmul(seg_ps[0:T, 0:NH * T], keep.below[:], steps_hi[:, b % 2].rearrange("s h t -> s (h t)"), start=True, stop=False)
                        pe.matmul(seg_ps[0:T, 0:NH * T], keep.below[:], steps_lo[:, b % 2].rearrange("s h t -> s (h t)"), start=False, stop=True).then_inc(seg_done, 1)
                    if project:
                        if (u + 1) % 2 == 0:
                            pe.wait_ge(wi_lo_done[b], g + (u + 1) // 2 + 1)
                        wait(pe, drained, 4 * (G + 1) + b - 1)
                        chunk(u, b, range(KD // 2))
                    if scan:
                        if b == 0:
                            pe.wait_ge(drained, 4 * (G + 1))
                            pe.wait_ge(silu_done, 2 * (G + 1))
                        wait(pe, y_gated, U)
                        wait(pe, x_skip_done, U)
                        for i, src in enumerate((xs, zs)):
                            for j in range(GJ):
                                o = (i * GJ + j) * P
                                ins = pe.transpose(xz_ps[0:T, o:o + P], src[:, u % 2, j, b * T:(b + 1) * T], keep.ident[:])
                        ins.then_inc(xz_done, 1)
                    if project:
                        chunk(u, b, range(KD // 2, KD)).then_inc(proj_done, 1)
                    if product and b == 1:
                        pe.wait_ge(y_normed, 4 * G)
                        pe.wait_ge(yt_lo_done, 2 * G)
                        pe.wait_ge(added, 4 * (G - 1) + 2)
                        for j in range(GJ):
                            for i in range(TGB):
                                ins = pe.transpose(t_ps[j][:, i * T:(i + 1) * T], y[:, (u - 1) % 2, i, j * P:(j + 1) * P], keep.ident[0:T, 0:T])
                            ins.then_inc(yt_done, 1)
                    if product and b == 2:
                        pe.wait_ge(yt_lo_done, 2 * G + 2)
                        pe.wait_ge(wo_lo_done, g + (u - 1) // 2 + 1)
                        output(0)
                    if product and b == 3:
                        output(2)
                    if scan:
                        pe.wait_ge(mix_done, U + 1)
                        pe.wait_ge(x_dt_done, U + 1)
                        wait(pe, y_skip_done, U)
                        for h in range(NH):
                            o = h * HP
                            ins = pe.matmul(y_ps[0:T, o:o + HP], mix[:, b % 2, h, :], x_dt[:, b % 2, h, :], start=True, stop=True)
                        ins.then_inc(y_done, 1)
                    if product and b >= 2:
                        output(2 * (b - 2) + 1)

            slots(pe, slot)

        @block.scalar
        def _(act):
            def split(c, i):
                act.wait_ge(wi_in[c], 16 * (i + 1))
                wait(act, proj_done, 8 * i - 4 + c + 1)
                act.activation(wi_hi[:, c, :], wi_raw[:, c, :], ACT.Copy).then_inc(wi_hi_done[c], 1)

            def slot(g, u, last):
                scan, project, product = parts(u, last)
                G = 2 * g + u
                Q = G + 1
                for b in range(TGB):
                    U = 4 * G + b
                    if scan:
                        act.wait_ge(seg_done, U + 1)
                        wait(act, mix_done, U - 1)
                        act.activation(decay[:, b % 2].rearrange("s h t -> s (h t)"), seg_ps[0:T, 0:NH * T], ACT.Exp).then_inc(decay_done, 1)
                    if project and b < GJ:
                        if b == 0:
                            act.wait_ge(par_done, 2 * (g + (u + 1) // 2) + 2)
                        act.wait_ge(proj_done, 4 * Q + b + 1)
                        wait(act, conv_done, 2 * TAPS * (Q - 1) + TAPS * (b + 1))
                        act.activation(pad[:, b, :, TAPS - 1:], p_ps[b % 2][:, 0:TGT].rearrange("p (b t) -> p b t", b=TGB),
                                       ACT.Identity, bias=bias[:, b:b + 1], scale=par[:, b, MUP_:MUP_ + 1]).then_inc(drained, 1)
                    if product and b == 1:
                        for j in range(GJ):
                            act.wait_ge(yt_done, 2 * (G - 1) + j + 1)
                            act.wait_ge(added, 4 * (G - 1) + 2)
                            act.wait_ge(norm_w_done, g + (u - 1) // 2 + 1)
                            act.activation(yt_hi[:, j, :], t_ps[j][:, 0:TGT], ACT.Copy, scale=norm_w[:, j:j + 1]).then_inc(yt_hi_done, 1)
                    if scan and b >= 1:
                        squares(g, u, b - 1)
                    if product and u == 1 and b == 0:
                        act.wait_ge(wo_in, 16 * (g + 1))
                        act.wait_ge(added, 4 * (G - 1) + 2)
                        act.activation(wo_hi[:], wo_raw[:], ACT.Copy).then_inc(wo_hi_done, 1)
                    c, i = next_split(u, b, last)
                    if c is not None:
                        split(c, g + i)
                if project:
                    wait(act, xz_done, 4 * (Q - 1))
                    for j in range(GJ):
                        act.wait_ge(proj_done, 4 * Q + GJ + j + 1)
                        act.activation(zs[:, (u + 1) % 2, j, :], p_ps[j % 2][:, 0:TGT], ACT.Silu,
                                       bias=bias[:, GJ + j:GJ + j + 1], scale=par[:, GJ + j, MUP_:MUP_ + 1]).then_inc(drained, 1)
                    for j in range(GJ):
                        act.wait_ge(conv_done, 2 * TAPS * Q + TAPS * (j + 1))
                        act.activation(xs[:, (u + 1) % 2, j, :], conv[:, j].rearrange("p b t -> p (b t)"), ACT.Silu).then_inc(silu_done, 1)
                if scan:
                    act.preload_act_table_set("natural_log_exp_and_others")
                    squares(g, u, TGB - 1)
                    act.wait_ge(square_done, 4 * G + 4)
                    act.activation(log_ms[:, u % 2, :], power[:, u % 2, :], ACT.Ln, bias=eps[:], scale=1.0 / GC).then_inc(log_done, 1)
                    act.wait_ge(log_done, G + 1)
                    act.activation(rstd[:, u % 2, :], log_ms[:, u % 2, :], ACT.Exp, scale=-0.5).then_inc(rstd_done, 1)

            def squares(g, u, b):
                U = 8 * g + 4 * u + b
                act.wait_ge(y_gated, U + 1)
                wait(act, square_done, U)
                act.activation(square[:], y[:, u % 2, b, :], ACT.Square, accum_out=power[:, u % 2, b:b + 1]).then_inc(square_done, 1)

            for c in range(4):
                act.sem_inc(wi_hi_done[c], 1)
            act.wait_ge(zeroed, 2)
            slots(act, slot)

        @block.gpsimd
        def _(pool):
            pool.memset(pad[:, :, :, 0:TAPS - 1], 0.0).then_inc(zeroed, 1)
            pool.memset(eps[:], LN_EPS).then_inc(zeroed, 1)

            def split(c, i):
                pool.wait_ge(wi_hi_done[c], i + 1)
                pool.tensor_tensor(wi_lo[:, c, :], wi_raw[:, c, :], wi_hi[:, c, :].bitcast(F32), ALU.subtract).then_inc(wi_lo_done[c], 1)

            def steps(g, tg, b, U):
                wait(pool, seg_done, U - 1)
                pool.sem_inc(held_pool, 1)
                for out, src in ((steps_hi, keep.da_hi), (steps_lo, keep.da_lo)):
                    pool.tensor_tensor(out[:, b % 2], src[:, tg * TGB + b, bass.ds(g * NH, NH)].bitcast(F32).unsqueeze(2).to_broadcast([T, NH, T]),
                                       keep.tri[:].unsqueeze(1).to_broadcast([T, NH, T]), ALU.mult).then_inc(steps_done, 1)

            def slot(g, u, last):
                scan, project, product = parts(u, last)
                if not scan:
                    return
                G = 2 * g + u
                for b in range(TGB):
                    U = 4 * G + b
                    if b + 1 < TGB:
                        steps(g + u // 2, u % 2, b + 1, U + 1)
                    elif not (last and u == 1):
                        steps(g + (u + 1) // 2, (u + 1) % 2, 0, U + 1)
                    if b >= 1:
                        c, i = next_split(u, b - 1, last)
                        if c is not None:
                            split(c, g + i)
                    pool.wait_ge(decay_done, U + 1)
                    wait(pool, y_done, U - 1)
                    pool.sem_inc(held_pool, 1)
                    pool.tensor_tensor(mix[:, b % 2], decay[:, b % 2],
                                       keep.cb[:, u % 2 * TGB + b, bass.ds(g + u // 2, 1), :].to_broadcast([T, NH, T]), ALU.mult).then_inc(mix_done, 1)
                c, i = next_split(u, TGB - 1, last)
                if c is not None:
                    split(c, g + i)

            for c in range(4):
                pool.sem_inc(wi_lo_done[c], 1)
            steps(0, 0, 0, 0)
            slots(pool, slot)

        @block.vector
        def _(dve):
            dve.sem_inc(added, 2)
            dve.sem_inc(yt_lo_done, 2)

            def slot(g, u, last):
                scan, project, product = parts(u, last)
                G = 2 * g + u
                Q = G + 1
                if u % 2 == 1:
                    if product:
                        dve.tensor_copy(norm_w[:], par[:, 4, 0:GJ]).then_inc(norm_w_done, 1)
                    if project:
                        i = g + (u + 1) // 2
                        dve.wait_ge(par_in, 16 * (i + 1))
                        wait(dve, silu_done, 2 * Q)
                        wait(dve, norm_w_done, i)
                        dve.tensor_copy(par[:], par_raw[:]).then_inc(par_done, 1)
                        dve.wait_ge(par_done, 2 * i + 1)
                        dve.tensor_tensor(bias[:], par[:, 0:4, BIAS_], par[:, 0:4, MUP_], ALU.mult).then_inc(par_done, 1)
                for b in range(TGB):
                    U = 4 * G + b
                    if scan:
                        p = b % 2
                        heads = bass.ds((g + u // 2) * NH, NH)
                        dve.wait_ge(xz_done, U + 1)
                        wait(dve, y_done, U - 1)
                        x_tok = xz_ps[0:T, 0:GC].rearrange("t (h p) -> t h p", h=NH)
                        dve.tensor_tensor(x_dt[:, p], x_tok, keep.dt[:, u % 2 * TGB + b, heads].unsqueeze(2).to_broadcast([T, NH, HP]),
                                          ALU.mult).then_inc(x_dt_done, 1)
                        dve.tensor_tensor(x_skip[:, p, :].rearrange("t (h p) -> t h p", h=NH), x_tok,
                                          keep.skip[:, heads].unsqueeze(2).to_broadcast([T, NH, HP]), ALU.mult).then_inc(x_skip_done, 1)
                    if product and b >= 2:
                        add(G, u, 2 * (b - 2))
                    if project and 1 <= b <= GJ:
                        j = b - 1
                        dve.wait_ge(drained, 4 * Q + j + 1)
                        wait(dve, silu_done, 2 * (Q - 1) + j + 1)
                        convolve(dve, conv[:, j], pad[:, j], par[:, j, :], conv_done, 2 * TAPS * Q + TAPS * j, range(TAPS // 2))
                    if product and u == 1 and b == 1:
                        dve.wait_ge(wo_hi_done, g + 1)
                        dve.tensor_tensor(wo_lo[:], wo_raw[:], wo_hi[:].bitcast(F32), ALU.subtract).then_inc(wo_lo_done, 1)
                    if scan:
                        dve.wait_ge(y_done, U + 1)
                        dve.wait_ge(x_skip_done, U + 1)
                        dve.tensor_tensor(y[:, u % 2, b, :], y_ps[0:T, 0:GC], x_skip[:, p, :], ALU.add).then_inc(y_skip_done, 1)
                        dve.wait_ge(y_skip_done, U + 1)
                        dve.tensor_tensor(y[:, u % 2, b, :], y[:, u % 2, b, :], xz_ps[0:T, GC:2 * GC], ALU.mult).then_inc(y_gated, 1)
                    if product and b == 0:
                        v = (u - 1) % 2
                        dve.wait_ge(rstd_done, G)
                        dve.tensor_scalar(ms[:], power[:, v, :], 1.0 / GC, LN_EPS, ALU.mult, ALU.add).then_inc(newton, 1)
                        dve.wait_ge(newton, 4 * G - 3)
                        dve.tensor_tensor(part[:], ms[:], rstd[:, v, :], ALU.mult).then_inc(newton, 1)
                        dve.wait_ge(newton, 4 * G - 2)
                        dve.scalar_tensor_tensor(part[:], part[:], -0.5, rstd[:, v, :], ALU.mult, ALU.mult).then_inc(newton, 1)
                        dve.wait_ge(newton, 4 * G - 1)
                        dve.scalar_tensor_tensor(rstd[:, v, :], part[:], 1.5, rstd[:, v, :], ALU.add, ALU.mult).then_inc(newton, 1)
                        dve.wait_ge(newton, 4 * G)
                        for i in range(TGB):
                            dve.tensor_scalar(y[:, (u - 1) % 2, i, :], y[:, (u - 1) % 2, i, :], rstd[:, (u - 1) % 2, i:i + 1], None,
                                              ALU.mult).then_inc(y_normed, 1)
                    if product and b == 1:
                        for j in range(GJ):
                            dve.wait_ge(yt_hi_done, 2 * (G - 1) + j + 1)
                            dve.scalar_tensor_tensor(yt_lo[:, j, :], t_ps[j][:, 0:TGT], norm_w[:, j:j + 1], yt_hi[:, j, :].bitcast(F32),
                                                     ALU.mult, ALU.subtract).then_inc(yt_lo_done, 1)
                    if project and 1 <= b <= GJ:
                        convolve(dve, conv[:, b - 1], pad[:, b - 1], par[:, b - 1, :], conv_done, 2 * TAPS * Q + TAPS * (b - 1), range(TAPS // 2, TAPS))
                    if product and b >= 2:
                        add(G, u, 2 * (b - 2) + 1)

            def add(G, u, b):
                m = (u - 1) % 2 * TGB + b
                dve.wait_ge(r_done, 4 * (G - 1) + b + 1)
                dve.tensor_tensor(keep.x[:, m, :], r_bank(b)[0:T, :], keep.x[:, m, :], ALU.add).then_inc(added, 1)

            slots(dve, slot)


def attn_phase(nc, x_dram, d, out_dram):
    for half in range(2):
        with ExitStack() as ctx:
            sb, ps, sem = opener(nc, ctx, f"ak{half}")
            keep = Kept(sb)
            attn_prepare(nc, half, x_dram, d, keep)
            attn_main(nc, half, d, out_dram, keep)


B = 16
T = 112
S = 375
SE = S + 1
DC = 256
KC = DC // P
SCH = 3
SL = S // SCH
HD = 128
NKV = 8
QH = 2
HB = B // 2
HT = HB * T
TGB = 4
TGT = TGB * T
HEAD2 = 2
WQ, WK, WO = KD * QH * HD, KC * HD, QH * DM
WV = KC * HEAD2 * HD
WKV = HEAD2 * WK + WV
PAIR = HEAD2 * HB
NPAIR = NKV // 2
MASKED = 1e30


def xattn_half(nc, half, x_dram, ctx_dram, mask_dram, w_dram, ident_dram, out_dram):
    with ExitStack() as ctx:
        sb, ps, sem = opener(nc, ctx, f"xa{half}")
        x = sb("x", [T, HB, DM])
        xt_hi = sb("xt_hi", [P, KD, HT], F32R)
        xt_lo = sb("xt_lo", [P, KD, HT], F32R)
        shared = sb("shared", [P, WO + WKV])
        c_raw = shared[:, 0:2 * KC * SE].rearrange("p (i k s) -> p i k s", i=2, k=KC)
        wo0_raw, wkv_raw = shared[:, 0:WO], shared[:, WO:WO + WKV]
        c_hi = sb("c_hi", [P, HB, KC, SE], F32R)
        c_lo = sb("c_lo", [P, HB, KC, SE], F32R)
        ident = sb("ident", [P, P])
        o_hi = sb("o_hi", [P, 2, QH * T], F32R)
        o_lo = sb("o_lo", [P, 2, QH * T], F32R)
        bias_all = sb("bias", [T, HB * S])
        bias = bias_all[:].rearrange("t (b s) -> t b s", b=HB)
        valid = sb("valid", [T, HB])
        w_raw = sb("w_raw", [P, WQ])
        wq_hi = sb("wq_hi", [P, HEAD2, WQ], F32R)
        wq_lo = sb("wq_lo", [P, HEAD2, WQ], F32R)
        wk_hi = sb("wk_hi", [P, HEAD2, WK], F32R)
        wk_lo = sb("wk_lo", [P, HEAD2, WK], F32R)
        wv_hi = sb("wv_hi", [P, WV], F32R)
        wv_lo = sb("wv_lo", [P, WV], F32R)
        wo_hi = sb("wo_hi", [P, HEAD2, WO], F32R)
        wo_lo = sb("wo_lo", [P, HEAD2, WO], F32R)
        q_hi = sb("q_hi", [P, 2, QH, TGT], F32R)
        q_lo = sb("q_lo", [P, 2, QH, TGT], F32R)
        k_hi = sb("k_hi", [P, 2, SE], F32R)
        k_lo = sb("k_lo", [P, 2, SE], F32R)
        v_hi = sb("v_hi", [SL, 2, SCH * HEAD2 * HD], F32R)
        v_lo = sb("v_lo", [SL, 2, SCH * HEAD2 * HD], F32R)
        prob_all = sb("prob", [T, 2 * QH * S])
        prob = prob_all[:].rearrange("t (i h s) -> t i h s", i=2, h=QH)
        mask_raw = prob_all[:].bitcast(mybir.dt.uint8)[:, 0:HB * S].rearrange("t (b s) -> t b s", b=HB)
        least = sb("least", [T, 2, QH])
        total = sb("total", [T, 2, QH])
        recip = sb("recip", [T, 2, QH])
        pt_hi = sb("pt_hi", [SL, 2, SCH, QH, T], F32R)
        pt_lo = sb("pt_lo", [SL, 2, SCH, QH, T], F32R)

        k_ps = ps("k", [P, 512])
        v_ps = ps("v", [P, 512])
        s_ps = [ps(f"s{h}", [P, 512]) for h in range(QH)]
        t_ps = [ps(f"t{h}", [P, 512]) for h in range(QH)]
        o_ps = ps("o", [P, 512])
        r_ps = ps("r", [P, 512])

        xn = bias_all[:, 0:2 * DM].rearrange("t (i d) -> t i d", i=2)
        ln = Norm(sb, sem, T, HB, x, xt_hi, xt_lo, ident, s_ps + t_ps, [(0, 2), (2, 5), (5, 8)], xn)
        mask_in, bias_done = sem("mask_in"), sem("bias_done")
        c_in = [sem(f"c_in{i}") for i in range(2)]
        c_hi_done = sem("c_hi_done")
        c_lo_done = [sem(f"c_lo_done{i}") for i in range(2)]
        w_in = sem("w_in")
        wkv_in, wo0_in = sem("wkv_in"), sem("wo0_in")
        wq_hi_done, wq_lo_done = sem("wq_hi_done"), sem("wq_lo_done")
        wk_hi_done, wk_lo_done = sem("wk_hi_done"), sem("wk_lo_done")
        wv_hi_done, wv_lo_done = sem("wv_hi_done"), sem("wv_lo_done")
        wo_hi_done, wo_lo_done = sem("wo_hi_done"), sem("wo_lo_done")
        q_done, q_hi_done, q_lo_done = sem("q_done"), sem("q_hi_done"), sem("q_lo_done")
        k_done, k_hi_done, k_lo_done = sem("k_done"), sem("k_hi_done"), sem("k_lo_done")
        v_done, v_hi_done, v_lo_done = sem("v_done"), sem("v_hi_done"), sem("v_lo_done")
        s_done, max_done, exp_done = sem("s_done"), sem("max_done"), sem("exp_done")
        recip_done, norm_done = sem("recip_done"), sem("norm_done")
        t_done, pt_hi_done, pt_lo_done = sem("t_done"), sem("pt_hi_done"), sem("pt_lo_done")
        o_done, o_hi_done, o_lo_done = sem("o_done"), sem("o_hi_done"), sem("o_lo_done")
        r_done = sem("r_done")
        added = sem("added")
        stored = sem("stored")
        held_dve, held_pool, held_sp = sem("held_dve"), sem("held_pool"), sem("held_sp")

        def slots(eng, slot, split_context=None):
            for u in (-2, -1, 0):
                slot(0, u, False)
                if split_context:
                    split_context(2 * u + 6)
            with eng.Fori(0, NPAIR - 1) as b:
                for u in range(1, PAIR + 1):
                    slot(b, u, False)
            for u in range(1, PAIR + 1):
                slot(NPAIR - 1, u, True)

        def parts(u, last):
            return (u >= 0 and not (last and u >= PAIR), u >= -1 and not (last and u + 1 >= PAIR),
                    u >= 1, not (last and u + 2 >= PAIR))

        def wait(eng, sem_, value):
            if not isinstance(value, int) or value > 0:
                eng.wait_ge(sem_, value)

        def splits(u, last):
            if last or u <= 0:
                return None, 0
            return {8: ("q", 0), 10: ("q", 1), 14: ("k", 1), 15: ("o", 0), 16: ("o", 1)}.get(u, (None, 0))

        def late_splits(u, last):
            if last or u <= 0:
                return None, 0
            return {12: ("k", 0), 13: ("v", 0)}.get(u, (None, 0))

        def v_chunks(i):
            return (0, 1) if i == 0 else (2,)

        def v_part(w):
            first = v_chunks(w % 2)[0] * HEAD2 * HD
            return w // 2 % 2, slice(first, first + len(v_chunks(w % 2)) * HEAD2 * HD), slice(0, len(v_chunks(w % 2)) * HEAD2 * HD)

        def q_products(w):
            return w // HB * 2 * QH + w % 2 * QH

        def raw(kind, i, first):
            kv = w_raw if first else wkv_raw
            return {"q": w_raw[:], "o": w_raw[:] if first or i == 1 else wo0_raw,
                    "k": kv[:, i * WK:(i + 1) * WK], "v": kv[:, HEAD2 * WK:WKV]}[kind]

        block = ctx.enter_context(nc.Block())

        @block.sync
        def _(sp):
            norm_load(ln, sp, x_dram.rearrange("(b t) d -> t b d", t=T)[:, half * HB:(half + 1) * HB, :], ident_dram)
            w_first = w_dram[0]
            Q0, Q1, O0, O1, KV = (slice(n * WQ, (n + 1) * WQ) for n in range(5))

            def load_context(b):
                if b >= 2:
                    sp.wait_ge(c_lo_done[b % 2], b // 2)
                sp.dma_start(c_raw[:, b % 2], ctx_dram[half * HB + b].rearrange("(k p) s -> p k s", p=P)).then_inc(c_in[b % 2], 16)

            sp.dma_start(w_raw[:], w_first[:, Q0]).then_inc(w_in, 16)
            sp.dma_start(mask_raw, mask_dram[half:half + 1].to_broadcast([T, HB, S])).then_inc(mask_in, 16)
            load_context(0)
            load_context(1)
            sp.wait_ge(wq_lo_done, 1)
            sp.dma_start(w_raw[:], w_first[:, KV]).then_inc(w_in, 16)
            sp.wait_ge(wk_lo_done, 2)
            sp.wait_ge(wv_lo_done, 1)
            sp.dma_start(w_raw[:], w_first[:, Q1]).then_inc(w_in, 16)
            load_context(2)
            load_context(3)
            sp.wait_ge(wq_lo_done, 2)
            sp.dma_start(w_raw[:], w_first[:, O0]).then_inc(w_in, 16)
            load_context(4)
            load_context(5)
            sp.wait_ge(wo_lo_done, 1)
            sp.dma_start(w_raw[:], w_first[:, O1]).then_inc(w_in, 16)
            load_context(6)
            load_context(7)
            for i in range(2):
                sp.wait_ge(c_lo_done[i], HB // 2)

            with sp.Fori(1, NPAIR) as p:
                w = w_dram[bass.ds(p, 1)].rearrange("o p n -> p (o n)")
                sp.wait_ge(wk_lo_done, 2 * p)
                sp.sem_inc(held_sp, 1)
                sp.dma_start(wkv_raw, w[:, KV]).then_inc(wkv_in, 16)
                sp.wait_ge(wo_lo_done, 2 * p - 1)
                sp.sem_inc(held_sp, 1)
                sp.dma_start(wo0_raw, w[:, O0]).then_inc(wo0_in, 16)
                sp.wait_ge(wo_lo_done, 2 * p)
                sp.sem_inc(held_sp, 1)
                sp.dma_start(w_raw[:], w[:, Q0]).then_inc(w_in, 16)
                sp.wait_ge(wq_lo_done, 2 * p + 1)
                sp.sem_inc(held_sp, 1)
                sp.dma_start(w_raw[:], w[:, Q1]).then_inc(w_in, 16)
                sp.wait_ge(wq_lo_done, 2 * p + 2)
                sp.sem_inc(held_sp, 1)
                sp.dma_start(w_raw[:], w[:, O1]).then_inc(w_in, 16)
            out_v = out_dram.rearrange("(b t) d -> t b d", t=T)[:, half * HB:(half + 1) * HB, :]
            for a in range(0, HB, 2):
                sp.wait_ge(added, 1 + (NPAIR - 1) * HB + a + 2)
                sp.dma_start(out_v[:, a:a + 2, :], x[:, a:a + 2, :]).then_inc(stored, 16)
            sp.wait_ge(stored, 16 * HB // 2)

        @block.tensor
        def _(pe):
            norm_tensor(ln, pe)
            pe.wait_ge(ln.lo_done, HB)

            def slot(b, u, last):
                turn, score, product, keys = parts(u, last)
                n = b * PAIR + u
                if turn:
                    for h in range(QH):
                        wait(pe, norm_done, 2 * n + h + 1)
                        wait(pe, pt_lo_done, 2 * n - 1 + h)
                        view = t_ps[h][0:SL, 0:SCH * T].rearrange("s (c t) -> s c t", c=SCH)
                        for c in range(SCH):
                            ins = pe.transpose(view[:, c, :], prob[:, u % 2, h, c * SL:(c + 1) * SL], ident[0:T, 0:T])
                        ins.then_inc(t_done, 1)
                if score:
                    w = u + 1
                    pe.wait_ge(k_lo_done, n + 2)
                    if w % HB < 2:
                        pe.wait_ge(q_lo_done, b * 4 * QH + q_products(w) + QH)
                    a = slice(w // 2 % TGB * T, (w // 2 % TGB + 1) * T)
                    for h in range(QH):
                        wait(pe, max_done, 2 * n + h + 1)
                        ins = matmul_split(pe, s_ps[h][0:T, 0:SE], q_hi[:, w % 2, h, a], q_lo[:, w % 2, h, a],
                                           k_hi[:, w % 2, :], k_lo[:, w % 2, :], True, True)
                        ins.then_inc(s_done, 1)
                if product:
                    m = u - 1
                    pe.wait_ge(o_lo_done, n)
                    if m < 2:
                        pe.wait_ge(wo_lo_done, 2 * b + m + 1)
                    if m % 2 == 0:
                        pe.wait_ge(added, b * HB + m // 2 + 1)
                    for h in range(QH):
                        a, w = slice(h * T, (h + 1) * T), slice(h * DM, (h + 1) * DM)
                        ins = matmul_split(pe, r_ps[0:T, :], o_hi[:, m % 2, a], o_lo[:, m % 2, a],
                                           wo_hi[:, m % 2, w], wo_lo[:, m % 2, w], m % 2 == 0 and h == 0, m % 2 == 1 and h == QH - 1)
                    ins.then_inc(r_done, 1)
                if keys:
                    w = u + 2
                    i, m, p = w % 2, w // 2 % HB, w // PAIR
                    wait(pe, k_lo_done, n + 2)
                    wait(pe, v_lo_done, n + 2)
                    if w % HB < 2:
                        if w % PAIR < 2:
                            pe.wait_ge(wq_lo_done, 2 * (b + p) + i + 1)
                        for h, bank in enumerate((k_ps, v_ps)):
                            for k in range(KD):
                                c = slice((k * QH + h) * HD, (k * QH + h + 1) * HD)
                                a = slice(m // TGB * TGT, (m // TGB + 1) * TGT)
                                ins = matmul_split(pe, bank[:, 0:TGT], wq_hi[:, i, c], wq_lo[:, i, c],
                                                   xt_hi[:, k, a], xt_lo[:, k, a], k == 0, k == KD - 1)
                            ins.then_inc(q_done, 1)
                        pe.wait_ge(q_lo_done, b * 4 * QH + q_products(w) + 1)
                    if w % PAIR < 2:
                        pe.wait_ge(wk_lo_done, 2 * (b + p) + i + 1)
                    if w < PAIR and i == 0:
                        pe.wait_ge(c_lo_done[m % 2], m // 2 + 1)
                    for k in range(KC):
                        c = slice(k * HD, (k + 1) * HD)
                        ins = matmul_split(pe, k_ps[:, 0:SE], wk_hi[:, i, c], wk_lo[:, i, c],
                                           c_hi[:, m, k, :], c_lo[:, m, k, :], k == 0, k == KC - 1)
                    ins.then_inc(k_done, 1)
                    if w % PAIR == 0:
                        pe.wait_ge(wv_lo_done, b + p + 1)
                    if w % HB < 2:
                        pe.wait_ge(q_lo_done, b * 4 * QH + q_products(w) + QH)
                    for o, c in enumerate(v_chunks(i)):
                        for k in range(KC):
                            a, d = slice(c * SL, (c + 1) * SL), slice(k * HEAD2 * HD, (k + 1) * HEAD2 * HD)
                            ins = matmul_split(pe, v_ps[0:SL, o * HEAD2 * HD:(o + 1) * HEAD2 * HD], c_hi[:, m, k, a], c_lo[:, m, k, a],
                                               wv_hi[:, d], wv_lo[:, d], k == 0, k == KC - 1)
                    ins.then_inc(v_done, 1)
                if turn:
                    pe.wait_ge(pt_lo_done, 2 * n + 2)
                    pe.wait_ge(v_lo_done, n + 2 - u % 2)
                    wait(pe, o_lo_done, n)
                    for c in range(SCH):
                        d, m = slice((c * HEAD2 + u % 2) * HD, (c * HEAD2 + u % 2 + 1) * HD), u // 2 % 2
                        ins = matmul_split(pe, o_ps[:, 0:QH * T], v_hi[:, m, d], v_lo[:, m, d],
                                           pt_hi[:, u % 2, c].rearrange("s h t -> s (h t)"),
                                           pt_lo[:, u % 2, c].rearrange("s h t -> s (h t)"), c == 0, c == SCH - 1)
                    ins.then_inc(o_done, 1)

            slots(pe, slot)

        @block.scalar
        def _(act):
            norm_scalar(ln, act)

            def split(kind, i, b, first=False):
                if kind == "q":
                    if first:
                        act.wait_ge(w_in, 48)
                    else:
                        act.wait_ge(w_in, 48 * b + 96 + 16 * i)
                        act.wait_ge(q_done, b * 4 * QH + (3 + i) * QH)
                    act.activation(wq_hi[:, i], raw(kind, i, first), ACT.Copy).then_inc(wq_hi_done, 1)
                if kind == "k":
                    if first:
                        act.wait_ge(w_in, 32)
                    else:
                        act.wait_ge(wkv_in, 16 * b + 16)
                        act.wait_ge(k_done, b * PAIR + PAIR - 1 + i)
                    act.activation(wk_hi[:, i], raw(kind, i, first), ACT.Copy).then_inc(wk_hi_done, 1)
                if kind == "v":
                    if not first:
                        act.wait_ge(v_done, b * PAIR + PAIR)
                    act.activation(wv_hi[:], raw(kind, i, first), ACT.Copy).then_inc(wv_hi_done, 1)
                if kind == "o":
                    if first:
                        act.wait_ge(w_in, 64 + 16 * i)
                    elif i == 0:
                        act.wait_ge(wo0_in, 16 * b + 16)
                    else:
                        act.wait_ge(w_in, 48 * b + 128)
                    if not first:
                        act.wait_ge(r_done, b * PAIR + PAIR - 1 + i)
                    act.activation(wo_hi[:, i], raw(kind, i, first), ACT.Copy).then_inc(wo_hi_done, 1)

            def slot(b, u, last):
                turn, score, product, keys = parts(u, last)
                n = b * PAIR + u
                if turn:
                    for h in range(QH):
                        act.wait_ge(t_done, 2 * n + h + 1)
                        wait(act, o_done, n)
                        act.activation(pt_hi[:, u % 2, :, h, :], t_ps[h][0:SL, 0:SCH * T].rearrange("s (c t) -> s c t", c=SCH),
                                       ACT.Copy).then_inc(pt_hi_done, 1)
                if score:
                    w = (u + 1) % 2
                    for h in range(QH):
                        act.wait_ge(max_done, 2 * n + h + 3)
                        act.activation(prob[:, w, h, :], prob[:, w, h, :], ACT.Exp, bias=least[:, w, h:h + 1], scale=-1.0,
                                       accum_out=total[:, w, h:h + 1]).then_inc(exp_done, 1)
                kind, i = splits(u, last)
                if kind:
                    split(kind, i, b)
                if keys:
                    w = u + 2
                    wait(act, s_done, 2 * n + 2)
                    if w % HB < 2:
                        for h, bank in enumerate((k_ps, v_ps)):
                            act.wait_ge(q_done, b * 4 * QH + q_products(w) + h + 1)
                            act.activation(q_hi[:, w % 2, h, :], bank[:, 0:TGT], ACT.Copy).then_inc(q_hi_done, 1)
                    act.wait_ge(k_done, n + 3)
                    act.activation(k_hi[:, w % 2, :], k_ps[:, 0:SE], ACT.Copy).then_inc(k_hi_done, 1)
                if turn:
                    act.wait_ge(o_done, n + 1)
                    wait(act, r_done, n)
                    act.activation(o_hi[:, u % 2, :], o_ps[:, 0:QH * T], ACT.Copy).then_inc(o_hi_done, 1)
                if keys:
                    act.wait_ge(v_done, n + 3)
                    wait(act, o_done, n + 1)
                    m, to, of = v_part(w)
                    act.activation(v_hi[:, m, to], v_ps[0:SL, of], ACT.Copy).then_inc(v_hi_done, 1)
                kind, i = late_splits(u, last)
                if kind:
                    split(kind, i, b)

            def split_context(first):
                for b in (first, first + 1):
                    act.wait_ge(c_in[b % 2], 16 * (b // 2 + 1))
                    act.activation(c_hi[:, b], c_raw[:, b % 2], ACT.Copy).then_inc(c_hi_done, 1)
                if first == 2:
                    split("o", 0, 0, first=True)
                if first == 4:
                    split("o", 1, 0, first=True)

            split("k", 0, 0, first=True)
            split("k", 1, 0, first=True)
            split("v", 0, 0, first=True)
            split_context(0)
            split("q", 1, 0, first=True)
            slots(act, slot, split_context)

        @block.gpsimd
        def _(pool):

            def split(kind, i, b, first=False):
                p = 0 if first else b + 1
                if kind == "q":
                    pool.wait_ge(wq_hi_done, 2 * p + i + 1)
                    pool.tensor_tensor(wq_lo[:, i], raw(kind, i, first), wq_hi[:, i].bitcast(F32), ALU.subtract).then_inc(wq_lo_done, 1)
                if kind == "k":
                    pool.wait_ge(wk_hi_done, 2 * p + i + 1)
                    pool.tensor_tensor(wk_lo[:, i], raw(kind, i, first), wk_hi[:, i].bitcast(F32), ALU.subtract).then_inc(wk_lo_done, 1)
                if kind == "v":
                    pool.wait_ge(wv_hi_done, p + 1)
                    pool.tensor_tensor(wv_lo[:], raw(kind, i, first), wv_hi[:].bitcast(F32), ALU.subtract).then_inc(wv_lo_done, 1)
                if kind == "o":
                    pool.wait_ge(wo_hi_done, 2 * p + i + 1)
                    pool.tensor_tensor(wo_lo[:, i], raw(kind, i, first), wo_hi[:, i].bitcast(F32), ALU.subtract).then_inc(wo_lo_done, 1)

            def slot(b, u, last):
                turn, score, product, keys = parts(u, last)
                n = b * PAIR + u
                if score:
                    w = (u + 1) % 2
                    pool.wait_ge(recip_done, n + 2)
                    pool.sem_inc(held_pool, 1)
                    for h in range(QH):
                        pool.tensor_scalar(prob[:, w, h, :], prob[:, w, h, :], recip[:, w, h:h + 1],
                                           valid[:, (u + 1) // 2 % HB:(u + 1) // 2 % HB + 1], ALU.mult, ALU.mult).then_inc(norm_done, 1)
                for kind, i in (splits(u, last), late_splits(u, last)):
                    if kind:
                        split(kind, i, b)

            def split_context(b):
                pool.wait_ge(c_hi_done, b + 1)
                pool.tensor_tensor(c_lo[:, b], c_raw[:, b % 2], c_hi[:, b].bitcast(F32), ALU.subtract).then_inc(c_lo_done[0], 1)
                if b == 2:
                    split("o", 0, 0, first=True)
                if b == 4:
                    split("o", 1, 0, first=True)

            pool.wait_ge(w_in, 16)
            pool.tensor_copy(wq_hi[:, 0], w_raw[:]).then_inc(wq_hi_done, 1)
            split("q", 0, 0, first=True)
            split("k", 0, 0, first=True)
            split("k", 1, 0, first=True)
            split("v", 0, 0, first=True)
            split_context(0)
            pool.wait_ge(mask_in, 16)
            pool.wait_ge(ln.turned, HB)
            pool.tensor_scalar(bias_all[:], prob_all[:].bitcast(mybir.dt.uint8)[:, 0:HB * S], MASKED, -MASKED, ALU.mult, ALU.add).then_inc(bias_done, 1)
            split("q", 1, 0, first=True)
            slots(pool, slot, split_context)

        @block.vector
        def _(dve):
            dve.sem_inc(added, 1)
            norm_vector(ln, dve)
            dve.wait_ge(mask_in, 16)
            dve.tensor_reduce(valid[:], mask_raw, AX.X, ALU.max).then_inc(bias_done, 1)

            def slot(b, u, last):
                turn, score, product, keys = parts(u, last)
                n = b * PAIR + u
                if turn:
                    for h in range(QH):
                        dve.wait_ge(pt_hi_done, 2 * n + h + 1)
                        dve.tensor_tensor(pt_lo[:, u % 2, :, h, :], t_ps[h][0:SL, 0:SCH * T].rearrange("s (c t) -> s c t", c=SCH),
                                          pt_hi[:, u % 2, :, h, :].bitcast(F32), ALU.subtract).then_inc(pt_lo_done, 1)
                if score:
                    w = (u + 1) % 2
                    for h in range(QH):
                        dve.wait_ge(s_done, 2 * n + h + 3)
                        wait(dve, t_done, 2 * n - 1 + h)
                        dve.sem_inc(held_dve, 1)
                        dve.tensor_tensor_reduce(prob[:, w, h, :], s_ps[h][0:T, 0:S], bias[:, (u + 1) // 2 % HB, :],
                                                 -(HD ** -0.5), 3e38, ALU.add, ALU.min,
                                                 least[:, w, h:h + 1]).then_inc(max_done, 1)
                if product and u % 2 == 0:
                    m = (u - 1) // 2
                    dve.wait_ge(r_done, n)
                    dve.tensor_tensor(x[:, m, :], r_ps[0:T, :], x[:, m, :], ALU.add).then_inc(added, 1)
                if score:
                    dve.wait_ge(exp_done, 2 * n + 4)
                    wait(dve, norm_done, 2 * n)
                    dve.reciprocal(recip[:, w, :], total[:, w, :]).then_inc(recip_done, 1)
                if keys:
                    w = u + 2
                    if w % HB < 2:
                        for h, bank in enumerate((k_ps, v_ps)):
                            dve.wait_ge(q_hi_done, b * 4 * QH + q_products(w) + h + 1)
                            dve.tensor_tensor(q_lo[:, w % 2, h, :], bank[:, 0:TGT], q_hi[:, w % 2, h, :].bitcast(F32),
                                              ALU.subtract).then_inc(q_lo_done, 1)
                    dve.wait_ge(k_hi_done, n + 3)
                    dve.tensor_tensor(k_lo[:, w % 2, :], k_ps[:, 0:SE], k_hi[:, w % 2, :].bitcast(F32), ALU.subtract).then_inc(k_lo_done, 1)
                if turn:
                    dve.wait_ge(o_hi_done, n + 1)
                    dve.tensor_tensor(o_lo[:, u % 2, :], o_ps[:, 0:QH * T], o_hi[:, u % 2, :].bitcast(F32), ALU.subtract).then_inc(o_lo_done, 1)
                if keys:
                    dve.wait_ge(v_hi_done, n + 3)
                    m, to, of = v_part(w)
                    dve.tensor_tensor(v_lo[:, m, to], v_ps[0:SL, of], v_hi[:, m, to].bitcast(F32),
                                      ALU.subtract).then_inc(v_lo_done, 1)

            def split_context(b):
                dve.wait_ge(c_hi_done, b + 2)
                dve.tensor_tensor(c_lo[:, b + 1], c_raw[:, (b + 1) % 2], c_hi[:, b + 1].bitcast(F32), ALU.subtract).then_inc(c_lo_done[1], 1)

            split_context(0)
            dve.wait_ge(bias_done, 2)
            slots(dve, slot, split_context)


def xattn_phase(nc, x_dram, ctx_dram, mask_dram, w_dram, ident_dram, out_dram):
    for half in range(2):
        xattn_half(nc, half, x_dram, ctx_dram, mask_dram, w_dram, ident_dram, out_dram)

E_N = 8
I_N = 352
IS_N = 1408
FT = TOKENS // P
FCH = (E_N * I_N + IS_N) // P
BCH = 3
NBLK = FCH // BCH
GU = 2 * KD * P
WCH = GU + DM
PIECE = 32
NPIECE = FCH * P // PIECE
EPIECE = I_N // PIECE
TG = [(0, 2), (2, 4), (6, 4), (10, 4)]
STEPS = len(TG) * BCH


def ffn_phase(nc, x_dram, w_dram, router_dram, rank_dram, ident_dram, c_dram, cexp_dram, out_dram):
    with ExitStack() as ctx:
        sb, ps, sem = opener(nc, ctx, "ff")
        x = sb("x", [P, FT, DM])
        xt_hi = sb("xt_hi", [P, KD, TOKENS], F32R)
        xt_lo = sb("xt_lo", [P, KD, TOKENS], F32R)
        w_raw = sb("w_raw", [P, BCH, WCH])
        w_hi = sb("w_hi", [P, BCH, WCH], F32R)
        w_lo = sb("w_lo", [P, BCH, WCH], F32R)
        scale = sb("scale", [P, BCH, TOKENS])
        silu = sb("silu", [P, 2, 512])
        scaled = sb("scaled", [P, 2, 512])
        h = sb("h", [P, 2, 512])
        h_hi = sb("h_hi", [P, 2, 512], F32R)
        h_lo = sb("h_lo", [P, 2, 512], F32R)
        ident = sb("ident", [P, P])
        r_raw = sb("r_raw", [P, KD, E_N + 2])
        r_hi = sb("r_hi", [P, KD, E_N + 2], F32R)
        r_lo = sb("r_lo", [P, KD, E_N + 2], F32R)
        rank = sb("rank", [P, FT, E_N])
        logits_t = sb("logits_t", [E_N + 2, TOKENS])
        logits = sb("logits", [P, FT, E_N + 2])
        prob = sb("prob", [P, FT, E_N])
        rest = sb("rest", [P, FT, E_N])
        key = sb("key", [P, FT, E_N])
        first = sb("first", [P, FT, E_N])
        stat = sb("stat", [P, 4, FT])
        comb = sb("comb", [P, FT, E_N + 1])
        comb_t = sb("comb_t", [E_N + 1, TOKENS])

        gate_ps = [ps(f"gate{i}", [P, 512]) for i in range(2)]
        up_ps = [ps(f"up{i}", [P, 512]) for i in range(2)]
        acc = [ps(f"acc{i}", [P, 512]) for i in range(4)]

        ln = Norm(sb, sem, P, FT, x, xt_hi, xt_lo, ident, acc, [(0, 2), (2, 6), (6, 10), (10, 14)])
        router_in = sem("router_in")
        r_split = sem("r_split")
        logits_ps = sem("logits_ps")
        logits_out = sem("logits_out")
        routed = sem("routed")
        exp_done = sem("exp_done")
        comb_turned = sem("comb_turned")
        comb_out = sem("comb_out")
        c_stored = sem("c_stored")
        w_in = [sem(f"w_in{j}") for j in range(BCH)]
        scale_in = [sem(f"scale_in{j}") for j in range(BCH)]
        gu_hi = [sem(f"gu_hi{j}") for j in range(BCH)]
        gu_lo = [sem(f"gu_lo{j}") for j in range(BCH)]
        dn_hi = [sem(f"dn_hi{j}") for j in range(BCH)]
        dn_lo = [sem(f"dn_lo{j}") for j in range(BCH)]
        gu_done = sem("gu_done")
        silu_done = sem("silu_done")
        scaled_done = sem("scaled_done")
        h_done = sem("h_done")
        h_hi_done = sem("h_hi_done")
        h_lo_done = sem("h_lo_done")
        down_done = sem("down_done")
        acc_done = sem("acc_done")
        added = sem("added")
        stored = sem("stored")

        def n_tok(s):
            return TG[s // BCH][1] * P

        def tok(s):
            return TG[s // BCH][0] * P

        block = ctx.enter_context(nc.Block())

        @block.sync
        def _(sp):
            norm_load(ln, sp, x_dram.rearrange("(t p) d -> p t d", p=P), ident_dram)
            sp.dma_start(r_raw[:], router_dram).then_inc(router_in, 16)
            sp.dma_start(rank[:], rank_dram).then_inc(router_in, 16)
            for j in range(BCH):
                sp.dma_start(w_raw[:, j, :], w_dram[j]).then_inc(w_in[j], 16)
            sp.wait_ge(comb_out, 4)
            sp.dma_start(c_dram, comb_t[:]).then_inc(c_stored, 16)
            sp.wait_ge(c_stored, 16)
            for j in range(BCH):
                for r in range(P // PIECE):
                    e = (j * (P // PIECE) + r) // EPIECE
                    sp.dma_start(scale[r * PIECE:(r + 1) * PIECE, j, :],
                                 c_dram[e:e + 1, :].to_broadcast([PIECE, TOKENS])).then_inc(scale_in[j], 16)
            sp.dma_start(cexp_dram[0:E_N * EPIECE, :].rearrange("(e r) t -> e r t", r=EPIECE),
                         c_dram[0:E_N, :].unsqueeze(1).to_broadcast([E_N, EPIECE, TOKENS])).then_inc(c_stored, 16)
            sp.dma_start(cexp_dram[E_N * EPIECE:NPIECE, :],
                         c_dram[E_N:E_N + 1, :].to_broadcast([NPIECE - E_N * EPIECE, TOKENS])).then_inc(c_stored, 16)
            sp.wait_ge(c_stored, 48)

            def load_scale(b, j):
                for r in range(P // PIECE):
                    q = (b * BCH + j) * (P // PIECE) + r
                    sp.dma_start(scale[r * PIECE:(r + 1) * PIECE, j, :],
                                 cexp_dram[bass.ds(q, 1), :].to_broadcast([PIECE, TOKENS])).then_inc(scale_in[j], 16)

            def load_weights(b, j):
                sp.wait_ge(gu_lo[j], b)
                sp.wait_ge(dn_lo[j], b)
                sp.dma_start(w_raw[:, j, :], w_dram[bass.ds(b * BCH + j, 1)].rearrange("o p n -> p (o n)")).then_inc(w_in[j], 16)

            for j in range(BCH):
                load_weights(1, j)
            with sp.Fori(1, NBLK - 1) as b:
                for j in range(BCH):
                    sp.wait_ge(scaled_done, (b - 1) * STEPS + STEPS - BCH + j + 3)
                    load_scale(b, j)
                    load_weights(b + 1, j)
            for j in range(BCH):
                sp.wait_ge(scaled_done, (NBLK - 2) * STEPS + STEPS - BCH + j + 3)
                load_scale(NBLK - 1, j)
            out_v = out_dram.rearrange("(t p) d -> p t d", p=P)
            for g, (t, n) in enumerate(TG):
                sp.wait_ge(added, NBLK * FT + t + n)
                sp.dma_start(out_v[:, t:t + n, :], x[:, t:t + n, :]).then_inc(stored, 16)
            sp.wait_ge(stored, 16 * len(TG))

        @block.tensor
        def _(pe):
            def gate_up(b, s, first=False):
                j, n, a = s % BCH, n_tok(s), tok(s)
                if s < BCH:
                    pe.wait_ge(gu_lo[j], b + 1)
                if not first:
                    pe.wait_ge(h_done, b * STEPS + s + 1)
                for bank, o in ((gate_ps[s % 2], 0), (up_ps[s % 2], KD * P)):
                    for k in range(KD):
                        w = slice(o + k * P, o + (k + 1) * P)
                        ins = matmul_split(pe, bank[:, 0:n], w_hi[:, j, w], w_lo[:, j, w],
                                           xt_hi[:, k, a:a + n], xt_lo[:, k, a:a + n], k == 0, k == KD - 1)
                ins.then_inc(gu_done, 1)

            norm_tensor(ln, pe)
            pe.wait_ge(r_split, 2)
            pe.wait_ge(ln.lo_done, FT)
            for i in range(4):
                a = slice(4 * i * P, min(4 * i + 4, FT) * P)
                for k in range(KD):
                    ins = matmul_split(pe, acc[i][0:E_N + 2, 0:a.stop - a.start], r_hi[:, k, :], r_lo[:, k, :],
                                       xt_hi[:, k, a], xt_lo[:, k, a], k == 0, k == KD - 1)
                ins.then_inc(logits_ps, 1)
            for t in range(FT):
                if t % 4 == 0:
                    pe.wait_ge(logits_out, t // 4 + 1)
                ins = pe.transpose(up_ps[1][:, t * (E_N + 2):(t + 1) * (E_N + 2)], logits_t[:, t * P:(t + 1) * P], ident[0:E_N + 2, 0:E_N + 2])
            ins.then_inc(logits_ps, 1)
            gate_up(0, 0, first=True)
            pe.wait_ge(r_split, 5)
            for t in range(FT):
                ins = pe.transpose(acc[t // 4][0:E_N + 1, (t % 4) * P:(t % 4 + 1) * P], comb[:, t, :], ident[:])
                if t % 4 == 3 or t == FT - 1:
                    ins.then_inc(comb_turned, 1)
            pe.wait_ge(comb_out, 4)

            def down(b, s):
                j, (t0, nt) = s % BCH, TG[s // BCH]
                if s < BCH:
                    pe.wait_ge(dn_lo[j], b + 1)
                pe.wait_ge(h_lo_done, b * STEPS + s + 1)
                for m in range(nt):
                    if j == 0:
                        g = s // BCH - 1
                        if g >= 0:
                            pe.wait_ge(added, (b + 1) * FT + TG[g][0] + min(m + 1, TG[g][1]))
                        else:
                            pe.wait_ge(added, b * FT + TG[-1][0] + m + 1)
                    a, w = slice(m * P, (m + 1) * P), slice(GU, WCH)
                    ins = matmul_split(pe, acc[m][:], h_hi[:, s % 2, a], h_lo[:, s % 2, a],
                                       w_hi[:, j, w], w_lo[:, j, w], j == 0, j == BCH - 1)
                    if j == BCH - 1:
                        ins.then_inc(acc_done, 1)
                if j < BCH - 1:
                    ins.then_inc(down_done, 1)

            def one_block(b, last):
                for s in range(1, STEPS):
                    gate_up(b, s)
                    down(b, s - 1)
                if not last:
                    gate_up(b + 1, 0)
                down(b, STEPS - 1)

            with pe.Fori(0, NBLK - 1) as b:
                one_block(b, False)
            one_block(NBLK - 1, True)

        @block.scalar
        def _(act):
            def split_gu(b, j, first=False):
                act.wait_ge(w_in[j], 16 * (b + 1))
                if not first:
                    act.wait_ge(gu_done, b * STEPS - BCH + j + 1)
                act.activation(w_hi[:, j, 0:GU], w_raw[:, j, 0:GU], ACT.Copy).then_inc(gu_hi[j], 1)

            def split_dn(b, j, first=False):
                if not first and j < BCH - 1:
                    act.wait_ge(down_done, b * len(TG) * (BCH - 1) - (BCH - 1) + j + 1)
                elif not first:
                    act.wait_ge(acc_done, b * FT)
                act.activation(w_hi[:, j, GU:WCH], w_raw[:, j, GU:WCH], ACT.Copy).then_inc(dn_hi[j], 1)

            norm_scalar(ln, act)
            for j in range(BCH):
                split_gu(0, j, first=True)
                split_dn(0, j, first=True)
            act.wait_ge(routed, 1)
            act.activation(prob[:], rest[:], ACT.Exp).then_inc(exp_done, 1)
            act.activation(comb[:, :, E_N], logits[:, :, E_N], ACT.Sigmoid).then_inc(exp_done, 1)

            def step(b, s, first=False):
                n = n_tok(s)
                act.wait_ge(gu_done, b * STEPS + s + 1)
                if not first:
                    act.wait_ge(scaled_done, b * STEPS + s + 1)
                act.activation(silu[:, s % 2, 0:n], gate_ps[s % 2][:, 0:n], ACT.Silu).then_inc(silu_done, 1)
                act.wait_ge(h_done, b * STEPS + s + 3)
                act.activation(h_hi[:, s % 2, 0:n], h[:, s % 2, 0:n], ACT.Copy).then_inc(h_hi_done, 1)

            def one_block(b, last):
                for s in range(1, STEPS + 1):
                    if s < STEPS:
                        step(b, s)
                    elif not last:
                        step(b + 1, 0)
                    if s >= STEPS - BCH and s < STEPS and not last:
                        split_gu(b + 1, s - (STEPS - BCH))
                    if s > STEPS - BCH and not last:
                        split_dn(b + 1, s - (STEPS - BCH) - 1)

            step(0, 0, first=True)
            with act.Fori(0, NBLK - 1) as b:
                one_block(b, False)
            one_block(NBLK - 1, True)

        @block.gpsimd
        def _(pool):
            def split_gu(b, j):
                pool.wait_ge(gu_hi[j], b + 1)
                pool.tensor_tensor(w_lo[:, j, 0:GU], w_raw[:, j, 0:GU], w_hi[:, j, 0:GU].bitcast(F32),
                                   ALU.subtract).then_inc(gu_lo[j], 1)

            def split_dn(b, j):
                pool.wait_ge(dn_hi[j], b + 1)
                pool.tensor_tensor(w_lo[:, j, GU:WCH], w_raw[:, j, GU:WCH], w_hi[:, j, GU:WCH].bitcast(F32),
                                   ALU.subtract).then_inc(dn_lo[j], 1)

            def step(b, s, first=False):
                n, a, j = n_tok(s), tok(s), s % BCH
                if s < BCH:
                    pool.wait_ge(scale_in[j], 16 * (P // PIECE) * (b + 1))
                pool.wait_ge(silu_done, b * STEPS + s + 1)
                if not first:
                    pool.wait_ge(h_done, b * STEPS + s + 1)
                pool.tensor_tensor(scaled[:, s % 2, 0:n], silu[:, s % 2, 0:n], scale[:, j, a:a + n],
                                   ALU.mult).then_inc(scaled_done, 1)

            def one_block(b, last):
                for s in range(1, STEPS + 1):
                    if s < STEPS:
                        step(b, s)
                    elif not last:
                        step(b + 1, 0)
                    if s >= STEPS - BCH and s < STEPS and not last:
                        split_gu(b + 1, s - (STEPS - BCH))
                    if s > STEPS - BCH and not last:
                        split_dn(b + 1, s - (STEPS - BCH) - 1)

            for j in range(BCH):
                split_gu(0, j)
                split_dn(0, j)
            step(0, 0, first=True)
            with pool.Fori(0, NBLK - 1) as b:
                one_block(b, False)
            one_block(NBLK - 1, True)

        @block.vector
        def _(dve):
            dve.sem_inc(added, FT)
            dve.sem_inc(h_done, 2)
            dve.sem_inc(scaled_done, 2)
            norm_vector(ln, dve)
            dve.wait_ge(router_in, 32)
            dve.tensor_copy(r_hi[:], r_raw[:]).then_inc(r_split, 1)
            dve.wait_ge(r_split, 1)
            dve.tensor_tensor(r_lo[:], r_raw[:], r_hi[:].bitcast(F32), ALU.subtract).then_inc(r_split, 1)

            chain = [0]

            def link(ins):
                chain[0] += 1
                ins.then_inc(routed, 1)
                dve.wait_ge(routed, chain[0])

            def wide(a):
                return a.unsqueeze(2).to_broadcast([P, FT, E_N])

            top, total, top1, top2 = (stat[:, i, :] for i in range(4))
            for i in range(4):
                dve.wait_ge(logits_ps, i + 1)
                n = min(4, FT - 4 * i) * P
                dve.tensor_copy(logits_t[:, 512 * i:512 * i + n], acc[i][0:E_N + 2, 0:n]).then_inc(logits_out, 1)
            dve.wait_ge(logits_ps, 5)
            dve.tensor_copy(logits[:], up_ps[1][:, 0:FT * (E_N + 2)].rearrange("p (t e) -> p t e", e=E_N + 2)).then_inc(r_split, 1)
            dve.wait_ge(r_split, 3)
            dve.tensor_reduce(top, logits[:, :, 0:E_N], AX.X, ALU.max).then_inc(r_split, 1)
            dve.wait_ge(r_split, 4)
            link(dve.tensor_tensor(rest[:], logits[:, :, 0:E_N], wide(top), ALU.subtract))
            dve.wait_ge(exp_done, 2)
            link(dve.tensor_reduce(total, prob[:], AX.X, ALU.add))
            link(dve.reciprocal(total, total))
            link(dve.tensor_tensor(prob[:], prob[:], wide(total), ALU.mult))

            def choose(out, of, best):
                link(dve.tensor_reduce(best, of, AX.X, ALU.max))
                link(dve.tensor_tensor(key[:], of, wide(best), ALU.is_equal))
                link(dve.tensor_tensor(key[:], key[:], rank[:], ALU.mult))
                link(dve.tensor_reduce(top, key[:], AX.X, ALU.max))
                link(dve.tensor_tensor(out, key[:], wide(top), ALU.is_equal))

            choose(first[:], prob[:], top1)
            link(dve.scalar_tensor_tensor(rest[:], first[:], -2.0, prob[:], ALU.mult, ALU.add))
            choose(key[:], rest[:], top2)
            link(dve.tensor_tensor(first[:], first[:], key[:], ALU.add))
            link(dve.tensor_tensor(first[:], first[:], prob[:], ALU.mult))
            link(dve.tensor_tensor(total, top1, top2, ALU.add))
            link(dve.reciprocal(total, total))
            dve.tensor_tensor(comb[:, :, 0:E_N], first[:], wide(total), ALU.mult).then_inc(r_split, 1)
            for i in range(4):
                dve.wait_ge(comb_turned, i + 1)
                n = min(4, FT - 4 * i) * P
                dve.tensor_copy(comb_t[:, 512 * i:512 * i + n], acc[i][0:E_N + 1, 0:n]).then_inc(comb_out, 1)

            def step(b, s):
                n = n_tok(s)
                dve.wait_ge(scaled_done, b * STEPS + s + 3)
                dve.tensor_tensor(h[:, s % 2, 0:n], up_ps[s % 2][:, 0:n], scaled[:, s % 2, 0:n],
                                  ALU.mult).then_inc(h_done, 1)
                dve.wait_ge(h_hi_done, b * STEPS + s + 1)
                dve.tensor_tensor(h_lo[:, s % 2, 0:n], h[:, s % 2, 0:n], h_hi[:, s % 2, 0:n].bitcast(F32),
                                  ALU.subtract).then_inc(h_lo_done, 1)

            def one_block(b, last):
                for s in range(1, STEPS + 1):
                    if s < STEPS:
                        step(b, s)
                    elif not last:
                        step(b + 1, 0)
                    if s % BCH == 0:
                        t0, nt = TG[s // BCH - 1]
                        for m in range(nt):
                            dve.wait_ge(acc_done, b * FT + t0 + m + 1)
                            dve.tensor_tensor(x[:, t0 + m, :], acc[m][:], x[:, t0 + m, :], ALU.add).then_inc(added, 1)

            step(0, 0)
            with dve.Fori(0, NBLK - 1) as b:
                one_block(b, False)
            one_block(NBLK - 1, True)


def build(nc, d, out):
    x1 = nc.dram_tensor("x1", (TOKENS, DM), F32, kind="Internal").ap()
    attn_phase(nc, d["x"], d, x1)
    x2 = nc.dram_tensor("x2", (TOKENS, DM), F32, kind="Internal").ap()
    xattn_phase(nc, x1, d["ctx_t"], d["mask"], d["w_xattn"], d["ident"], x2)
    c = nc.dram_tensor("c_scratch", (E_N + 1, TOKENS), F32, kind="Internal").ap()
    cexp = nc.dram_tensor("c_spread", (NPIECE, TOKENS), F32, kind="Internal").ap()
    ffn_phase(nc, x2, d["w_ffn"], d["router"], d["rank"], d["ident"], c, cexp, out)



def kernel(x, ctx_1024, mask_BxS2_bf1, L0_attn_W_in, L0_attn_b_in, L0_attn_conv_w, L0_attn_conv_b, L0_attn_A_log,
           L0_attn_D_param, L0_attn_dt_bias, L0_attn_norm_w, L0_attn_W_out, L0_attn_b_out, L0_attn_mup_vector,
           L0_xattn_Wq, L0_xattn_Wk, L0_xattn_Wv, L0_xattn_Wo, L0_ffn_gate_w, L0_ffn_w_gate, L0_ffn_w_up,
           L0_ffn_w_down, L0_ffn_sw_gate, L0_ffn_sw_up, L0_ffn_sw_down, L0_ffn_shared_gate_w):
    import numpy as np
    import concourse.bacc as bacc
    from concourse import mybir
    from concourse.bass_utils import run_bass_kernel_spmd

    f = lambda a: np.ascontiguousarray(a)

    def feature_chunks(w, width=128):
        k, n = w.shape
        return w.reshape(k // 128, 128, n // width, width).transpose(2, 1, 0, 3)

    arrays = {
        "x": f(x).reshape(1792, 512),
        "ident": np.eye(128, dtype=np.float32),
    }
    gate = np.concatenate([f(L0_ffn_w_gate).transpose(1, 0, 2).reshape(512, 2816), f(L0_ffn_sw_gate)], 1)
    up = np.concatenate([f(L0_ffn_w_up).transpose(1, 0, 2).reshape(512, 2816), f(L0_ffn_sw_up)], 1)
    down = np.concatenate([f(L0_ffn_w_down).reshape(2816, 512), f(L0_ffn_sw_down)], 0)
    arrays["w_ffn"] = np.concatenate([feature_chunks(gate).reshape(33, 128, 512), feature_chunks(up).reshape(33, 128, 512),
                                      down.reshape(33, 128, 512)], 2)
    router = np.concatenate([f(L0_ffn_gate_w).T, f(L0_ffn_shared_gate_w), np.zeros((512, 1), np.float32)], 1)
    arrays["router"] = router.reshape(4, 128, 10).transpose(1, 0, 2)
    arrays["rank"] = np.broadcast_to(np.arange(8, 0, -1, dtype=np.float32), (128, 14, 8))
    ctx_t = f(ctx_1024).transpose(0, 2, 1)
    arrays["ctx_t"] = np.concatenate([ctx_t, np.zeros((16, 256, 1), np.float32)], 2)
    arrays["mask"] = f(mask_BxS2_bf1).view(np.uint8).reshape(2, 8, 375)
    wq = f(L0_xattn_Wq).reshape(4, 128, 8, 256).transpose(2, 1, 0, 3).reshape(8, 128, 1024)
    wk = f(L0_xattn_Wk).reshape(2, 128, 8, 128).transpose(2, 1, 0, 3).reshape(8, 128, 256)
    wv = f(L0_xattn_Wv).reshape(2, 128, 4, 256).transpose(2, 1, 0, 3).reshape(4, 128, 512)
    wo = f(L0_xattn_Wo).reshape(8, 2, 128, 512).transpose(0, 2, 1, 3).reshape(8, 128, 1024)
    arrays["w_xattn"] = np.concatenate([wq[0::2], wq[1::2], wo[0::2], wo[1::2], wk[0::2], wk[1::2], wv], 2)
    w_in = f(L0_attn_W_in)
    xz = np.concatenate([w_in[:, 2048:4096], w_in[:, 0:2048]], 1)
    xz = feature_chunks(xz).reshape(2, 8, 2, 128, 512).transpose(1, 3, 0, 2, 4).reshape(8, 128, 2048)
    w_out = f(L0_attn_W_out).reshape(8, 2, 128, 512).transpose(0, 2, 1, 3).reshape(8, 128, 1024)
    arrays["w_mix"] = np.concatenate([xz, w_out], 2)
    bcdt = np.concatenate([w_in[:, 4096:4640], np.zeros((512, 96), np.float32)], 1)
    arrays["w_bcdt"] = bcdt.reshape(4, 128, 640).transpose(1, 0, 2)

    def channels(a, first, n):
        return f(a)[first:first + n]

    def params(first, n):
        p = np.zeros((n, 8), np.float32)
        p[:, 0], p[:, 1] = channels(L0_attn_b_in, first, n), channels(L0_attn_mup_vector, first, n)
        if first >= 2048:
            p[:, 2:6], p[:, 6] = channels(L0_attn_conv_w, first - 2048, n), channels(L0_attn_conv_b, first - 2048, n)
        return p

    par_x = params(2048, 2048).reshape(8, 2, 128, 8)
    par_z = params(0, 2048).reshape(8, 2, 128, 8)
    par_n = np.zeros((8, 1, 128, 8), np.float32)
    par_n[:, 0, :, 0:2] = f(L0_attn_norm_w).reshape(8, 2, 128).transpose(0, 2, 1)
    arrays["par_mix"] = np.concatenate([par_x, par_z, par_n], 1).transpose(0, 2, 1, 3)
    par_dt = np.zeros((128, 8), np.float32)
    par_dt[0:32, 0], par_dt[0:32, 1] = channels(L0_attn_b_in, 4608, 32), channels(L0_attn_mup_vector, 4608, 32)
    par_dt[0:32, 7] = f(L0_attn_dt_bias)
    arrays["par_bcdt"] = np.concatenate([params(4096, 512).reshape(4, 128, 8), par_dt.reshape(1, 128, 8)], 0).transpose(1, 0, 2)
    arrays["tri"] = np.triu(np.ones((112, 112), np.float32))
    arrays["below"] = np.tril(np.ones((112, 112), np.float32), -1)
    arrays["a_log"] = f(L0_attn_A_log).reshape(1, 32)
    arrays["skip"] = f(L0_attn_D_param).reshape(1, 32)
    arrays["b_out"] = f(L0_attn_b_out).reshape(1, 512)

    nc = bacc.Bacc("TRN2", target_bir_lowering=False, num_devices=1)
    arrays = {f"in_{k}_dram": f(a) for k, a in arrays.items()}
    given = {k: nc.dram_tensor(k, a.shape, mybir.dt.from_np(a.dtype), kind="ExternalInput").ap()
             for k, a in arrays.items()}
    out = nc.dram_tensor("out_0_dram", (1792, 512), mybir.dt.float32, kind="ExternalOutput").ap()
    build(nc, {k[3:-5]: a for k, a in given.items()}, out)
    r = run_bass_kernel_spmd(nc, [arrays], core_ids=[0])
    return r.results[0]["out_0_dram"].reshape(16, 112, 512)
```
